# Optimizing a Trainium2 kernel written in Bass

```python
import numpy as np
import jax
import jax.numpy as jnp

def _softmax(x, axis=-1):
    return jax.nn.softmax(x, axis=axis)

def _gelu(x):
    return jax.nn.gelu(x, approximate=True)

def _silu(x):
    return jax.nn.silu(x)

def _sigmoid(x):
    return jax.nn.sigmoid(x)

def _layernorm(x, axis=-1, eps=1e-05):
    m = jnp.mean(x, axis=axis, keepdims=True)
    v = jnp.var(x, axis=axis, keepdims=True)
    return (x - m) / jnp.sqrt(v + eps)

def _scatter_add(tgt, idx, src, axis=0):
    return tgt.at[idx].add(src)

def _segment_sum(src, seg, n):
    return jax.ops.segment_sum(src, seg, n)
kernel_name = 'mk_macaron_d2_jaxref_r8_7416b0'

def setup_inputs(seed: int=0):
    np.random.seed(seed)
    _w = jnp.asarray

    def _L0_attn_setup():
        import jax, jax.numpy as jnp
        import numpy as np
        EMBED_DIM = 128
        NUM_HEADS = 16
        HEAD_DIM = EMBED_DIM // NUM_HEADS
        NUM_FEATS = 32
        YAT_EPS = 0.1
        BATCH = 4
        SEQ = 512

        def _spherical_features(x, projection):
            x_norm = x / (jnp.linalg.norm(x, axis=-1, keepdims=True) + 1e-08)
            proj = jnp.einsum('bhsd,hfd->bhsf', x_norm, projection)
            return jax.nn.relu(proj) + YAT_EPS
        key = jax.random.key(seed)
        ks = jax.random.split(key, 6)
        s = 1.0 / np.sqrt(EMBED_DIM)
        return {'x': jax.random.normal(ks[0], (BATCH, SEQ, EMBED_DIM), jnp.float32), 'Wq': jax.random.normal(ks[1], (EMBED_DIM, EMBED_DIM), jnp.float32) * s, 'bq': jnp.zeros((EMBED_DIM,), jnp.float32), 'Wk': jax.random.normal(ks[2], (EMBED_DIM, EMBED_DIM), jnp.float32) * s, 'bk': jnp.zeros((EMBED_DIM,), jnp.float32), 'Wv': jax.random.normal(ks[3], (EMBED_DIM, EMBED_DIM), jnp.float32) * s, 'bv': jnp.zeros((EMBED_DIM,), jnp.float32), 'Wo': jax.random.normal(ks[4], (EMBED_DIM, EMBED_DIM), jnp.float32) * s, 'bo': jnp.zeros((EMBED_DIM,), jnp.float32), 'projection': jax.random.normal(ks[5], (NUM_HEADS, NUM_FEATS, HEAD_DIM), jnp.float32)}
    _L0_attn_in = _L0_attn_setup()

    def _L0_ffn_setup():
        import jax, jax.numpy as jnp
        import numpy as np
        DMODEL = 128
        N_EXPERTS = 32
        EXPERT_SIZE = 64
        N_HEADS = 4
        WEIGHT_SCALE = 1.0
        key = jax.random.key(seed)
        k0, k1, k2, k3 = jax.random.split(key, 4)
        x = jax.random.normal(k0, (2, 256, DMODEL), dtype=jnp.float32)
        expert_sel = jax.random.normal(k1, (N_EXPERTS, DMODEL), dtype=jnp.float32) * DMODEL ** (-0.5)
        keys = jax.random.normal(k2, (N_EXPERTS, DMODEL, EXPERT_SIZE), dtype=jnp.float32) * DMODEL ** (-0.5)
        values = jax.random.normal(k3, (N_EXPERTS, EXPERT_SIZE, DMODEL), dtype=jnp.float32) * (N_EXPERTS * EXPERT_SIZE) ** (-0.5)
        return {'x': x, 'expert_sel': expert_sel, 'keys': keys, 'values': values}
    _L0_ffn_in = _L0_ffn_setup()

    def _L1_attn_setup():
        import jax, jax.numpy as jnp
        import numpy as np
        import math
        D_K = 64
        key = jax.random.key(seed)
        ks = jax.random.split(key, 5)
        b, m, d, h, dk, dv = (8, 128, 128, 16, 64, 64)
        return {'x': jax.random.normal(ks[0], (b, m, d), dtype=jnp.float32), 'P_q': jax.random.normal(ks[1], (h, d, dk), dtype=jnp.float32) * 0.02, 'P_k': jax.random.normal(ks[2], (h, d, dk), dtype=jnp.float32) * 0.02, 'P_v': jax.random.normal(ks[3], (h, d, dv), dtype=jnp.float32) * 0.02, 'P_o': jax.random.normal(ks[4], (h, d, dv), dtype=jnp.float32) * 0.02}
    _L1_attn_in = _L1_attn_setup()

    def _L1_ffn_setup():
        import jax, jax.numpy as jnp
        import numpy as np
        B, S, D, F, E, K = (2, 256, 128, 512, 8, 2)
        key = jax.random.key(seed)
        ks = jax.random.split(key, 5)
        x = jax.random.normal(ks[0], (B, S, D), dtype=jnp.float32)
        Wg = jax.random.normal(ks[1], (D, E), dtype=jnp.float32) * 0.02
        W1 = jax.random.normal(ks[2], (E, D, F), dtype=jnp.float32) * 0.02
        b1 = jnp.zeros((E, F), dtype=jnp.float32)
        W2 = jax.random.normal(ks[3], (E, F, D), dtype=jnp.float32) * 0.02
        b2 = jnp.zeros((E, D), dtype=jnp.float32)
        return {'x': x, 'Wg': Wg, 'W1': W1, 'b1': b1, 'W2': W2, 'b2': b2}
    _L1_ffn_in = _L1_ffn_setup()
    _d = {'L0_attn_x': _L0_attn_in['x'], 'L0_attn_Wq': _L0_attn_in['Wq'], 'L0_attn_bq': _L0_attn_in['bq'], 'L0_attn_Wk': _L0_attn_in['Wk'], 'L0_attn_bk': _L0_attn_in['bk'], 'L0_attn_Wv': _L0_attn_in['Wv'], 'L0_attn_bv': _L0_attn_in['bv'], 'L0_attn_Wo': _L0_attn_in['Wo'], 'L0_attn_bo': _L0_attn_in['bo'], 'L0_attn_projection': _L0_attn_in['projection'], 'L0_ffn_expert_sel': _L0_ffn_in['expert_sel'], 'L0_ffn_keys': _L0_ffn_in['keys'], 'L0_ffn_values': _L0_ffn_in['values'], 'L1_attn_P_q': _L1_attn_in['P_q'], 'L1_attn_P_k': _L1_attn_in['P_k'], 'L1_attn_P_v': _L1_attn_in['P_v'], 'L1_attn_P_o': _L1_attn_in['P_o'], 'L1_ffn_Wg': _L1_ffn_in['Wg'], 'L1_ffn_W1': _L1_ffn_in['W1'], 'L1_ffn_b1': _L1_ffn_in['b1'], 'L1_ffn_W2': _L1_ffn_in['W2'], 'L1_ffn_b2': _L1_ffn_in['b2']}
    _x0 = _d['L0_attn_x']
    _d['L0_attn_x'] = jax.random.normal(jax.random.fold_in(jax.random.key(seed), 1), (4, 1024, 128), dtype=_x0.dtype)
    del _x0
    return _d

def reference(L0_attn_x, L0_attn_Wq, L0_attn_bq, L0_attn_Wk, L0_attn_bk, L0_attn_Wv, L0_attn_bv, L0_attn_Wo, L0_attn_bo, L0_attn_projection, L0_ffn_expert_sel, L0_ffn_keys, L0_ffn_values, L1_attn_P_q, L1_attn_P_k, L1_attn_P_v, L1_attn_P_o, L1_ffn_Wg, L1_ffn_W1, L1_ffn_b1, L1_ffn_W2, L1_ffn_b2):

    def _L0_attn_ref(x, Wq, bq, Wk, bk, Wv, bv, Wo, bo, projection):
        import jax, jax.numpy as jnp
        import numpy as np
        EMBED_DIM = 128
        NUM_HEADS = 16
        HEAD_DIM = EMBED_DIM // NUM_HEADS
        NUM_FEATS = 32
        YAT_EPS = 0.1
        BATCH = 4
        SEQ = 512

        def _spherical_features(x, projection):
            x_norm = x / (jnp.linalg.norm(x, axis=-1, keepdims=True) + 1e-08)
            proj = jnp.einsum('bhsd,hfd->bhsf', x_norm, projection)
            return jax.nn.relu(proj) + YAT_EPS
        b, s, _ = x.shape

        def heads(t):
            return jnp.transpose(t.reshape(b, s, NUM_HEADS, HEAD_DIM), (0, 2, 1, 3))
        Q = heads(x @ Wq + bq)
        K = heads(x @ Wk + bk)
        V = heads(x @ Wv + bv)
        Qp = _spherical_features(Q, projection)
        Kp = _spherical_features(K, projection)
        KV = jnp.einsum('bhsf,bhsd->bhfd', Kp, V)
        QKV = jnp.einsum('bhsf,bhfd->bhsd', Qp, KV)
        K_sum = jnp.sum(Kp, axis=2)
        normalizer = jnp.einsum('bhsf,bhf->bhs', Qp, K_sum)[..., None]
        normalizer = jnp.maximum(normalizer, 1e-06)
        out = QKV / normalizer
        out = jnp.transpose(out, (0, 2, 1, 3)).reshape(b, s, EMBED_DIM)
        return out @ Wo + bo

    def _L0_ffn_ref(x, expert_sel, keys, values):
        import jax, jax.numpy as jnp
        import numpy as np
        DMODEL = 128
        N_EXPERTS = 32
        EXPERT_SIZE = 64
        N_HEADS = 4
        WEIGHT_SCALE = 1.0
        B, S, D = x.shape
        xt = x.reshape(-1, D)
        N = xt.shape[0]
        sel_logits = jnp.einsum('nd,ed->ne', xt, expert_sel)
        gates = jax.nn.sigmoid(sel_logits)
        sel_val, sel_idx = jax.lax.top_k(gates, N_HEADS)
        gate_full = jnp.zeros_like(gates).at[jnp.arange(N)[:, None], sel_idx].set(sel_val)
        scores = jax.nn.relu(jnp.einsum('nd,edf->nef', xt, keys))
        scores = scores * gate_full[:, :, None]
        out = jnp.einsum('nef,efv->nv', scores, values)
        return out.reshape(B, S, -1)

    def _L1_attn_ref(x, P_q, P_k, P_v, P_o):
        import jax, jax.numpy as jnp
        import numpy as np
        import math
        D_K = 64
        m = x.shape[1]
        Q = jnp.einsum('bmd,hdk->bhmk', x, P_q)
        K = jnp.einsum('bmd,hdk->bhmk', x, P_k)
        V = jnp.einsum('bmd,hdv->bhmv', x, P_v)
        logits = jnp.einsum('bhmk,bhnk->bhmn', Q, K) * math.sqrt(D_K)
        causal = jnp.tril(jnp.ones((m, m), dtype=bool))
        logits = jnp.where(causal[None, None], logits, -jnp.inf)
        key_weights = jax.nn.softmax(logits, axis=-1)
        o = jnp.einsum('bhmm,bhmv->bhmv', key_weights, V)
        y = jnp.einsum('bhmv,hdv->bmd', o, P_o)
        return y

    def _L1_ffn_ref(x, Wg, W1, b1, W2, b2):
        import jax, jax.numpy as jnp
        import numpy as np
        B, S, D, F, E, K = (2, 256, 128, 512, 8, 2)
        b, s, d = x.shape
        e = Wg.shape[1]
        T = b * s
        C = 2 * K * T // e
        xt = x.reshape(T, d)
        logits = xt.astype(jnp.float32) @ Wg.astype(jnp.float32)
        gates = jax.nn.softmax(logits, axis=-1)
        idx1 = jnp.argmax(gates, axis=-1)
        mask1 = jax.nn.one_hot(idx1, e, dtype=gates.dtype)
        gate1 = jnp.sum(gates * mask1, axis=-1)
        logits2 = jnp.where(mask1 > 0, -jnp.inf, logits)
        idx2 = jnp.argmax(logits2, axis=-1)
        mask2 = jax.nn.one_hot(idx2, e, dtype=gates.dtype)
        gate2 = jnp.sum(gates * mask2, axis=-1)
        denom = gate1 + gate2 + 1e-09
        w1 = gate1 / denom
        w2 = gate2 / denom
        p1 = jnp.cumsum(mask1, axis=0) - mask1
        pos1 = jnp.sum(p1 * mask1, axis=-1).astype(jnp.int32)
        off = jnp.sum(mask1, axis=0)
        p2 = jnp.cumsum(mask2, axis=0) - mask2 + off[None, :]
        pos2 = jnp.sum(p2 * mask2, axis=-1).astype(jnp.int32)
        keep1 = (pos1 < C).astype(xt.dtype)
        keep2 = (pos2 < C).astype(xt.dtype)
        pos1 = jnp.clip(pos1, 0, C - 1)
        pos2 = jnp.clip(pos2, 0, C - 1)
        xe = jnp.zeros((e, C, d), dtype=xt.dtype)
        xe = xe.at[idx1, pos1].add(xt * keep1[:, None])
        xe = xe.at[idx2, pos2].add(xt * keep2[:, None])
        h = jax.nn.gelu(jnp.einsum('ecd,edf->ecf', xe, W1) + b1[:, None, :], approximate=False)
        ye = jnp.einsum('ecf,efd->ecd', h, W2) + b2[:, None, :]
        out = ye[idx1, pos1] * (w1 * keep1)[:, None] + ye[idx2, pos2] * (w2 * keep2)[:, None]
        return out.reshape(b, s, d)
    x = L0_attn_x
    x = x + 0.5 * _L0_ffn_ref(_layernorm(x, axis=-1), L0_ffn_expert_sel, L0_ffn_keys, L0_ffn_values)
    x = x + _L0_attn_ref(_layernorm(x, axis=-1), L0_attn_Wq, L0_attn_bq, L0_attn_Wk, L0_attn_bk, L0_attn_Wv, L0_attn_bv, L0_attn_Wo, L0_attn_bo, L0_attn_projection)
    x = x + 0.5 * _L0_ffn_ref(_layernorm(x, axis=-1), L0_ffn_expert_sel, L0_ffn_keys, L0_ffn_values)
    x = x + 0.5 * _L1_ffn_ref(_layernorm(x, axis=-1), L1_ffn_Wg, L1_ffn_W1, L1_ffn_b1, L1_ffn_W2, L1_ffn_b2)
    x = x + _L1_attn_ref(_layernorm(x, axis=-1), L1_attn_P_q, L1_attn_P_k, L1_attn_P_v, L1_attn_P_o)
    x = x + 0.5 * _L1_ffn_ref(_layernorm(x, axis=-1), L1_ffn_Wg, L1_ffn_W1, L1_ffn_b1, L1_ffn_W2, L1_ffn_b2)
    return x

_drawn_inputs = setup_inputs


def setup_inputs(seed=0):
    import zlib

    import numpy as np

    out = dict(_drawn_inputs(seed))
    spreads = {'L0_attn_bq': (0.0, 0.8),
     'L0_attn_bk': (0.0, 0.8),
     'L0_attn_bv': (0.0, 0.1),
     'L0_attn_bo': (0.0, 0.1),
     'L1_ffn_b1': (0.0, 0.463),
     'L1_ffn_b2': (0.0, 0.1)}
    factors = {'L1_attn_P_q': 8.0, 'L1_attn_P_k': 8.0, 'L1_attn_P_v': 6.32, 'L1_attn_P_o': 6.274}
    for name, (base, spread) in spreads.items():
        noise = np.random.default_rng([zlib.crc32(name.encode()), seed]).standard_normal(out[name].shape)
        drawn = base * np.exp(spread * noise) if base else spread * noise
        out[name] = jnp.asarray(drawn.astype(out[name].dtype))
    for name, factor in factors.items():
        out[name] = (out[name] * factor).astype(out[name].dtype)
    return out
```

```python
from contextlib import ExitStack

import concourse.bass as bass
from concourse import mybir

F32 = mybir.dt.float32
F32R = mybir.dt.float32r
BF16 = mybir.dt.bfloat16
I32 = mybir.dt.int32
U32 = mybir.dt.uint32
ALU = mybir.AluOpType
ACT = mybir.ActivationFunctionType
AX = mybir.AxisListType

P = 128
BATCH, SEQ = 4, 1024
T = BATCH * SEQ
NT = T // P
BT = 4
BLK = BT * P
NB = T // BLK
LN_EPS = 1e-5
E0, F0, TOP0 = 32, 64, 4
NF0 = E0 * F0 // P
H0, HD0, FEAT0 = 16, 8, 32
NCH = H0 * FEAT0 // P
HPC = P // FEAT0
KVW = HPC * HD0
YAT_EPS, NORM_EPS, DEN_MIN = 0.1, 1e-8, 1e-6
E1, F1 = 8, 512
NF1 = E1 * F1 // P
CAP = 2 * 2 * T // E1
GATE_EPS = 1e-9
H1, DK = 16, 64
NF2 = H1 * DK // P
QT = SEQ // P
LOGIT_SCALE = 8.0
MASKED = -1e38
LO_ROW = 32
LAG = 3
SLOTS = 4
PICK = E1 * P + (E0 - E1) * 64
MAGIC = 0x5F3759DF


def build(nc, I, out):
    top = ExitStack()

    def sb(name, shape, dt, stack=top):
        return stack.enter_context(nc.sbuf_tensor(name, shape, dt))

    held = []

    def sem(name):
        held.append(nc.alloc_semaphore(name))
        return held[-1]

    def end_phase():
        nc.clear_and_free_semaphores(list(held))
        nc.all_engine_barrier()
        held.clear()

    x = sb("x", [P, NT, P], F32)
    xh = sb("xh", [P, T], F32R)
    xl = sb("xl", [P, T], F32R)
    wreg = sb("wreg", [P, 4, 2048], F32R)
    r = sb("r", [P, 2, BLK], F32)
    hg = sb("hg", [P, 2, BLK], F32)
    hh = sb("hh", [P, SLOTS, BLK], F32R)
    hl = sb("hl", [P, SLOTS, BLK], F32R)
    gT = sb("gT", [2 * LO_ROW, T], F32R)
    pick = sb("pick", [2 * LO_ROW, PICK], F32R)
    gate = sb("gate", [P, NT, 32], F32)
    ident = sb("ident", [P, P], F32)
    identb = sb("identb", [P, P], BF16)
    before = sb("before", [P, P], BF16)
    onesb = sb("onesb", [P, P], BF16)
    cmask = sb("cmask", [P, P], BF16)
    iota = sb("iota", [P, 32], F32)
    routers = sb("routers", [P, 2, P], F32R)
    selw, wgw = routers[:, :, 0:E0], routers[:, :, E0:E0 + E1]
    b1c = sb("b1c", [P, NF1], F32)
    b2w = sb("b2w", [2 * LO_ROW, 2, P], F32R)
    st = sb("st", [P, BT, 6], F32)
    mv = sb("mv", [P, BT, 2], F32)
    var = sb("var", [P, BT], F32)
    rs = sb("rs", [P, BT], F32)
    rt = sb("rt", [P, BT], F32)
    ed = sb("ed", [P, 2, BT, P], F32)
    xn = ed[:, 0]
    oT = ed[:, 1].rearrange("p t d -> p (t d)")
    gtok = r[:, 1, 0:BT * E0].rearrange("p (t e) -> p t e", t=BT)
    gsel = r[:, 1, BT * E0:2 * BT * E0].rearrange("p (t e) -> p t e", t=BT)
    raw = sb("raw", [P, 2, DK], F32)
    psum = top.enter_context(nc.psum_tensor("psum", [P, 8, BLK], F32))

    def bank(k):
        return psum[:, k, :]

    def tiles(k):
        return psum[:, k, :].rearrange("p (t d) -> p t d", t=BT)

    def blk(i, n=BLK):
        return bass.ds(i * n, n)

    x_in = I["L0_attn_x"].rearrange("b s d -> (b s) d").rearrange("(t p) d -> p t d", p=P)
    out_v = out.rearrange("b s d -> (b s) d").rearrange("(t p) d -> p t d", p=P)

    spare_v, spare_p = sb("spare_v", [P, 1], F32), sb("spare_p", [P, 1], F32)

    def apart(e, spare):
        e.tensor_tensor(spare[:], spare[:], spare[:], ALU.mult)

    LN_STEPS = 14

    def ln_dve(e, i, step, xn_ready):
        n = LN_STEPS * i

        def then(ins):
            nonlocal n
            n = n + 1
            ins.then_inc(step, 1)
            e.wait_ge(step, n)

        apart(e, spare_v)
        for t in range(BT):
            last = e.bn_stats(st[:, t, :], x[:, bass.ds(i * BT + t, 1), :].rearrange("p a d -> p (a d)"))
        then(last)
        apart(e, spare_v)
        for t in range(BT):
            last = e.bn_aggr(mv[:, t, :], st[:, t, :])
        then(last)
        then(e.tensor_scalar(var[:], mv[:, :, 1], LN_EPS, None, ALU.add))
        then(e.tensor_scalar(rt[:].bitcast(I32), var[:].bitcast(I32), 1, None, ALU.logical_shift_right))
        then(e.tensor_scalar(rs[:].bitcast(I32), rt[:].bitcast(I32), -1.0, float(MAGIC), ALU.mult, ALU.add))
        for _ in range(3):
            then(e.tensor_tensor(rt[:], rs[:], rs[:], ALU.mult))
            then(e.scalar_tensor_tensor(rt[:], rt[:], -0.5, var[:], ALU.mult, ALU.mult))
            then(e.scalar_tensor_tensor(rs[:], rt[:], 1.5, rs[:], ALU.add, ALU.mult))
        for t in range(BT):
            last = e.tensor_scalar(xn[:, t, :], x[:, bass.ds(i * BT + t, 1), :].rearrange("p a d -> p (a d)"),
                                   mv[:, t, 0:1], rs[:, t:t + 1], ALU.subtract, ALU.mult)
        last.then_inc(xn_ready, 1)

    scope = ExitStack()
    w0 = sb("w0", [P, 2, 3, P], F32R, scope)
    wo0 = sb("wo0", [P, P], F32, scope)
    bcol = sb("bcol", [P, 3], F32, scope)
    borow = sb("borow", [1, P], F32, scope)
    onerow = sb("onerow", [1, P], F32, scope)
    headones = sb("headones", [P, P], F32, scope)
    pbd = sb("pbd", [P, NCH * P], F32, scope)
    m32 = sb("m32", [P, KVW], F32, scope)
    m4 = sb("m4", [P, HPC], F32, scope)
    vones = sb("vones", [P, BT, NCH, KVW + 1], F32, scope)
    kvbd = sb("kvbd", [P, BATCH, NCH, KVW + HPC], F32, scope)
    setup_mem = ExitStack()
    rawU = sb("rawU", [P, E0, F0], F32, setup_mem)
    rawD = sb("rawD", [P, NF0, P], F32, setup_mem)
    rawS = sb("rawS", [E0, P], F32, setup_mem)
    rawG = sb("rawG", [P, E1], F32, setup_mem)
    rawB1 = sb("rawB1", [NF1, P], F32, setup_mem)
    rawB2 = sb("rawB2", [2 * LO_ROW, P], F32, setup_mem)
    rawA = sb("rawA", [P, 3, P], F32, setup_mem)
    rawP = sb("rawP", [P, NCH, HD0], F32, setup_mem)
    bigP = sb("bigP", [P, NCH, H0, HD0], F32, setup_mem)
    pick32 = sb("pick32", [2 * LO_ROW, PICK], F32, setup_mem)
    setup_mem.close()
    aT = sb("aT", [P, BLK], F32, scope)
    vT = sb("vT", [P, BLK], F32, scope)
    sq = sb("sq", [P, BLK], F32, scope)
    nrm = sb("nrm", [P, BLK], F32, scope)
    an = sb("an", [P, BLK], F32, scope)
    feat = sb("feat", [P, NCH, BLK], F32, scope)
    den = sb("den", [P, BT, H0], F32, scope)
    o0 = sb("o0", [P, BT, P], F32, scope)
    o0T = sb("o0T", [P, BLK], F32, scope)
    scope.close()
    m_up = sb("m_up", [P, 2, NF1 * P], F32R)
    m_dn = sb("m_dn", [P, 2, NF1 * P], F32R)

    f_uph, f_upl = wreg[:, 0, :], wreg[:, 1, :]
    f_dnh, f_dnl = wreg[:, 2, :], wreg[:, 3, :]
    NV = H1 * DK
    v_h, v_l, o_h, o_l = (wreg[:, k // 2, (k % 2) * NV:(k % 2 + 1) * NV] for k in range(4))

    def setup():
        x_load, w_load = sem("x_load"), sem("w_load")
        consts, fixed, cast, wsplit = sem("consts"), sem("fixed"), sem("cast"), sem("wsplit")
        tr_done, tr_out, a_hi, selT_lo = sem("tr_done"), sem("tr_out"), sem("a_hi"), sem("selT_lo")
        step, xn_ready, xT_done, xh_done, xl_done = (sem("s_" + s) for s in (
            "step", "xn_ready", "xT_done", "xh_done", "xl_done"))
        zeroed, b2_zero = sem("zeroed"), sem("b2_zero")
        NLOAD = 17

        with nc.Block() as block:
            @block.sync
            def _(sp):
                for i in range(2):
                    sp.dma_start(x[:, blk(i, NT // 2), :], x_in[:, blk(i, NT // 2), :]).then_inc(x_load, 16)
                sp.dma_start(rawS[:], I["L0_ffn_expert_sel"]).then_inc(w_load, 16)
                sp.dma_start(rawU[:], I["L0_ffn_keys"].rearrange("e d f -> d e f")).then_inc(w_load, 16)
                sp.dma_start(rawD[:], I["L0_ffn_values"].rearrange("(j e) f d -> (e f) j d", e=2)).then_inc(w_load, 16)
                sp.dma_start(rawG[:], I["L1_ffn_Wg"]).then_inc(w_load, 16)
                sp.dma_start(rawB1[:], I["L1_ffn_b1"].rearrange("e (q p) -> (e q) p", p=P)).then_inc(w_load, 16)
                sp.wait_ge(b2_zero, 1)
                for k in range(2):
                    sp.dma_start(rawB2[LO_ROW * k:LO_ROW * k + E1, :], I["L1_ffn_b2"]).then_inc(w_load, 16)
                sp.dma_start(rawP[:], I["L0_attn_projection"].rearrange("(c h) f d -> (h f) c d", c=NCH)).then_inc(w_load, 16)
                for k, n in enumerate("qkv"):
                    sp.dma_start(rawA[:, k, :], I["L0_attn_W" + n]).then_inc(w_load, 16)
                    sp.dma_start(bcol[:, k:k + 1], I["L0_attn_b" + n].rearrange("(p a) -> p a", a=1)).then_inc(w_load, 16)
                sp.dma_start(wo0[:], I["L0_attn_Wo"]).then_inc(w_load, 16)
                sp.dma_start(borow[:], I["L0_attn_bo"].rearrange("(a p) -> a p", a=1)).then_inc(w_load, 16)
                sp.dma_start(gate[:, 0, 0:1], I["L0_attn_bo"].rearrange("(p a) -> p a", a=1)).then_inc(w_load, 16)

            @block.gpsimd
            def _(pool):
                pool.memset(rawB2[:], 0.0).then_inc(b2_zero, 1)
                n = 0

                def then(ins):
                    nonlocal n
                    n += 1
                    ins.then_inc(fixed, 1)
                    pool.wait_ge(fixed, n)

                def select(m, pattern, base, cm, op, fill):
                    then(pool.affine_select(out=m, in_=m, compare_op=op, fill=fill, base=base,
                                            pattern=pattern, channel_multiplier=cm))

                then(pool.memset(ident[:], 0.0))
                select(ident[:], [[-1, P]], 0, 1, ALU.not_equal, 1.0)
                pool.tensor_copy(identb[:], ident[:]).then_inc(consts, 1)
                then(pool.memset(before[:], 1.0))
                select(before[:], [[1, P]], 0, -1, ALU.is_gt, 0.0)
                pool.memset(onesb[:], 1.0).then_inc(consts, 1)
                then(pool.memset(cmask[:], 0.0))
                select(cmask[:], [[-1, P]], 0, 1, ALU.is_ge, MASKED)
                pool.iota(iota[:], [[1, 32]], base=0, channel_multiplier=0,
                          allow_small_or_imprecise_dtypes=True).then_inc(consts, 1)
                pool.iota(iota8[:], [[1, E1]], base=-E1, channel_multiplier=0,
                          allow_small_or_imprecise_dtypes=True)
                pool.memset(onerow[:], 1.0).then_inc(consts, 1)
                then(pool.memset(headones[:], 1.0))
                v = headones[:].rearrange("p (g d) -> p g d", d=HD0)
                select(v, [[-HD0, H0], [0, HD0]], 0, 1, ALU.is_ge, 0.0)
                select(v, [[HD0, H0], [0, HD0]], HD0 - 1, -1, ALU.is_ge, 0.0)
                then(pool.memset(m32[:], 1.0))
                v = m32[:].rearrange("p (g d) -> p g d", d=HD0)
                select(v, [[-FEAT0, HPC], [0, HD0]], 0, 1, ALU.is_ge, 0.0)
                select(v, [[FEAT0, HPC], [0, HD0]], FEAT0 - 1, -1, ALU.is_ge, 0.0)
                then(pool.memset(m4[:], 1.0))
                select(m4[:], [[-FEAT0, HPC]], 0, 1, ALU.is_ge, 0.0)
                select(m4[:], [[FEAT0, HPC]], FEAT0 - 1, -1, ALU.is_ge, 0.0)
                then(pool.memset(pick32[:], 0.0))
                for base in (0, -LO_ROW):
                    select(pick32[:, 0:E1 * P], [[-1, E1], [0, P]], base, 1, ALU.not_equal, 1.0)
                    select(pick32[:, E1 * P:], [[-1, E0 - E1], [0, 64]], base - E1, 1, ALU.not_equal, 1.0)
                pool.tensor_copy(pick[:], pick32[:]).then_inc(consts, 1)
                pool.memset(spare_p[:], 0.0)
                pool.memset(vones[:], 1.0).then_inc(consts, 1)
                pool.wait_ge(w_load, 16 * NLOAD)
                for c in range(NCH):
                    then(pool.tensor_copy(bigP[:, c], rawP[:, c:c + 1, :].to_broadcast([P, H0, HD0])))
                    select(bigP[:, c], [[-FEAT0, H0], [0, HD0]], FEAT0 * HPC * c, 1, ALU.is_ge, 0.0)
                    select(bigP[:, c], [[FEAT0, H0], [0, HD0]], FEAT0 - 1 - FEAT0 * HPC * c, -1, ALU.is_ge, 0.0)
                pool.tensor_copy(iota[0:1, 0:1], iota[0:1, 0:1]).then_inc(consts, 1)
                k = 0
                for hi, lo, w in ((f_uph, f_upl, rawU[:].rearrange("p e f -> p (e f)")),
                                  (f_dnh, f_dnl, rawD[:].rearrange("p j d -> p (j d)")),
                                  (w0[:, 0], w0[:, 1], rawA[:]),
                                  (b2w[:, 0], b2w[:, 1], rawB2[:])):
                    pool.tensor_copy(hi, w).then_inc(cast, 1)
                    k += 1
                    pool.wait_ge(cast, k)
                    pool.tensor_tensor(lo, w, hi.bitcast(F32), ALU.subtract).then_inc(wsplit, 1)
                pool.memset(gT[:].bitcast(F32), 0.0).then_inc(wsplit, 1)

            @block.tensor
            def _(pe):
                pe.wait_ge(w_load, 16 * NLOAD)
                pe.wait_ge(consts, 7)
                pe.transpose(bank(2)[:, 0:E0], rawS[:], ident[0:E0, 0:E0]).then_inc(tr_done, 1)
                pe.transpose(bank(3)[:, 0:NF1], rawB1[:], ident[0:NF1, 0:NF1]).then_inc(tr_done, 1)
                for c in range(NCH):
                    last = pe.transpose(tiles(4)[:, c, :], bigP[:, c].rearrange("p h d -> p (h d)"), ident[:])
                last.then_inc(tr_done, 1)
                with pe.Fori(0, NB) as i:
                    pe.wait_ge(xn_ready, i + 1)
                    pe.wait_ge(xl_done, i)
                    for t in range(BT):
                        last = pe.transpose(tiles(0)[:, t, :], xn[:, t, :], ident[:])
                    last.then_inc(xT_done, 1)

            @block.scalar
            def _(act):
                act.wait_ge(tr_done, 3)
                act.wait_ge(zeroed, 3)
                act.activation(selw[:, 0], bank(2)[:, 0:E0], ACT.Copy).then_inc(a_hi, 1)
                act.activation(wgw[:, 0], rawG[:], ACT.Copy).then_inc(a_hi, 1)
                act.activation(b1c[:], bank(3)[:, 0:NF1], ACT.Copy).then_inc(tr_out, 1)
                act.activation(pbd[:], bank(4), ACT.Copy).then_inc(tr_out, 1)
                with act.Fori(0, NB) as i:
                    act.wait_ge(xT_done, i + 1)
                    act.activation(xh[:, blk(i)], bank(0), ACT.Copy).then_inc(xh_done, 1)

            @block.vector
            def _(dve):
                dve.memset(routers[:].bitcast(F32), 0.0).then_inc(zeroed, 1)
                dve.memset(spare_v[:], 0.0).then_inc(zeroed, 1)
                dve.memset(kvbd[:], 0.0).then_inc(zeroed, 1)
                dve.wait_ge(zeroed, 3)
                dve.wait_ge(x_load, 32)
                with dve.Fori(0, NB) as i:
                    dve.wait_ge(xT_done, i)
                    ln_dve(dve, i, step, xn_ready)
                    dve.wait_ge(xh_done, i + 1)
                    dve.tensor_tensor(xl[:, blk(i)], bank(0), xh[:, blk(i)].bitcast(F32),
                                      ALU.subtract).then_inc(xl_done, 1)
                dve.wait_ge(a_hi, 2)
                dve.tensor_tensor(selw[:, 1], bank(2)[:, 0:E0], selw[:, 0].bitcast(F32),
                                  ALU.subtract).then_inc(selT_lo, 1)
                dve.tensor_tensor(wgw[:, 1], rawG[:], wgw[:, 0].bitcast(F32),
                                  ALU.subtract).then_inc(selT_lo, 1)

    top8 = sb("top8", [P, BT, 8], F32)
    idx8 = sb("idx8", [P, BT, 8], U32)

    def product3(pe, dst, wh, wl, i, start=True, stop=True):
        pe.matmul(dst, wh, xl[:, blk(i)], start=start, stop=False)
        pe.matmul(dst, wl, xh[:, blk(i)], start=False, stop=False)
        return pe.matmul(dst, wh, xh[:, blk(i)], start=False, stop=stop)

    def route_ffn(ph, load_moe):
        names = ("logit_done", "gate_e", "gate_t", "g_in", "max_done", "idx_done", "eq_done", "val_done",
                 "gate_set", "gT_ps", "gT_hi", "gT_lo")
        S = {n: sem(f"{ph}_{n}") for n in names}
        gE = r[:, 0, :]
        eq = hg[:].rearrange("p a b -> p (a b)")[:, 0:BT * TOP0 * E0].rearrange("p (t k e) -> p t k e", t=BT, k=TOP0)
        with nc.Block() as block:
            @block.tensor
            def _(pe):
                with pe.Fori(0, NB) as i:
                    product3(pe, bank(0), routers[:, 0], routers[:, 1], i).then_inc(S["logit_done"], 1)
                    pe.wait_ge(S["gate_e"], i + 1)
                    for t in range(BT):
                        last = pe.transpose(tiles(1)[:, t, :], gE[:, t * P:(t + 1) * P], ident[:])
                    last.then_inc(S["gate_t"], 1)
                    pe.wait_ge(S["gate_set"], i + 1)
                    for t in range(BT):
                        last = pe.transpose(bank(2)[0:E0, t * P:(t + 1) * P], gsel[:, t, :], ident[:])
                    last.then_inc(S["gT_ps"], 1)

            @block.scalar
            def _(act):
                with act.Fori(0, NB) as i:
                    act.wait_ge(S["logit_done"], i + 1)
                    act.activation(gE, bank(0), ACT.Sigmoid).then_inc(S["gate_e"], 1)
                    act.wait_ge(S["gT_ps"], i + 1)
                    act.activation(gT[0:E0, blk(i)], bank(2)[0:E0, :], ACT.Copy).then_inc(S["gT_hi"], 1)

            @block.vector
            def _(dve):
                with dve.Fori(0, NB) as i:
                    dve.wait_ge(S["gate_t"], i + 1)
                    dve.tensor_copy(gtok, tiles(1)[:, :, 0:E0]).then_inc(S["g_in"], 1)
                    dve.wait_ge(S["g_in"], i + 1)
                    apart(dve, spare_v)
                    for t in range(BT):
                        last = dve.max(top8[:, t, :], gtok[:, t, :])
                    last.then_inc(S["max_done"], 1)
                    dve.wait_ge(S["max_done"], i + 1)
                    apart(dve, spare_v)
                    for t in range(BT):
                        last = dve.max_index(idx8[:, t, :], top8[:, t, :], gtok[:, t, :])
                    last.then_inc(S["idx_done"], 1)
                    dve.wait_ge(S["idx_done"], i + 1)
                    dve.tensor_tensor(eq, iota[:].unsqueeze(1).unsqueeze(1).to_broadcast([P, BT, TOP0, E0]),
                                      idx8[:, :, 0:TOP0].unsqueeze(3).to_broadcast([P, BT, TOP0, E0]),
                                      ALU.is_equal).then_inc(S["eq_done"], 1)
                    dve.wait_ge(S["eq_done"], i + 1)
                    dve.tensor_tensor(eq, eq, top8[:, :, 0:TOP0].unsqueeze(3).to_broadcast([P, BT, TOP0, E0]),
                                      ALU.mult).then_inc(S["val_done"], 1)
                    dve.wait_ge(S["val_done"], i + 1)
                    dve.tensor_reduce(gsel, eq.rearrange("p t k e -> p t e k"), AX.X,
                                      ALU.add).then_inc(S["gate_set"], 1)
                    dve.wait_ge(S["gT_hi"], i + 1)
                    dve.tensor_tensor(gT[LO_ROW:LO_ROW + E0, blk(i)], bank(2)[0:E0, :],
                                      gT[0:E0, blk(i)].bitcast(F32), ALU.subtract).then_inc(S["gT_lo"], 1)

            if load_moe:
                m_load, m_cast, m_split = sem("m_load"), sem("m_cast"), sem("m_split")

                @block.sync
                def _(sp):
                    with sp.Fori(0, E1) as e:
                        sp.wait_ge(m_split, 2 * e)
                        sp.dma_start(ed[:, 0].rearrange("p t d -> p (t d)"),
                                     I["L1_ffn_W1"].rearrange("e d f -> d e f")[:, bass.ds(e, 1), :]
                                     .rearrange("d a f -> d (a f)")).then_inc(m_load, 16)
                        sp.dma_start(ed[:, 1],
                                     I["L1_ffn_W2"].rearrange("e (q p) d -> p (e q) d", p=P)[:, blk(e, BT), :]
                                     ).then_inc(m_load, 16)

                @block.gpsimd
                def _(pool):
                    with pool.Fori(0, E1) as e:
                        pool.wait_ge(m_load, 32 * e + 32)
                        for k, w in enumerate((m_up, m_dn)):
                            raw_w = ed[:, k].rearrange("p t d -> p (t d)")
                            apart(pool, spare_p)
                            pool.tensor_copy(w[:, 0, blk(e)], raw_w).then_inc(m_cast, 1)
                            pool.wait_ge(m_cast, 2 * e + k + 1)
                            pool.tensor_tensor(w[:, 1, blk(e)], raw_w, w[:, 0, blk(e)].bitcast(F32),
                                               ALU.subtract).then_inc(m_split, 1)

    def gated(ph, nf, up, dn, per_gate, func, bias, b2, scale, final):
        names = ("up_done", "g_done", "act_done", "hg_done", "hi_done", "lo_done", "dn_done", "oT_ready",
                 "back_done", "added", "xn_ready", "xT_done", "xh_done", "xl_done", "step", "stored")
        S = {n: sem(f"{ph}_{n}") for n in names}
        B_UP, B_G, B_OUT, B_BACK, B_XT = (0, 1), (2, 3), 4, 5, 6
        AT_EVAC, AT_BACK, AT_ADD, AT_XT = LAG, LAG + 2, LAG + 2, nf - 1

        def col(w, j):
            return w[:, j * P:(j + 1) * P]

        def picker(j):
            if per_gate > 1:
                at = j // per_gate * P
            else:
                at = 2 * j * P + 64 if 2 * j < E1 else E1 * P + (2 * j - E1) * 64
            return pick[:, at:at + P]

        with nc.Block() as block:
            @block.tensor
            def _(pe):
                def up_product(i, j, first):
                    n = i * nf + j
                    if not first or j >= 2:
                        pe.wait_ge(S["act_done"], n - 1)
                    q = j // per_gate
                    if j % per_gate == 0 and (not first or q >= 2):
                        pe.wait_ge(S["hg_done"], n - per_gate)
                    product3(pe, bank(B_UP[j % 2]), col(up[0], j), col(up[1], j), i).then_inc(S["up_done"], 1)
                    if j % per_gate == 0:
                        pe.matmul(bank(B_G[q % 2]), picker(j), gT[:, blk(i)], start=True,
                                  stop=True).then_inc(S["g_done"], 1)

                def down_product(i, j, first):
                    n = i * nf + j
                    s = j % SLOTS
                    if j == 0 and not first:
                        pe.wait_ge(S["oT_ready"], i)
                    pe.wait_ge(S["lo_done"], n + 1)
                    pe.matmul(bank(B_OUT), col(dn[1], j), hh[:, s, :], start=(j == 0), stop=False)
                    pe.matmul(bank(B_OUT), col(dn[0], j), hl[:, s, :], start=False, stop=False)
                    last = pe.matmul(bank(B_OUT), col(dn[0], j), hh[:, s, :], start=False,
                                     stop=(j == nf - 1 and b2 is None))
                    if j == nf - 1 and b2 is not None:
                        pe.matmul(bank(B_OUT), b2[:, 1], gT[:, blk(i)], start=False, stop=False)
                        last = pe.matmul(bank(B_OUT), b2[:, 0], gT[:, blk(i)], start=False, stop=True)
                    last.then_inc(S["dn_done"], 1)

                def back(i, first):
                    pe.wait_ge(S["oT_ready"], i + 1)
                    if not first:
                        pe.wait_ge(S["added"], i)
                    for t in range(BT):
                        last = pe.transpose(tiles(B_BACK)[:, t, :], oT[:, t * P:(t + 1) * P], ident[:])
                    last.then_inc(S["back_done"], 1)

                def next_xT(i, first):
                    if final:
                        return
                    pe.wait_ge(S["xn_ready"], i + 1)
                    if not first:
                        pe.wait_ge(S["xl_done"], i)
                    for t in range(BT):
                        last = pe.transpose(tiles(B_XT)[:, t, :], xn[:, t, :], ident[:])
                    last.then_inc(S["xT_done"], 1)

                def one_block(i, at):
                    for j in range(nf):
                        up_product(i, j, at == 0)
                        if at >= 1 or j >= LAG:
                            down_product(i - (j < LAG), (j - LAG) % nf, at == 0 or (at == 1 and j < LAG))
                        if at >= 1 and j == AT_BACK:
                            back(i - 1, at == 1)
                        if at >= 1 and j == AT_XT:
                            next_xT(i - 1, at == 1)

                one_block(0, 0)
                one_block(1, 1)
                with pe.Fori(2, NB) as i:
                    one_block(i, 2)
                for j in range(nf - LAG, nf):
                    down_product(NB - 1, j, False)
                back(NB - 1, False)
                next_xT(NB - 1, False)

            @block.scalar
            def _(act):
                def activate(i, j, first):
                    n = i * nf + j
                    act.wait_ge(S["up_done"], n + 1)
                    if not first or j >= 2:
                        act.wait_ge(S["hg_done"], n - 1)
                    act.activation(r[:, j % 2, :], bank(B_UP[j % 2]), func,
                                   **({} if bias is None else {"bias": bias[:, j:j + 1]})).then_inc(S["act_done"], 1)

                def high(i, j, first):
                    n = i * nf + j
                    act.wait_ge(S["hg_done"], n + 1)
                    if not first or j >= SLOTS:
                        act.wait_ge(S["dn_done"], n - SLOTS + 1)
                    act.activation(hh[:, j % SLOTS, :], hg[:, j % 2, :], ACT.Copy).then_inc(S["hi_done"], 1)

                def evacuate(i, first):
                    act.wait_ge(S["dn_done"], nf * i + nf)
                    if not first:
                        act.wait_ge(S["back_done"], i)
                    act.activation(oT, bank(B_OUT), ACT.Copy, scale=scale).then_inc(S["oT_ready"], 1)

                def next_high(i):
                    if not final:
                        act.wait_ge(S["xT_done"], i + 1)
                        act.activation(xh[:, blk(i)], bank(B_XT), ACT.Copy).then_inc(S["xh_done"], 1)

                def one_block(i, at):
                    for j in range(nf):
                        activate(i, j, at == 0)
                        if at >= 1 or j >= 1:
                            high(i - (j < 1), (j - 1) % nf, at == 0 or (at == 1 and j < 1))
                        if at >= 1 and j == AT_EVAC:
                            evacuate(i - 1, at == 1)
                        if at >= 2 and j == 0:
                            next_high(i - 2)

                one_block(0, 0)
                one_block(1, 1)
                with act.Fori(2, NB) as i:
                    one_block(i, 2)
                high(NB - 1, nf - 1, False)
                next_high(NB - 2)
                evacuate(NB - 1, False)
                next_high(NB - 1)

            @block.vector
            def _(dve):
                def apply_gate(i, j, first):
                    n = i * nf + j
                    dve.wait_ge(S["act_done"], n + 1)
                    dve.wait_ge(S["g_done"], n // per_gate + 1 if first and isinstance(n, int)
                                else i * (nf // per_gate) + j // per_gate + 1)
                    if not first or j >= 2:
                        dve.wait_ge(S["lo_done"], n - 1)
                    dve.tensor_tensor(hg[:, j % 2, :], r[:, j % 2, :], bank(B_G[(j // per_gate) % 2]),
                                      ALU.mult).then_inc(S["hg_done"], 1)

                def add_residual(i, first):
                    dve.wait_ge(S["back_done"], i + 1)
                    xb = x[:, blk(i, BT), :]
                    dve.tensor_tensor(xb, xb, tiles(B_BACK), ALU.add).then_inc(S["added"], 1)
                    if not final:
                        dve.wait_ge(S["added"], i + 1)
                        if not first:
                            dve.wait_ge(S["xT_done"], i)
                        ln_dve(dve, i, S["step"], S["xn_ready"])

                def next_low(i):
                    if not final:
                        dve.wait_ge(S["xh_done"], i + 1)
                        dve.tensor_tensor(xl[:, blk(i)], bank(B_XT), xh[:, blk(i)].bitcast(F32),
                                          ALU.subtract).then_inc(S["xl_done"], 1)

                def one_block(i, at):
                    for j in range(nf):
                        apply_gate(i, j, at == 0)
                        if at >= 1 and j == AT_ADD:
                            add_residual(i - 1, at == 1)
                        if at >= 2 and j == 1:
                            next_low(i - 2)

                one_block(0, 0)
                one_block(1, 1)
                with dve.Fori(2, NB) as i:
                    one_block(i, 2)
                next_low(NB - 2)
                add_residual(NB - 1, False)
                next_low(NB - 1)

            @block.gpsimd
            def _(pool):
                def low(i, j, first):
                    n = i * nf + j
                    pool.wait_ge(S["hi_done"], n + 1)
                    if not first or j >= SLOTS:
                        pool.wait_ge(S["dn_done"], n - SLOTS + 1)
                    pool.tensor_tensor(hl[:, j % SLOTS, :], hg[:, j % 2, :], hh[:, j % SLOTS, :].bitcast(F32),
                                       ALU.subtract).then_inc(S["lo_done"], 1)

                for j in range(nf):
                    low(0, j, True)
                with pool.Fori(1, NB) as i:
                    for j in range(nf):
                        low(i, j, False)

            if final:
                @block.sync
                def _(sp):
                    for i in range(NB):
                        sp.wait_ge(S["added"], i + 1)
                        sp.dma_start(out_v[:, blk(i, BT), :], x[:, blk(i, BT), :]).then_inc(S["stored"], 16)
                    sp.wait_ge(S["stored"], 16 * NB)

    def linear_kv():
        names = ("k_done", "v_done", "aT_ready", "sq_ready", "vT_ready", "n_done", "root", "eps", "inv", "an_ready",
                 "vt_done", "v_ready", "f_done", "f_ready", "kv_done", "kv_read")
        S = {n: sem(f"a0_{n}") for n in names}
        B_K, B_V, B_N, B_VT, B_F, B_KV = 0, 1, 2, 3, (4, 5), 6
        kv = bank(B_KV)[:, 0:NCH * (KVW + 1)].rearrange("p (c w) -> p c w", c=NCH)
        UNROLL = SEQ // BLK

        with nc.Block() as block:
            @block.tensor
            def _(pe):
                with pe.Fori(0, BATCH) as b:
                    for u in range(UNROLL):
                        i = b * UNROLL + u
                        pe.wait_ge(S["sq_ready"], i)
                        product3(pe, bank(B_K), w0[:, 0, 1], w0[:, 1, 1], i).then_inc(S["k_done"], 1)
                        pe.wait_ge(S["vT_ready"], i)
                        product3(pe, bank(B_V), w0[:, 0, 2], w0[:, 1, 2], i).then_inc(S["v_done"], 1)
                        pe.wait_ge(S["sq_ready"], i + 1)
                        pe.matmul(bank(B_N), headones[:], sq[:], start=True, stop=True).then_inc(S["n_done"], 1)
                        pe.wait_ge(S["vT_ready"], i + 1)
                        pe.wait_ge(S["v_ready"], i)
                        for t in range(BT):
                            last = pe.transpose(tiles(B_VT)[:, t, :], vT[:, t * P:(t + 1) * P], ident[:])
                        last.then_inc(S["vt_done"], 1)
                        pe.wait_ge(S["an_ready"], i + 1)
                        for t in range(BT):
                            n = i * BT + t
                            if t >= 2:
                                pe.wait_ge(S["f_ready"], n - 1)
                            pe.matmul(bank(B_F[t % 2]), an[:, t * P:(t + 1) * P], pbd[:], start=True,
                                      stop=True).then_inc(S["f_done"], 1)
                        if u == 0:
                            pe.wait_ge(S["kv_read"], b)
                        pe.wait_ge(S["v_ready"], i + 1)
                        for t in range(BT):
                            pe.wait_ge(S["f_ready"], i * BT + t + 1)
                            for c in range(NCH):
                                last = pe.matmul(kv[:, c, :], feat[:, t, c * P:(c + 1) * P], vones[:, t, c, :],
                                                 start=(u == 0 and t == 0 and c == 0),
                                                 stop=(u == UNROLL - 1 and t == BT - 1), skip_group_check=True)
                        last.then_inc(S["kv_done"], 1)

            @block.scalar
            def _(act):
                with act.Fori(0, NB) as i:
                    act.wait_ge(S["k_done"], i + 1)
                    act.wait_ge(S["an_ready"], i)
                    act.activation(aT[:], bank(B_K), ACT.Identity, bias=bcol[:, 1:2]).then_inc(S["aT_ready"], 1)
                    act.activation(sq[:], bank(B_K), ACT.Square, bias=bcol[:, 1:2]).then_inc(S["sq_ready"], 1)
                    act.wait_ge(S["v_done"], i + 1)
                    act.wait_ge(S["vt_done"], i)
                    act.activation(vT[:], bank(B_V), ACT.Identity, bias=bcol[:, 2:3]).then_inc(S["vT_ready"], 1)
                    act.wait_ge(S["n_done"], i + 1)
                    act.activation(nrm[:], bank(B_N), ACT.Sqrt).then_inc(S["root"], 1)

            @block.vector
            def _(dve):
                with dve.Fori(0, BATCH) as b:
                    for u in range(UNROLL):
                        i = b * UNROLL + u
                        dve.wait_ge(S["root"], i + 1)
                        dve.tensor_scalar(nrm[:], nrm[:], NORM_EPS, None, ALU.add).then_inc(S["eps"], 1)
                        dve.wait_ge(S["eps"], i + 1)
                        dve.reciprocal(nrm[:], nrm[:]).then_inc(S["inv"], 1)
                        dve.wait_ge(S["inv"], i + 1)
                        dve.wait_ge(S["f_done"], i * BT)
                        dve.tensor_tensor(an[:], aT[:], nrm[:], ALU.mult).then_inc(S["an_ready"], 1)
                        dve.wait_ge(S["vt_done"], i + 1)
                        dve.wait_ge(S["kv_done"], i)
                        dve.tensor_copy(vones[:, :, :, 0:KVW],
                                        tiles(B_VT).rearrange("p t (c w) -> p t c w", c=NCH)).then_inc(S["v_ready"], 1)
                        for t in range(BT):
                            dve.wait_ge(S["f_done"], i * BT + t + 1)
                            dve.tensor_scalar(feat[:, t, :], bank(B_F[t % 2]), 0.0, YAT_EPS, ALU.max,
                                              ALU.add).then_inc(S["f_ready"], 1)
                    dve.wait_ge(S["kv_done"], UNROLL * b + UNROLL)
                    mine = kvbd[:, bass.ds(b, 1)].rearrange("p a c w -> p (a c) w")
                    dve.tensor_tensor(mine[:, :, 0:KVW], kv[:, :, 0:KVW],
                                      m32[:].unsqueeze(1).to_broadcast([P, NCH, KVW]), ALU.mult)
                    dve.tensor_tensor(mine[:, :, KVW:KVW + HPC], kv[:, :, KVW:KVW + 1].to_broadcast([P, NCH, HPC]),
                                      m4[:].unsqueeze(1).to_broadcast([P, NCH, HPC]), ALU.mult).then_inc(S["kv_read"], 1)

    def linear_q():
        names = ("q_done", "aT_ready", "sq_ready", "n_done", "root", "eps", "inv", "an_ready", "f_done", "f_ready",
                 "qkv_done", "den_max", "den_inv", "o_ready", "oT_done", "oT_ready", "y_done", "added", "step",
                 "xn_ready", "xT_done", "xh_done", "xl_done")
        S = {n: sem(f"a0q_{n}") for n in names}
        B_Q, B_N, B_F, B_OT, B_Y, B_XT, B_QKV = 0, 0, (4, 5), 3, 1, 2, (6, 7)
        UNROLL = SEQ // BLK
        W = KVW + HPC

        with nc.Block() as block:
            @block.tensor
            def _(pe):
                with pe.Fori(0, BATCH) as b:
                    for u in range(UNROLL):
                        i = b * UNROLL + u
                        pe.wait_ge(S["root"], i)
                        product3(pe, bank(B_Q), w0[:, 0, 0], w0[:, 1, 0], i).then_inc(S["q_done"], 1)
                        pe.wait_ge(S["sq_ready"], i + 1)
                        pe.matmul(bank(B_N), headones[:], sq[:], start=True, stop=True).then_inc(S["n_done"], 1)
                        pe.wait_ge(S["an_ready"], i + 1)
                        for c in range(NCH):
                            n = i * NCH + c
                            if c >= 2:
                                pe.wait_ge(S["f_ready"], n - 1)
                            pe.matmul(bank(B_F[c % 2]), pbd[:, c * P:(c + 1) * P], an[:], start=True,
                                      stop=True).then_inc(S["f_done"], 1)
                        pe.wait_ge(S["f_ready"], i * NCH + NCH)
                        pe.wait_ge(S["o_ready"], i)
                        for t in range(BT):
                            for c in range(NCH):
                                at = (t % 2 * NCH + c) * W
                                last = pe.matmul(bank(B_QKV[t // 2])[:, at:at + W], feat[:, c, t * P:(t + 1) * P],
                                                 kvbd[:, bass.ds(b, 1), c, :].rearrange("p a w -> p (a w)"),
                                                 start=True, stop=True)
                        last.then_inc(S["qkv_done"], 1)
                        pe.wait_ge(S["o_ready"], i + 1)
                        for t in range(BT):
                            last = pe.transpose(tiles(B_OT)[:, t, :], o0[:, t, :], ident[:])
                        last.then_inc(S["oT_done"], 1)
                        pe.wait_ge(S["oT_ready"], i + 1)
                        for t in range(BT):
                            pe.matmul(tiles(B_Y)[:, t, :], o0T[:, t * P:(t + 1) * P], wo0[:], start=True, stop=False)
                            last = pe.matmul(tiles(B_Y)[:, t, :], onerow[:], borow[:], start=False, stop=True)
                        last.then_inc(S["y_done"], 1)
                        pe.wait_ge(S["xn_ready"], i + 1)
                        pe.wait_ge(S["xl_done"], i)
                        for t in range(BT):
                            last = pe.transpose(tiles(B_XT)[:, t, :], xn[:, t, :], ident[:])
                        last.then_inc(S["xT_done"], 1)

            @block.scalar
            def _(act):
                with act.Fori(0, NB) as i:
                    act.wait_ge(S["q_done"], i + 1)
                    act.wait_ge(S["an_ready"], i)
                    act.activation(aT[:], bank(B_Q), ACT.Identity, bias=bcol[:, 0:1]).then_inc(S["aT_ready"], 1)
                    act.activation(sq[:], bank(B_Q), ACT.Square, bias=bcol[:, 0:1]).then_inc(S["sq_ready"], 1)
                    act.wait_ge(S["n_done"], i + 1)
                    act.activation(nrm[:], bank(B_N), ACT.Sqrt).then_inc(S["root"], 1)
                    act.wait_ge(S["oT_done"], i + 1)
                    act.activation(o0T[:], bank(B_OT), ACT.Copy).then_inc(S["oT_ready"], 1)
                    act.wait_ge(S["xT_done"], i + 1)
                    act.activation(xh[:, blk(i)], bank(B_XT), ACT.Copy).then_inc(S["xh_done"], 1)

            @block.vector
            def _(dve):
                with dve.Fori(0, NB) as i:
                    dve.wait_ge(S["root"], i + 1)
                    dve.tensor_scalar(nrm[:], nrm[:], NORM_EPS, None, ALU.add).then_inc(S["eps"], 1)
                    dve.wait_ge(S["eps"], i + 1)
                    dve.reciprocal(nrm[:], nrm[:]).then_inc(S["inv"], 1)
                    dve.wait_ge(S["inv"], i + 1)
                    dve.tensor_tensor(an[:], aT[:], nrm[:], ALU.mult).then_inc(S["an_ready"], 1)
                    for c in range(NCH):
                        dve.wait_ge(S["f_done"], i * NCH + c + 1)
                        dve.tensor_scalar(feat[:, c, :], bank(B_F[c % 2]), 0.0, YAT_EPS, ALU.max,
                                          ALU.add).then_inc(S["f_ready"], 1)
                    dve.wait_ge(S["qkv_done"], i + 1)
                    for g in range(2):
                        acc = bank(B_QKV[g])[:, 0:2 * NCH * W].rearrange("p (t w) -> p t w", w=W)
                        d = den[:, 2 * g:2 * g + 2, :].rearrange("p t (c h) -> p (t c) h", c=NCH)
                        last = dve.tensor_scalar(d, acc[:, :, KVW:W], DEN_MIN, None, ALU.max)
                    last.then_inc(S["den_max"], 1)
                    dve.wait_ge(S["den_max"], i + 1)
                    dve.reciprocal(den[:], den[:]).then_inc(S["den_inv"], 1)
                    dve.wait_ge(S["den_inv"], i + 1)
                    for g in range(2):
                        acc = bank(B_QKV[g])[:, 0:2 * NCH * W].rearrange("p (t w) -> p t w", w=W)
                        d = den[:, 2 * g:2 * g + 2, :].rearrange("p t (c h) -> p (t c) h", c=NCH)
                        last = dve.tensor_tensor(
                            o0[:, 2 * g:2 * g + 2, :].rearrange("p t (c h d) -> p (t c) h d", c=NCH, h=HPC),
                            acc[:, :, 0:KVW].rearrange("p t (h d) -> p t h d", h=HPC),
                            d.unsqueeze(3).to_broadcast([P, 2 * NCH, HPC, HD0]), ALU.mult)
                    last.then_inc(S["o_ready"], 1)
                    dve.wait_ge(S["y_done"], i + 1)
                    xb = x[:, blk(i, BT), :]
                    dve.tensor_tensor(xb, xb, tiles(B_Y), ALU.add).then_inc(S["added"], 1)
                    dve.wait_ge(S["added"], i + 1)
                    ln_dve(dve, i, S["step"], S["xn_ready"])
                    dve.wait_ge(S["xh_done"], i + 1)
                    dve.tensor_tensor(xl[:, blk(i)], bank(B_XT), xh[:, blk(i)].bitcast(F32),
                                      ALU.subtract).then_inc(S["xl_done"], 1)

    def turn_gates(ph, n_exp):
        names = ("g_ready", "g_turned", "g_hi", "g_lo")
        S = {n: sem(f"{ph}_{n}") for n in names}
        with nc.Block() as block:
            @block.vector
            def _(dve):
                with dve.Fori(0, NB) as i:
                    dve.wait_ge(S["g_turned"], i)
                    dve.tensor_copy(gsel[:, :, 0:n_exp], gate[:, blk(i, BT), 0:n_exp]).then_inc(S["g_ready"], 1)
                    dve.wait_ge(S["g_hi"], i + 1)
                    dve.tensor_tensor(gT[LO_ROW:LO_ROW + n_exp, blk(i)], bank(0)[0:n_exp, :],
                                      gT[0:n_exp, blk(i)].bitcast(F32), ALU.subtract).then_inc(S["g_lo"], 1)

            @block.tensor
            def _(pe):
                with pe.Fori(0, NB) as i:
                    pe.wait_ge(S["g_ready"], i + 1)
                    pe.wait_ge(S["g_lo"], i)
                    for t in range(BT):
                        last = pe.transpose(bank(0)[0:n_exp, t * P:(t + 1) * P], gsel[:, t, 0:n_exp], ident[:])
                    last.then_inc(S["g_turned"], 1)

            @block.scalar
            def _(act):
                with act.Fori(0, NB) as i:
                    act.wait_ge(S["g_turned"], i + 1)
                    act.activation(gT[0:n_exp, blk(i)], bank(0)[0:n_exp, :], ACT.Copy).then_inc(S["g_hi"], 1)

    def route_moe(ph, load_vo):
        names = ("logit_done", "lg_ready", "lg_turned", "lg_in", "exp_done", "step", "m_ready", "counted")
        S = {n: sem(f"{ph}_{n}") for n in names}
        lgE = r[:, 0, :]
        N = NT * E1
        space = [hg[:, a, k * N:(k + 1) * N].rearrange("p (t e) -> p t e", t=NT) for a in range(2) for k in range(2)]
        L, G, A, M1 = space
        B2, M2 = (r[:, 1, k * N:(k + 1) * N].rearrange("p (t e) -> p t e", t=NT) for k in range(2))
        small = st16[:]
        if load_vo:
            v_load, o_load0, o_load1, v_cast, v_split, o_turned, o_hi, o_lo = (sem("vo_" + s) for s in (
                "v_load", "o_load0", "o_load1", "v_cast", "v_split", "o_turned", "o_hi", "o_lo"))
            o_load = (o_load0, o_load1)
        with nc.Block() as block:
            @block.tensor
            def _(pe):
                with pe.Fori(0, NB) as i:
                    product3(pe, bank(0), routers[:, 0], routers[:, 1], i).then_inc(S["logit_done"], 1)
                    pe.wait_ge(S["lg_in"], i)
                    pe.wait_ge(S["lg_ready"], i + 1)
                    for t in range(BT):
                        last = pe.transpose(tiles(1)[:, t, :], lgE[:, t * P:(t + 1) * P], ident[:])
                    last.then_inc(S["lg_turned"], 1)
                pe.wait_ge(S["m_ready"], 1)
                pe.matmul(bank(2), before[:], m16[:].rearrange("p t e -> p (t e)"), start=True,
                          stop=True).then_inc(S["counted"], 1)
                pe.matmul(bank(3), onesb[:], m16[:].rearrange("p t e -> p (t e)"), start=True,
                          stop=True).then_inc(S["counted"], 1)
                if load_vo:
                    for k in range(2):
                        pe.wait_ge(o_load[k], 16)
                        for q in range(BT):
                            last = pe.transpose(tiles(4 + k)[:, q, :], ed[:, k, q, :], ident[:])
                        last.then_inc(o_turned, 1)

            @block.scalar
            def _(act):
                with act.Fori(0, NB) as i:
                    act.wait_ge(S["logit_done"], i + 1)
                    act.wait_ge(S["lg_turned"], i)
                    act.activation(lgE, bank(0), ACT.Copy).then_inc(S["lg_ready"], 1)
                act.wait_ge(S["step"], 2)
                act.activation(G, A, ACT.Exp).then_inc(S["exp_done"], 1)
                if load_vo:
                    for k in range(2):
                        act.wait_ge(o_turned, k + 1)
                        act.activation(o_h[:, k * BLK:(k + 1) * BLK], bank(4 + k), ACT.Copy).then_inc(o_hi, 1)

            @block.vector
            def _(dve):
                with dve.Fori(0, NB) as i:
                    dve.wait_ge(S["lg_turned"], i + 1)
                    dve.tensor_copy(L[:, blk(i, BT), :], tiles(1)[:, :, E0:E0 + E1]).then_inc(S["lg_in"], 1)
                dve.wait_ge(S["lg_in"], NB)
                n = 0

                def then(ins):
                    nonlocal n
                    n += 1
                    ins.then_inc(S["step"], 1)
                    dve.wait_ge(S["step"], n)

                def wide(v):
                    return v.unsqueeze(2).to_broadcast([P, NT, E1])

                back8 = iota8[:].unsqueeze(1).to_broadcast([P, NT, E1])
                s1, s2 = small[:, 0, :], small[:, 1, :]

                def first_max(values, mask):
                    then(dve.tensor_reduce(s1, values, AX.X, ALU.max))
                    then(dve.tensor_tensor(A, values, wide(s1), ALU.is_equal))
                    then(dve.tensor_tensor(A, A, back8, ALU.mult))
                    then(dve.tensor_reduce(s2, A, AX.X, ALU.min))
                    then(dve.tensor_tensor(mask, back8, wide(s2), ALU.is_equal))

                then(dve.tensor_reduce(s1, L, AX.X, ALU.max))
                then(dve.tensor_tensor(A, L, wide(s1), ALU.subtract))
                dve.wait_ge(S["exp_done"], 1)
                then(dve.tensor_reduce(s1, G, AX.X, ALU.add))
                then(dve.reciprocal(s2, s1))
                then(dve.tensor_tensor(G, G, wide(s2), ALU.mult))
                first_max(G, M1)
                then(dve.scalar_tensor_tensor(B2, M1, -3e38, L, ALU.mult, ALU.add))
                first_max(B2, M2)
                then(dve.tensor_copy(m16[:, :, 0:E1], M1))
                n += 1
                dve.tensor_copy(m16[:, :, E1:], M2).then_inc(S["step"], 1)
                dve.wait_ge(S["step"], n)
                dve.tensor_copy(small[:, 2, 0:1], small[:, 2, 0:1]).then_inc(S["m_ready"], 1)
                dve.wait_ge(S["counted"], 2)
                c0 = bank(3).rearrange("p (t e) -> p t e", t=NT)
                then(dve.tensor_copy(p16[:, 0], c0))
                src, reach = 0, 1
                while reach < NT:
                    dve.tensor_copy(p16[:, 1 - src, 0:reach, :], p16[:, src, 0:reach, :])
                    then(dve.tensor_tensor(p16[:, 1 - src, reach:, :], p16[:, src, reach:, :],
                                           p16[:, src, 0:NT - reach, :], ALU.add))
                    src, reach = 1 - src, 2 * reach
                tot, pos = p16[:, src], p16[:, 1 - src]
                then(dve.tensor_tensor(pos, tot, c0, ALU.subtract))
                then(dve.tensor_tensor(pos, pos, bank(2).rearrange("p (t e) -> p t e", t=NT), ALU.add))
                then(dve.tensor_tensor(pos[:, :, E1:], pos[:, :, E1:],
                                       tot[:, NT - 1:NT, 0:E1].to_broadcast([P, NT, E1]), ALU.add))
                then(dve.tensor_scalar(pos, pos, float(CAP), None, ALU.is_lt))
                then(dve.tensor_tensor(A, M1, pos[:, :, 0:E1], ALU.mult))
                then(dve.tensor_tensor(B2, M2, pos[:, :, E1:], ALU.mult))
                then(dve.tensor_tensor(B2, A, B2, ALU.add))
                then(dve.tensor_tensor(A, M1, M2, ALU.add))
                then(dve.tensor_tensor(A, A, G, ALU.mult))
                then(dve.tensor_reduce(s1, A, AX.X, ALU.add))
                then(dve.tensor_scalar(s1, s1, GATE_EPS, None, ALU.add))
                then(dve.reciprocal(s2, s1))
                then(dve.tensor_tensor(G, G, B2, ALU.mult))
                then(dve.tensor_tensor(gate[:, :, 0:E1], G, wide(s2), ALU.mult))
                if load_vo:
                    for k in range(2):
                        dve.wait_ge(o_hi, k + 1)
                        dve.tensor_tensor(o_l[:, k * BLK:(k + 1) * BLK], bank(4 + k),
                                          o_h[:, k * BLK:(k + 1) * BLK].bitcast(F32), ALU.subtract).then_inc(o_lo, 1)

            if load_vo:
                HH = H1 // 2

                @block.sync
                def _(sp):
                    for k in range(2):
                        sp.dma_start(ed[:, k].rearrange("p t (a v) -> p (t a) v", a=2),
                                     I["L1_attn_P_v"].rearrange("h d v -> d h v")[:, k * HH:(k + 1) * HH, :]
                                     ).then_inc(v_load, 16)
                    for k in range(2):
                        sp.wait_ge(v_split, k + 1)
                        sp.dma_start(ed[:, k].rearrange("p t (a v) -> p (t a) v", a=2),
                                     I["L1_attn_P_o"].rearrange("h d v -> d h v")[:, k * HH:(k + 1) * HH, :]
                                     ).then_inc(o_load[k], 16)

                @block.gpsimd
                def _(pool):
                    pool.wait_ge(v_load, 32)
                    for k in range(2):
                        w, to = ed[:, k].rearrange("p t d -> p (t d)"), slice(k * BLK, (k + 1) * BLK)
                        pool.tensor_copy(v_h[:, to], w).then_inc(v_cast, 1)
                        pool.wait_ge(v_cast, k + 1)
                        pool.tensor_tensor(v_l[:, to], w, v_h[:, to].bitcast(F32), ALU.subtract).then_inc(v_split, 1)

    def softmax_diagonal():
        names = ("raw_in", "w_cast", "w_ready", "p_done", "q_hi", "q_lo", "k_hi", "k_lo", "sc_done", "mx_done",
                 "exp_done", "dg_done", "red_done", "rec_done", "p_set")
        S = {n: sem(f"a1_{n}") for n in names}
        spare = [wreg[:, 2 + k // 2, (k % 2) * SEQ:(k % 2 + 1) * SEQ] for k in range(4)]
        for tile in (hh, hl):
            flat = tile[:].rearrange("p s n -> p (s n)")
            spare += [flat[:, 0:SEQ], flat[:, SEQ:2 * SEQ]]
        Q2, KH, KL = spare[0:2], spare[2:4], spare[4:6]
        hw = spare[6][:, 0:4 * P].rearrange("p (a s u v) -> p a s u v", a=2, s=2, u=2)
        E = [r[:].rearrange("p s n -> p (s n)"), hg[:].rearrange("p s n -> p (s n)")]
        HALF = QT // 2
        BANKS = [(0, 1), (1, 1), (2, 1), (3, 1), (4, 2), (0, 2), (2, 2), (4, 2)]
        FREED = [-2, -2, -1, -1, 0, 2, 4, 5]
        B_Q, B_K = 6, 7
        PER = BATCH

        def scores(q):
            k, n = BANKS[q]
            return psum[:, k:k + n, :].rearrange("p k n -> p (k n)")

        with nc.Block() as block:
            @block.sync
            def _(sp):
                with sp.Fori(0, H1) as h:
                    sp.wait_ge(S["w_ready"], h)
                    for k, n in enumerate("qk"):
                        sp.dma_start(raw[:, k, :], I["L1_attn_P_" + n].rearrange("h d v -> d h v")[:, bass.ds(h, 1), :]
                                     .rearrange("d a v -> d (a v)")).then_inc(S["raw_in"], 16)

            @block.gpsimd
            def _(pool):
                def split(h):
                    pool.wait_ge(S["raw_in"], 32 * h + 32)
                    apart(pool, spare_p)
                    twice = raw[:].unsqueeze(2).to_broadcast([P, 2, 2, DK])
                    pool.tensor_copy(hw[:, :, 0], twice).then_inc(S["w_cast"], 1)
                    pool.wait_ge(S["w_cast"], h + 1)
                    pool.tensor_tensor(hw[:, :, 1], twice, hw[:, :, 0].bitcast(F32), ALU.subtract
                                       ).then_inc(S["w_ready"], 1)

                def diagonals(u, first):
                    for q in range(QT):
                        n = u * QT + q
                        pool.wait_ge(S["exp_done"], n + 1)
                        if q % HALF == 0 and not (first and u == 0):
                            pool.wait_ge(S["red_done"], 2 * u + q // HALF - 1)
                        pool.tensor_tensor(ed[:, q // HALF, q % HALF, :], E[q % 2][:, q * P:(q + 1) * P], ident[:],
                                           ALU.mult).then_inc(S["dg_done"], 1)

                def head(h, first, last):
                    for b in range(PER):
                        if b == PER - 1 and not last:
                            pool.wait_ge(S["p_done"], 4 * (h * PER + PER))
                            split(h + 1)
                        diagonals(h * PER + b, first)

                split(0)
                head(0, True, False)
                with pool.Fori(1, H1 - 1) as h:
                    head(h, False, False)
                head(H1 - 1, False, True)

            @block.tensor
            def _(pe):
                def project(u, b, half, first):
                    at = bass.ds(b * SEQ + half * BLK, BLK)
                    for k, bk in enumerate((B_Q, B_K)):
                        if not (first and half == 0):
                            pe.wait_ge(S["q_lo"] if k == 0 else S["k_lo"], 2 * u + half)
                        wh, wl = (hw[:, k, s].rearrange("p u v -> p (u v)") for s in range(2))
                        pe.matmul(bank(bk), wh, xl[:, at], start=True, stop=False)
                        pe.matmul(bank(bk), wl, xh[:, at], start=False, stop=False)
                        pe.matmul(bank(bk), wh, xh[:, at], start=False, stop=True).then_inc(S["p_done"], 1)

                def logits(u, s, q, first):
                    n = u * QT + q
                    if not (first and FREED[q] <= 0):
                        pe.wait_ge(S["exp_done"], u * QT + FREED[q])
                        pe.wait_ge(S["mx_done"], u * QT + FREED[q])
                    dst, width = scores(q), (q + 1) * P
                    for a in range(0, width, BLK):
                        z = min(a + BLK, width)
                        pe.matmul(dst[:, a:z], Q2[s][:, q * P:(q + 1) * P], KL[s][:, a:z], start=True, stop=False)
                        last = pe.matmul(dst[:, a:z], Q2[s][:, q * P:(q + 1) * P], KH[s][:, a:z], start=False,
                                         stop=(z < width))
                    last = pe.matmul(dst[:, q * P:width], identb[:], cmask[:], start=False, stop=True)
                    last.then_inc(S["sc_done"], 1)

                def unit(u, b, first, last):
                    pe.wait_ge(S["q_lo"], 2 * u + 2)
                    pe.wait_ge(S["k_lo"], 2 * u + 2)
                    for q in range(QT):
                        logits(u, b % 2, q, first)
                        if q in (1, 4) and not last:
                            if b == PER - 1 and q == 1:
                                pe.wait_ge(S["w_ready"], u // PER + 2 if isinstance(u, int) else next_head + 1)
                            project(u + 1, (b + 1) % PER, 0 if q == 1 else 1, False)

                next_head = None
                pe.wait_ge(S["w_ready"], 1)
                project(0, 0, 0, True)
                project(0, 0, 1, False)
                for b in range(PER):
                    unit(b, b, b == 0, False)
                with pe.Fori(1, H1 - 1) as h:
                    next_head = h + 1
                    for b in range(PER):
                        unit(h * PER + b, b, False, False)
                for b in range(PER):
                    unit((H1 - 1) * PER + b, b, False, b == PER - 1)

            @block.scalar
            def _(act):
                def high(u, s, half, first):
                    to = slice(half * BLK, (half + 1) * BLK)
                    act.wait_ge(S["p_done"], 4 * u + 2 * half + 1)
                    if not first:
                        act.wait_ge(S["sc_done"], (u - 1) * QT)
                    act.activation(Q2[s][:, to], bank(B_Q), ACT.Copy, scale=LOGIT_SCALE).then_inc(S["q_hi"], 1)
                    act.wait_ge(S["p_done"], 4 * u + 2 * half + 2)
                    act.activation(KH[s][:, to], bank(B_K), ACT.Copy).then_inc(S["k_hi"], 1)

                def unit(u, b, first, last):
                    for q in range(QT):
                        n = u * QT + q
                        act.wait_ge(S["mx_done"], n + 1)
                        if not (first and q < 2):
                            act.wait_ge(S["dg_done"], n - 1)
                        width = (q + 1) * P
                        if q == 0 and not (first or (isinstance(u, int) and u < 2)):
                            act.wait_ge(S["rec_done"], 2 * u - 2)
                        act.activation(E[q % 2][:, 0:width], scores(q)[:, 0:width], ACT.Exp,
                                       bias=nmax[:, b % 2, q:q + 1],
                                       accum_out=esum[:, b % 2, q:q + 1]).then_inc(S["exp_done"], 1)
                        if q in (1, 4) and not last:
                            high(u + 1, (b + 1) % 2, 0 if q == 1 else 1, isinstance(u, int) and u == 0)

                high(0, 0, 0, True)
                high(0, 0, 1, True)
                for b in range(PER):
                    unit(b, b, b == 0, False)
                with act.Fori(1, H1 - 1) as h:
                    for b in range(PER):
                        unit(h * PER + b, b, False, False)
                for b in range(PER):
                    unit((H1 - 1) * PER + b, b, False, b == PER - 1)

            @block.vector
            def _(dve):
                def low(u, s, half):
                    to = slice(half * BLK, (half + 1) * BLK)
                    dve.wait_ge(S["q_hi"], 2 * u + half + 1)
                    dve.scalar_tensor_tensor(Q2[s][DK:P, to], bank(B_Q)[DK:P, :], LOGIT_SCALE,
                                             Q2[s][DK:P, to].bitcast(F32), ALU.mult, ALU.subtract).then_inc(S["q_lo"], 1)
                    dve.wait_ge(S["k_hi"], 2 * u + half + 1)
                    dve.tensor_tensor(KL[s][:, to], bank(B_K), KH[s][:, to].bitcast(F32), ALU.subtract
                                      ).then_inc(S["k_lo"], 1)

                def weights(u, h, b, half):
                    qs = slice(half * HALF, (half + 1) * HALF)
                    m = 2 * u + half
                    dve.wait_ge(S["dg_done"], u * QT + (half + 1) * HALF)
                    dve.tensor_reduce(dsum[:, half, :], ed[:, half], AX.X, ALU.add).then_inc(S["red_done"], 1)
                    dve.wait_ge(S["exp_done"], u * QT + (half + 1) * HALF)
                    dve.reciprocal(rsum[:, half, :], esum[:, b % 2, qs]).then_inc(S["rec_done"], 1)
                    dve.wait_ge(S["red_done"], m + 1)
                    dve.wait_ge(S["rec_done"], m + 1)
                    t0 = b * QT + half * HALF
                    col = h if isinstance(h, int) else None
                    dst = gate[:, t0:t0 + HALF, col:col + 1] if col is not None else gate[:, t0:t0 + HALF, bass.ds(h, 1)]
                    dve.tensor_tensor(dst.rearrange("p t a -> p (t a)"), dsum[:, half, :], rsum[:, half, :],
                                      ALU.mult).then_inc(S["p_set"], 1)

                def unit(u, h, b, first, last):
                    for q in range(QT):
                        n = u * QT + q
                        dve.wait_ge(S["sc_done"], n + 1)
                        if not (first or (isinstance(u, int) and u < 2)) and q == 0:
                            dve.wait_ge(S["exp_done"], (u - 1) * QT)
                        dve.tensor_reduce(nmax[:, b % 2, q:q + 1], scores(q)[:, 0:(q + 1) * P], AX.X, ALU.max,
                                          negate=True).then_inc(S["mx_done"], 1)
                        if q in (1, 4) and not last:
                            low(u + 1, (b + 1) % 2, 0 if q == 1 else 1)
                        if q == 2 and not first:
                            weights(u - 1, (h if b else h - 1), (b - 1) % PER, 1)
                        if q == 6:
                            weights(u, h, b, 0)

                low(0, 0, 0)
                low(0, 0, 1)
                for b in range(PER):
                    unit(b, 0, b, b == 0, False)
                with dve.Fori(1, H1 - 1) as h:
                    for b in range(PER):
                        unit(h * PER + b, h, b, False, False)
                for b in range(PER):
                    unit((H1 - 1) * PER + b, H1 - 1, b, False, b == PER - 1)
                weights(H1 * PER - 1, H1 - 1, PER - 1, 1)

    st16 = r[:, 0, NT * E1:NT * E1 + 3 * NT].rearrange("p (k t) -> p k t", k=3)
    m16 = r[:, 0, 0:NT * E1].bitcast(BF16).rearrange("p (t e) -> p t e", t=NT)
    p16 = gate[:].rearrange("p (k t) (a e) -> p k (t a) e", k=2, e=2 * E1)
    iota8 = sb("iota8", [P, E1], F32)
    nmax = sb("nmax", [P, 2, QT], F32)
    esum = sb("esum", [P, 2, QT], F32)
    dsum = sb("dsum", [P, 2, QT // 2], F32)
    rsum = sb("rsum", [P, 2, QT // 2], F32)

    ffn = dict(nf=NF0, up=(f_uph, f_upl), dn=(f_dnh, f_dnl), per_gate=1, func=ACT.Relu, bias=None, b2=None, scale=0.5)
    moe = dict(nf=NF1, up=(m_up[:, 0], m_up[:, 1]), dn=(m_dn[:, 0], m_dn[:, 1]), per_gate=F1 // P, func=ACT.Gelu,
               bias=b1c, b2=b2w, scale=0.5)
    setup()
    end_phase()
    route_ffn("r0", False)
    end_phase()
    gated("f0", final=False, **ffn)
    end_phase()
    linear_kv()
    end_phase()
    linear_q()
    end_phase()
    route_ffn("r1", True)
    end_phase()
    gated("f1", final=False, **ffn)
    end_phase()
    route_moe("r2", True)
    end_phase()
    turn_gates("g2", E1)
    end_phase()
    gated("m0", final=False, **moe)
    end_phase()
    softmax_diagonal()
    end_phase()
    turn_gates("g3", H1)
    end_phase()
    gated("a1o", nf=NF2, up=(v_h, v_l), dn=(o_h, o_l), per_gate=1, func=ACT.Identity, bias=None, b2=None, scale=1.0,
          final=False)
    end_phase()
    route_moe("r4", False)
    end_phase()
    turn_gates("g4", E1)
    end_phase()
    gated("m1", final=True, **moe)
    top.close()


_INS = ['L0_attn_x', 'L0_attn_Wq', 'L0_attn_bq', 'L0_attn_Wk', 'L0_attn_bk', 'L0_attn_Wv', 'L0_attn_bv', 'L0_attn_Wo',
        'L0_attn_bo', 'L0_attn_projection', 'L0_ffn_expert_sel', 'L0_ffn_keys', 'L0_ffn_values', 'L1_attn_P_q',
        'L1_attn_P_k', 'L1_attn_P_v', 'L1_attn_P_o', 'L1_ffn_Wg', 'L1_ffn_W1', 'L1_ffn_b1', 'L1_ffn_W2', 'L1_ffn_b2']
_OUTS = [((BATCH, SEQ, P), 'float32')]


def kernel(**inputs):
    import numpy as _np
    import concourse.bacc as _bacc
    from concourse import mybir as _mybir
    from concourse.bass_utils import run_bass_kernel_spmd as _run

    nc = _bacc.Bacc("TRN2", target_bir_lowering=False, num_devices=1)
    arrays, args = {}, {}
    for name in _INS:
        a = _np.ascontiguousarray(inputs[name])
        arrays[f"in_{name}_dram"] = a
        args[name] = nc.dram_tensor(f"in_{name}_dram", a.shape, _mybir.dt.from_np(a.dtype), kind="ExternalInput").ap()
    (shape, dtype), = _OUTS
    out = nc.dram_tensor("out_0_dram", shape, _mybir.dt.from_np(_np.dtype(dtype)), kind="ExternalOutput").ap()
    build(nc, args, out)
    r = _run(nc, [arrays], core_ids=[0])
    return r.results[0]["out_0_dram"]
```

```python
from contextlib import ExitStack

import concourse.bass as bass
from concourse import mybir

F32 = mybir.dt.float32
F32R = mybir.dt.float32r
BF16 = mybir.dt.bfloat16
I32 = mybir.dt.int32
U32 = mybir.dt.uint32
ALU = mybir.AluOpType
ACT = mybir.ActivationFunctionType
AX = mybir.AxisListType

P = 128
BATCH, SEQ = 4, 1024
T = BATCH * SEQ
NT = T // P
BT = 4
BLK = BT * P
NB = T // BLK
LN_EPS = 1e-5
E0, F0, TOP0 = 32, 64, 4
NF0 = E0 * F0 // P
H0, HD0, FEAT0 = 16, 8, 32
NCH = H0 * FEAT0 // P
HPC = P // FEAT0
KVW = HPC * HD0
YAT_EPS, NORM_EPS, DEN_MIN = 0.1, 1e-8, 1e-6
E1, F1 = 8, 512
NF1 = E1 * F1 // P
CAP = 2 * 2 * T // E1
GATE_EPS = 1e-9
H1, DK = 16, 64
NF2 = H1 * DK // P
QT = SEQ // P
LOGIT_SCALE = 8.0
MASKED = -1e38
LO_ROW = 32
LAG = 3
SLOTS = 4
PICK = E1 * P + (E0 - E1) * 64
MAGIC = 0x5F3759DF


def build(nc, I, out):
    top = ExitStack()

    def sb(name, shape, dt, stack=top):
        return stack.enter_context(nc.sbuf_tensor(name, shape, dt))

    held = []

    def sem(name):
        held.append(nc.alloc_semaphore(name))
        return held[-1]

    def end_phase():
        nc.clear_and_free_semaphores(list(held))
        nc.all_engine_barrier()
        held.clear()

    x = sb("x", [P, NT, P], F32)
    xh = sb("xh", [P, T], F32R)
    xl = sb("xl", [P, T], F32R)
    wreg = sb("wreg", [P, 4, 2048], F32R)
    r = sb("r", [P, 2, BLK], F32)
    hg = sb("hg", [P, 2, BLK], F32)
    raw_mem = ExitStack()
    raw_q, raw_k, raw_v, raw_o = (sb("raw_" + n, [P, H1 * DK], F32, raw_mem) for n in "qkvo")
    raw_mem.close()
    hh = sb("hh", [P, SLOTS, BLK], F32R)
    hl = sb("hl", [P, SLOTS, BLK], F32R)
    gT = sb("gT", [2 * LO_ROW, T], F32R)
    pick = sb("pick", [2 * LO_ROW, PICK], F32R)
    gate = sb("gate", [P, NT, 32], F32)
    ident = sb("ident", [P, P], F32)
    identb = sb("identb", [P, P], BF16)
    before = sb("before", [P, P], BF16)
    onesb = sb("onesb", [P, P], BF16)
    cmask = sb("cmask", [P, P], BF16)
    iota = sb("iota", [P, 32], F32)
    routers = sb("routers", [P, 2, P], F32R)
    selw, wgw = routers[:, :, 0:E0], routers[:, :, E0:E0 + E1]
    b1c = sb("b1c", [P, NF1], F32)
    b2w = sb("b2w", [2 * LO_ROW, 2, P], F32R)
    LN_TILES = 2 * BT
    st = sb("st", [P, LN_TILES, 6], F32)
    mv = sb("mv", [P, LN_TILES, 2], F32)
    var, rs, rt = (sb(n, [P, LN_TILES], F32) for n in ("var", "rs", "rt"))
    ed = sb("ed", [P, 2, BT, P], F32)
    xn = ed[:, 0]
    oT = ed[:, 1].rearrange("p t d -> p (t d)")
    hw = sb("hw", [P, 2, P], F32R)
    psum = top.enter_context(nc.psum_tensor("psum", [P, 8, BLK], F32))

    def bank(k):
        return psum[:, k, :]

    def tiles(k):
        return psum[:, k, :].rearrange("p (t d) -> p t d", t=BT)

    def blk(i, n=BLK):
        return bass.ds(i * n, n)

    x_in = I["L0_attn_x"].rearrange("b s d -> (b s) d").rearrange("(t p) d -> p t d", p=P)
    out_v = out.rearrange("b s d -> (b s) d").rearrange("(t p) d -> p t d", p=P)

    spare_v, spare_p = sb("spare_v", [P, 1], F32), sb("spare_p", [P, 1], F32)

    def apart(e, spare):
        e.tensor_tensor(spare[:], spare[:], spare[:], ALU.mult)

    LN_STEPS = 15

    def ln_step(e, i, k, step, xn_ready, nt=BT):
        xn = ed[:].rearrange("p k t d -> p (k t) d")
        v, y, z = var[:, 0:nt], rs[:, 0:nt], rt[:, 0:nt]
        if k > 0:
            e.wait_ge(step, (LN_STEPS - 1) * i + k)
        if k == 0:
            apart(e, spare_v)
            for t in range(nt):
                last = e.bn_stats(st[:, t, :], x[:, bass.ds(i * nt + t, 1), :].rearrange("p a d -> p (a d)"))
        elif k == 1:
            apart(e, spare_v)
            for t in range(nt):
                last = e.bn_aggr(mv[:, t, :], st[:, t, :])
        elif k == 2:
            last = e.tensor_scalar(v, mv[:, 0:nt, 1], LN_EPS, None, ALU.add)
        elif k == 3:
            last = e.tensor_scalar(z.bitcast(I32), v.bitcast(I32), 1, None, ALU.logical_shift_right)
        elif k == 4:
            last = e.tensor_scalar(y.bitcast(I32), z.bitcast(I32), -1.0, float(MAGIC), ALU.mult, ALU.add)
        elif k == LN_STEPS - 1:
            for t in range(nt):
                last = e.tensor_scalar(xn[:, t, :], x[:, bass.ds(i * nt + t, 1), :].rearrange("p a d -> p (a d)"),
                                       mv[:, t, 0:1], rs[:, t:t + 1], ALU.subtract, ALU.mult)
        elif k % 3 == 2:
            last = e.tensor_tensor(z, y, y, ALU.mult)
        elif k % 3 == 0:
            last = e.scalar_tensor_tensor(z, z, -0.5, v, ALU.mult, ALU.mult)
        else:
            last = e.scalar_tensor_tensor(y, z, 1.5, y, ALU.add, ALU.mult)
        last.then_inc(xn_ready if k == LN_STEPS - 1 else step, 1)

    scope = ExitStack()
    w0 = sb("w0", [P, 2, 3, P], F32R, scope)
    wo0 = sb("wo0", [P, P], F32, scope)
    bcol = sb("bcol", [P, 3], F32, scope)
    borow = sb("borow", [1, P], F32, scope)
    onerow = sb("onerow", [1, P], F32, scope)
    headones = sb("headones", [P, P], F32, scope)
    pbd = sb("pbd", [P, NCH * P], F32, scope)
    m32 = sb("m32", [P, KVW], F32, scope)
    m4 = sb("m4", [P, HPC], F32, scope)
    vones = sb("vones", [P, BT, NCH, KVW + 1], F32, scope)
    kvbd = sb("kvbd", [P, BATCH, NCH, KVW + HPC], F32, scope)
    setup_mem = ExitStack()
    rawU = sb("rawU", [P, E0, F0], F32, setup_mem)
    rawD = sb("rawD", [P, NF0, P], F32, setup_mem)
    rawS = sb("rawS", [E0, P], F32, setup_mem)
    rawG = sb("rawG", [P, E1], F32, setup_mem)
    rawB1 = sb("rawB1", [NF1, P], F32, setup_mem)
    rawB2 = sb("rawB2", [2 * LO_ROW, P], F32, setup_mem)
    rawA = sb("rawA", [P, 3, P], F32, setup_mem)
    rawP = sb("rawP", [P, NCH, HD0], F32, setup_mem)
    bigP = sb("bigP", [P, NCH, H0, HD0], F32, setup_mem)
    pick32 = sb("pick32", [2 * LO_ROW, PICK], F32, setup_mem)
    setup_mem.close()
    aT = sb("aT", [P, BLK], F32, scope)
    vT = sb("vT", [P, BLK], F32, scope)
    sq = sb("sq", [P, BLK], F32, scope)
    root = sb("root", [P, BT * H0], F32, scope)
    nrm = sb("nrm", [P, BLK], F32, scope)
    an = sb("an", [P, BLK], F32, scope)
    feat = sb("feat", [P, NCH, BLK], F32, scope)
    den = sb("den", [P, BT, H0], F32, scope)
    o0 = sb("o0", [P, BT, P], F32, scope)
    o0T = sb("o0T", [P, BLK], F32, scope)
    scope.close()
    m_up = sb("m_up", [P, 2, NF1 * P], F32R)
    m_dn = sb("m_dn", [P, 2, NF1 * P], F32R)

    f_uph, f_upl = wreg[:, 0, :], wreg[:, 1, :]
    f_dnh, f_dnl = wreg[:, 2, :], wreg[:, 3, :]
    NV = H1 * DK
    f_h, f_l = (wreg[:, k, :].rearrange("p (h d) -> p h d", h=H1) for k in (2, 3))
    qkT = ed[0:DK, 0].rearrange("p t d -> p (t d)").rearrange("p (k d) -> p k d", k=4)
    form = [ed[:, 1, 2 * k:2 * k + 2, :].rearrange("p t d -> p (t d)") for k in range(2)]
    v_h, v_l, o_h, o_l = (wreg[:, k // 2, (k % 2) * NV:(k % 2 + 1) * NV] for k in range(4))

    def setup():
        x_load0, x_load1, w_load = sem("x_load0"), sem("x_load1"), sem("w_load")
        consts, fixed, cast = sem("consts"), sem("fixed"), sem("cast")
        tr_done, tr_out, a_hi = sem("tr_done"), sem("tr_out"), sem("a_hi")
        step, xn_ready, xT_done, xh_done, xl_done = (sem("s_" + s) for s in (
            "step", "xn_ready", "xT_done", "xh_done", "xl_done"))
        zeroed, b2_zero = sem("zeroed"), sem("b2_zero")
        NLOAD = 17
        weights = ((f_uph, f_upl, rawU[:].rearrange("p e f -> p (e f)")), (f_dnh, f_dnl, rawD[:].rearrange("p j d -> p (j d)")),
                   (w0[:, 0], w0[:, 1], rawA[:]), (b2w[:, 0], b2w[:, 1], rawB2[:]))
        xn8 = ed[:].rearrange("p k t d -> p (k t) d")
        HALVES = LN_TILES // BT
        GROUPS = NT // LN_TILES

        with nc.Block() as block:
            @block.sync
            def _(sp):
                sp.dma_start(x[:, 0:LN_TILES, :], x_in[:, 0:LN_TILES, :]).then_inc(x_load0, 16)
                sp.dma_start(x[:, LN_TILES:, :], x_in[:, LN_TILES:, :]).then_inc(x_load1, 16)
                sp.dma_start(rawS[:], I["L0_ffn_expert_sel"]).then_inc(w_load, 16)
                sp.dma_start(rawU[:], I["L0_ffn_keys"].rearrange("e d f -> d e f")).then_inc(w_load, 16)
                sp.dma_start(rawD[:], I["L0_ffn_values"].rearrange("(j e) f d -> (e f) j d", e=2)).then_inc(w_load, 16)
                sp.dma_start(rawG[:], I["L1_ffn_Wg"]).then_inc(w_load, 16)
                sp.dma_start(rawB1[:], I["L1_ffn_b1"].rearrange("e (q p) -> (e q) p", p=P)).then_inc(w_load, 16)
                sp.wait_ge(b2_zero, 1)
                for k in range(2):
                    sp.dma_start(rawB2[LO_ROW * k:LO_ROW * k + E1, :], I["L1_ffn_b2"]).then_inc(w_load, 16)
                sp.dma_start(rawP[:], I["L0_attn_projection"].rearrange("(c h) f d -> (h f) c d", c=NCH)).then_inc(w_load, 16)
                for k, n in enumerate("qkv"):
                    sp.dma_start(rawA[:, k, :], I["L0_attn_W" + n]).then_inc(w_load, 16)
                    sp.dma_start(bcol[:, k:k + 1], I["L0_attn_b" + n].rearrange("(p a) -> p a", a=1)).then_inc(w_load, 16)
                sp.dma_start(wo0[:], I["L0_attn_Wo"]).then_inc(w_load, 16)
                sp.dma_start(borow[:], I["L0_attn_bo"].rearrange("(a p) -> a p", a=1)).then_inc(w_load, 16)
                sp.dma_start(gate[:, 0, 0:1], I["L0_attn_bo"].rearrange("(p a) -> p a", a=1)).then_inc(w_load, 16)

            @block.gpsimd
            def _(pool):
                pool.memset(rawB2[:], 0.0).then_inc(b2_zero, 1)
                n = 0

                def then(ins):
                    nonlocal n
                    n += 1
                    ins.then_inc(fixed, 1)
                    pool.wait_ge(fixed, n)

                def select(m, pattern, base, cm, op, fill):
                    then(pool.affine_select(out=m, in_=m, compare_op=op, fill=fill, base=base,
                                            pattern=pattern, channel_multiplier=cm))

                then(pool.memset(ident[:], 0.0))
                select(ident[:], [[-1, P]], 0, 1, ALU.not_equal, 1.0)
                pool.tensor_copy(identb[:], ident[:]).then_inc(consts, 1)
                then(pool.memset(before[:], 1.0))
                select(before[:], [[1, P]], 0, -1, ALU.is_gt, 0.0)
                pool.memset(onesb[:], 1.0).then_inc(consts, 1)
                then(pool.memset(cmask[:], 0.0))
                select(cmask[:], [[-1, P]], 0, 1, ALU.is_ge, MASKED)
                pool.iota(iota[:], [[1, 32]], base=0, channel_multiplier=0,
                          allow_small_or_imprecise_dtypes=True).then_inc(consts, 1)
                pool.iota(iota8[:], [[1, E1]], base=-E1, channel_multiplier=0,
                          allow_small_or_imprecise_dtypes=True)
                pool.memset(onerow[:], 1.0).then_inc(consts, 1)
                then(pool.memset(headones[:], 1.0))
                v = headones[:].rearrange("p (g d) -> p g d", d=HD0)
                select(v, [[-HD0, H0], [0, HD0]], 0, 1, ALU.is_ge, 0.0)
                select(v, [[HD0, H0], [0, HD0]], HD0 - 1, -1, ALU.is_ge, 0.0)
                then(pool.memset(m32[:], 1.0))
                v = m32[:].rearrange("p (g d) -> p g d", d=HD0)
                select(v, [[-FEAT0, HPC], [0, HD0]], 0, 1, ALU.is_ge, 0.0)
                select(v, [[FEAT0, HPC], [0, HD0]], FEAT0 - 1, -1, ALU.is_ge, 0.0)
                then(pool.memset(m4[:], 1.0))
                select(m4[:], [[-FEAT0, HPC]], 0, 1, ALU.is_ge, 0.0)
                select(m4[:], [[FEAT0, HPC]], FEAT0 - 1, -1, ALU.is_ge, 0.0)
                then(pool.memset(pick32[:], 0.0))
                for base in (0, -LO_ROW):
                    select(pick32[:, 0:E1 * P], [[-1, E1], [0, P]], base, 1, ALU.not_equal, 1.0)
                    select(pick32[:, E1 * P:], [[-1, E0 - E1], [0, 64]], base - E1, 1, ALU.not_equal, 1.0)
                pool.tensor_copy(iota[0:1, 0:1], iota[0:1, 0:1]).then_inc(consts, 1)
                pool.memset(gT[:].bitcast(F32), 0.0)
                pool.memset(spare_p[:], 0.0)
                pool.memset(vones[:], 1.0).then_inc(consts, 1)
                pool.wait_ge(w_load, 16 * NLOAD)
                for c in range(NCH):
                    then(pool.tensor_copy(bigP[:, c], rawP[:, c:c + 1, :].to_broadcast([P, H0, HD0])))
                    select(bigP[:, c], [[-FEAT0, H0], [0, HD0]], FEAT0 * HPC * c, 1, ALU.is_ge, 0.0)
                    select(bigP[:, c], [[FEAT0, H0], [0, HD0]], FEAT0 - 1 - FEAT0 * HPC * c, -1, ALU.is_ge, 0.0)
                pool.tensor_copy(iota[0:1, 0:1], iota[0:1, 0:1]).then_inc(consts, 1)
                for k, (hi, lo, w) in enumerate(weights):
                    pool.wait_ge(cast, k + 1)
                    pool.tensor_tensor(lo, w, hi.bitcast(F32), ALU.subtract)

            @block.tensor
            def _(pe):
                def turn(g, first):
                    pe.wait_ge(xn_ready, g + 1)
                    for k in range(HALVES):
                        if not first:
                            pe.wait_ge(xl_done, HALVES * g - HALVES + k + 1)
                        for t in range(BT):
                            last = pe.transpose(tiles(k)[:, t, :], xn8[:, k * BT + t, :], ident[:])
                        last.then_inc(xT_done, 1)

                pe.wait_ge(consts, 1)
                turn(0, True)
                with pe.Fori(1, GROUPS) as g:
                    turn(g, False)
                pe.wait_ge(w_load, 16 * NLOAD)
                pe.wait_ge(consts, 7)
                pe.transpose(bank(2)[:, 0:E0], rawS[:], ident[0:E0, 0:E0]).then_inc(tr_done, 1)
                pe.transpose(bank(3)[:, 0:NF1], rawB1[:], ident[0:NF1, 0:NF1]).then_inc(tr_done, 1)
                for c in range(NCH):
                    last = pe.transpose(tiles(4)[:, c, :], bigP[:, c].rearrange("p h d -> p (h d)"), ident[:])
                last.then_inc(tr_done, 1)

            @block.scalar
            def _(act):
                def high(g):
                    for k in range(HALVES):
                        act.wait_ge(xT_done, HALVES * g + k + 1)
                        act.activation(xh[:, blk(HALVES * g + k)], bank(k), ACT.Copy).then_inc(xh_done, 1)

                high(0)
                act.wait_ge(consts, 5)
                act.activation(pick[:], pick32[:], ACT.Copy)
                act.wait_ge(w_load, 16 * NLOAD)
                for hi, lo, w in weights:
                    act.activation(hi, w, ACT.Copy).then_inc(cast, 1)
                with act.Fori(1, GROUPS) as g:
                    high(g)
                act.wait_ge(tr_done, 3)
                act.wait_ge(xl_done, 1)
                act.activation(selw[:, 0], bank(2)[:, 0:E0], ACT.Copy).then_inc(a_hi, 1)
                act.activation(wgw[:, 0], rawG[:], ACT.Copy).then_inc(a_hi, 1)
                act.activation(b1c[:], bank(3)[:, 0:NF1], ACT.Copy).then_inc(tr_out, 1)
                act.activation(pbd[:], bank(4), ACT.Copy).then_inc(tr_out, 1)

            @block.vector
            def _(dve):
                def low(g):
                    for k in range(HALVES):
                        dve.wait_ge(xh_done, HALVES * g + k + 1)
                        dve.tensor_tensor(xl[:, blk(HALVES * g + k)], bank(k), xh[:, blk(HALVES * g + k)].bitcast(F32),
                                          ALU.subtract).then_inc(xl_done, 1)

                def normalise(g, first):
                    for k in range(LN_STEPS):
                        if k == 3 and not first:
                            low(g - 1)
                        ln_step(dve, g, k, step, xn_ready, LN_TILES)

                dve.memset(routers[:].bitcast(F32), 0.0)
                dve.memset(spare_v[:], 0.0)
                dve.memset(kvbd[:], 0.0).then_inc(zeroed, 1)
                dve.wait_ge(zeroed, 1)
                dve.wait_ge(x_load0, 16)
                normalise(0, True)
                dve.wait_ge(x_load1, 16)
                with dve.Fori(1, GROUPS) as g:
                    normalise(g, False)
                low(GROUPS - 1)
                dve.wait_ge(a_hi, 2)
                dve.tensor_tensor(selw[:, 1], bank(2)[:, 0:E0], selw[:, 0].bitcast(F32), ALU.subtract)
                dve.tensor_tensor(wgw[:, 1], rawG[:], wgw[:, 0].bitcast(F32), ALU.subtract)

    top8 = sb("top8", [P, BT, 8], F32)
    GW = E0 + 8 - TOP0
    FILL = -1.0

    def product3(pe, dst, wh, wl, i, start=True, stop=True):
        pe.matmul(dst, wh, xl[:, blk(i)], start=start, stop=False)
        pe.matmul(dst, wl, xh[:, blk(i)], start=False, stop=False)
        return pe.matmul(dst, wh, xh[:, blk(i)], start=False, stop=stop)

    def token_logits(pe, dst, w, ts):
        n = w.shape[2]
        for k, t in enumerate(ts):
            at, to = slice(t * P, (t + 1) * P), dst[:, k * n:(k + 1) * n]
            pe.matmul(to, xl[:, at], w[:, 0], start=True, stop=False)
            pe.matmul(to, xh[:, at], w[:, 1], start=False, stop=False)
            last = pe.matmul(to, xh[:, at], w[:, 0], start=False, stop=True)
        return last

    def route_ffn(ph, load_moe):
        names = ("filled", "logit_done", "gate_in", "max_done", "top_set", "rest_set", "gate_set", "gT_ps", "gT_hi", "gT_lo")
        S = {n: sem(f"{ph}_{n}") for n in names}
        gtok, gsel = ([r[:, a, k:k + BT * w].rearrange("p (t e) -> p t e", t=BT) for a in range(2)]
                      for k, w in ((0, GW), (BLK // 2, E0)))
        rest = [hg[:, a, 0:BT * GW].rearrange("p (t e) -> p t e", t=BT) for a in range(2)]
        B_L, B_G = (0, 1), (2, 3)
        raw_w = [[w[:, k * BLK:(k + 1) * BLK] for k in range(2)] for w in (raw_q, raw_k)]
        if load_moe:
            m_load, m_cast, m_split = (sem("m_load0"), sem("m_load1")), sem("m_cast"), sem("m_split")

        def pairs(e, step):
            step(0, 0, 0)
            step(1, 1, 0)
            with e.Fori(1, NB // 2) as g:
                for a in range(2):
                    step(2 * g + a, a, g)
            step(NB, 0, NB // 2)

        with nc.Block() as block:
            @block.tensor
            def _(pe):
                for i in range(NB + 1):
                    if i < NB:
                        if i >= 2:
                            pe.wait_ge(S["gate_in"], i - 1)
                        last = token_logits(pe, bank(B_L[i % 2]), selw, range(i * BT, (i + 1) * BT))
                        last.then_inc(S["logit_done"], 1)
                    if i >= 1:
                        pe.wait_ge(S["gate_set"], i)
                        if i >= 3:
                            pe.wait_ge(S["gT_lo"], i - 2)
                        for t in range(BT):
                            last = pe.transpose(bank(B_G[(i - 1) % 2])[0:E0, t * P:(t + 1) * P], gsel[(i - 1) % 2][:, t, :],
                                                ident[:])
                        last.then_inc(S["gT_ps"], 1)

            @block.scalar
            def _(act):
                def step(i, a, turn):
                    early = isinstance(turn, int) and turn == 0
                    if not (isinstance(i, int) and i == NB):
                        act.wait_ge(S["logit_done"], i + 1)
                        if not early:
                            act.wait_ge(S["gate_set"], i - 1)
                        act.activation(gtok[a][:, :, 0:E0], bank(B_L[a])[:, 0:BT * E0].rearrange("p (t e) -> p t e", t=BT),
                                       ACT.Sigmoid).then_inc(S["gate_in"], 1)
                    if not (early and i == 0):
                        act.wait_ge(S["gT_ps"], i)
                        act.activation(gT[0:E0, blk(i - 1)], bank(B_G[1 - a])[0:E0, :], ACT.Copy).then_inc(S["gT_hi"], 1)
                    if load_moe and not (isinstance(i, int) and i == NB):
                        act.wait_ge(m_load[a], 32 * (turn + 1))
                        for w, raw_one in zip((m_up, m_dn), raw_w[a]):
                            last = act.activation(w[:, 0, blk(i)], raw_one, ACT.Copy)
                        last.then_inc(m_cast, 1)

                act.wait_ge(S["filled"], 1)
                pairs(act, step)

            @block.vector
            def _(dve):
                def step(i, a, turn):
                    early = isinstance(turn, int) and turn == 0
                    if not (isinstance(i, int) and i == NB):
                        dve.wait_ge(S["gate_in"], i + 1)
                        apart(dve, spare_v)
                        for t in range(BT):
                            last = dve.max(top8[:, t, :], gtok[a][:, t, 0:E0])
                        last.then_inc(S["max_done"], 1)
                        dve.wait_ge(S["max_done"], i + 1)
                        dve.memset(top8[:, :, TOP0:], FILL).then_inc(S["top_set"], 1)
                        if not (early and i == 0):
                            low(i - 1, 1 - a)
                        dve.wait_ge(S["top_set"], i + 1)
                        apart(dve, spare_v)
                        for t in range(BT):
                            last = dve.match_replace(rest[a][:, t, :], top8[:, t, :], gtok[a][:, t, :], 0.0)
                        last.then_inc(S["rest_set"], 1)
                        dve.wait_ge(S["rest_set"], i + 1)
                        if not early:
                            dve.wait_ge(S["gT_ps"], i - 1)
                        dve.tensor_tensor(gsel[a], gtok[a][:, :, 0:E0], rest[a][:, :, 0:E0], ALU.subtract
                                          ).then_inc(S["gate_set"], 1)
                        dve.wait_ge(S["gate_set"], i + 1)
                    else:
                        low(i - 1, 1 - a)

                def low(i, a):
                    dve.wait_ge(S["gT_hi"], i + 1)
                    dve.tensor_tensor(gT[LO_ROW:LO_ROW + E0, blk(i)], bank(B_G[a])[0:E0, :],
                                      gT[0:E0, blk(i)].bitcast(F32), ALU.subtract).then_inc(S["gT_lo"], 1)

                for a in range(2):
                    last = dve.memset(gtok[a][:, :, E0:], FILL)
                last.then_inc(S["filled"], 1)
                pairs(dve, step)

            if load_moe:
                W1 = I["L1_ffn_W1"].rearrange("e d f -> d e f")
                W2 = I["L1_ffn_W2"].rearrange("e (q p) d -> p (e q) d", p=P)

                @block.sync
                def _(sp):
                    def load(e, a):
                        sp.dma_start(raw_w[a][0], W1[:, bass.ds(e, 1), :].rearrange("d a f -> d (a f)")).then_inc(m_load[a], 16)
                        sp.dma_start(raw_w[a][1].rearrange("p (q d) -> p q d", q=BT), W2[:, blk(e, BT), :]
                                     ).then_inc(m_load[a], 16)

                    load(0, 0)
                    load(1, 1)
                    with sp.Fori(1, E1 // 2) as g:
                        for a in range(2):
                            sp.wait_ge(m_split, 2 * g + a - 1)
                            load(2 * g + a, a)

                @block.gpsimd
                def _(pool):
                    with pool.Fori(0, E1 // 2) as g:
                        for a in range(2):
                            e = 2 * g + a
                            pool.wait_ge(m_cast, e + 1)
                            for w, raw_one in zip((m_up, m_dn), raw_w[a]):
                                last = pool.tensor_tensor(w[:, 1, blk(e)], raw_one, w[:, 0, blk(e)].bitcast(F32),
                                                          ALU.subtract)
                            last.then_inc(m_split, 1)

    def gated(ph, nf, up, dn, per_gate, func, bias, b2, scale, final):
        names = ("up_done", "g_done", "act_done", "hg_done", "hi_done", "lo_done", "dn_done", "oT_ready",
                 "back_done", "added", "xn_ready", "xT_done", "xh_done", "xl_done", "step", "stored")
        S = {n: sem(f"{ph}_{n}") for n in names}
        B_UP, B_G, B_OUT, B_BACK, B_XT = (0, 1), (2, 3), (4, 7), 5, 6
        AT_EVAC, AT_BACK, AT_ADD = nf + LAG, nf + LAG + 3, nf + LAG + 4
        AT_LN = AT_ADD + 1
        AT_XT = AT_LN + (LN_STEPS + 1) // 2 + 1
        AT_HIGH, AT_LOW = AT_XT + 1, AT_XT + 2
        PEEL = 1 + (AT_ADD if final else AT_LOW) // nf

        def tail_blocks(i, at, j, place):
            back_by = place // nf
            past = isinstance(i, int) and i - back_by >= NB
            return [(i - back_by, at == back_by)] if j == place % nf and at >= back_by and not past else []

        def all_blocks(e, one_block):
            for i in range(PEEL):
                one_block(i, i, i % 2)
            with e.Fori(0, (NB - PEEL) // 2) as g:
                for a in range(2):
                    one_block(2 * g + PEEL + a, PEEL, (PEEL + a) % 2)
            for i in range(NB - (NB - PEEL) % 2, NB + PEEL):
                one_block(i, PEEL, i % 2, i < NB)

        def col(w, j):
            return w[:, j * P:(j + 1) * P]

        def picker(j):
            if per_gate > 1:
                at = j // per_gate * P
            else:
                at = 2 * j * P + 64 if 2 * j < E1 else E1 * P + (2 * j - E1) * 64
            return pick[:, at:at + P]

        with nc.Block() as block:
            @block.tensor
            def _(pe):
                def up_product(i, j, first):
                    n = i * nf + j
                    if not first or j >= 2:
                        pe.wait_ge(S["act_done"], n - 1)
                    q = j // per_gate
                    if j % per_gate == 0 and (not first or q >= 2):
                        pe.wait_ge(S["hg_done"], n - per_gate)
                    product3(pe, bank(B_UP[j % 2]), col(up[0], j), col(up[1], j), i).then_inc(S["up_done"], 1)
                    if j % per_gate == 0:
                        pe.matmul(bank(B_G[q % 2]), picker(j), gT[:, blk(i)], start=True,
                                  stop=True).then_inc(S["g_done"], 1)

                def down_product(i, j, at, odd):
                    n = i * nf + j
                    s = j % SLOTS
                    dst = bank(B_OUT[odd])
                    if j == 0 and at >= 2:
                        pe.wait_ge(S["oT_ready"], i - 1)
                    pe.wait_ge(S["lo_done"], n + 1)
                    pe.matmul(dst, col(dn[1], j), hh[:, s, :], start=(j == 0), stop=False)
                    pe.matmul(dst, col(dn[0], j), hl[:, s, :], start=False, stop=False)
                    last = pe.matmul(dst, col(dn[0], j), hh[:, s, :], start=False,
                                     stop=(j == nf - 1 and b2 is None))
                    if j == nf - 1 and b2 is not None:
                        pe.matmul(dst, b2[:, 1], gT[:, blk(i)], start=False, stop=False)
                        last = pe.matmul(dst, b2[:, 0], gT[:, blk(i)], start=False, stop=True)
                    last.then_inc(S["dn_done"], 1)

                def back(i, first):
                    pe.wait_ge(S["oT_ready"], i + 1)
                    if not first:
                        pe.wait_ge(S["added"], i)
                    for t in range(BT):
                        last = pe.transpose(tiles(B_BACK)[:, t, :], oT[:, t * P:(t + 1) * P], ident[:])
                    last.then_inc(S["back_done"], 1)

                def next_xT(i, first):
                    if final:
                        return
                    pe.wait_ge(S["xn_ready"], i + 1)
                    if not first:
                        pe.wait_ge(S["xl_done"], i)
                    for t in range(BT):
                        last = pe.transpose(tiles(B_XT)[:, t, :], xn[:, t, :], ident[:])
                    last.then_inc(S["xT_done"], 1)

                def one_block(i, at, odd, live=True):
                    for j in range(nf):
                        if live:
                            up_product(i, j, at == 0)
                        if j < LAG and at >= 1 and (live or i == NB):
                            down_product(i - 1, j - LAG + nf, at - 1, 1 - odd)
                        if j >= LAG and live:
                            down_product(i, j - LAG, at, odd)
                        for k, first in tail_blocks(i, at, j, AT_BACK):
                            back(k, first)
                        for k, first in tail_blocks(i, at, j, AT_XT):
                            next_xT(k, first)

                all_blocks(pe, one_block)

            @block.scalar
            def _(act):
                def activate(i, j, first):
                    n = i * nf + j
                    act.wait_ge(S["up_done"], n + 1)
                    if not first or j >= 2:
                        act.wait_ge(S["hg_done"], n - 1)
                    act.activation(r[:, j % 2, :], bank(B_UP[j % 2]), func,
                                   **({} if bias is None else {"bias": bias[:, j:j + 1]})).then_inc(S["act_done"], 1)

                def high(i, j, first):
                    n = i * nf + j
                    act.wait_ge(S["hg_done"], n + 1)
                    if not first or j >= SLOTS:
                        act.wait_ge(S["dn_done"], n - SLOTS + 1)
                    act.activation(hh[:, j % SLOTS, :], hg[:, j % 2, :], ACT.Copy).then_inc(S["hi_done"], 1)

                def evacuate(i, odd, first):
                    act.wait_ge(S["dn_done"], nf * i + nf)
                    if not first:
                        act.wait_ge(S["back_done"], i)
                    act.activation(oT, bank(B_OUT[odd]), ACT.Copy, scale=scale).then_inc(S["oT_ready"], 1)

                def next_high(i):
                    if not final:
                        act.wait_ge(S["xT_done"], i + 1)
                        act.activation(xh[:, blk(i)], bank(B_XT), ACT.Copy).then_inc(S["xh_done"], 1)

                def one_block(i, at, odd, live=True):
                    for j in range(nf):
                        if live:
                            activate(i, j, at == 0)
                        if j == 0 and at >= 1 and (live or i == NB):
                            high(i - 1, nf - 1, at == 1)
                        if j >= 1 and live:
                            high(i, j - 1, at == 0)
                        for k, first in tail_blocks(i, at, j, AT_EVAC):
                            evacuate(k, 1 - odd, first)
                        for k, first in tail_blocks(i, at, j, AT_HIGH):
                            next_high(k)

                all_blocks(act, one_block)

            @block.vector
            def _(dve):
                def apply_gate(i, j, first):
                    n = i * nf + j
                    dve.wait_ge(S["act_done"], n + 1)
                    dve.wait_ge(S["g_done"], n // per_gate + 1 if first and isinstance(n, int)
                                else i * (nf // per_gate) + j // per_gate + 1)
                    if not first or j >= 2:
                        dve.wait_ge(S["lo_done"], n - 1)
                    dve.tensor_tensor(hg[:, j % 2, :], r[:, j % 2, :], bank(B_G[(j // per_gate) % 2]),
                                      ALU.mult).then_inc(S["hg_done"], 1)

                def add_residual(i, first):
                    dve.wait_ge(S["back_done"], i + 1)
                    xb = x[:, blk(i, BT), :]
                    dve.tensor_tensor(xb, xb, tiles(B_BACK), ALU.add).then_inc(S["added"], 1)

                def normalise(i, k, first):
                    if final:
                        return
                    if k == 0:
                        dve.wait_ge(S["added"], i + 1)
                    if k == LN_STEPS - 1 and not first:
                        dve.wait_ge(S["xT_done"], i)
                    ln_step(dve, i, k, S["step"], S["xn_ready"])

                def next_low(i):
                    if not final:
                        dve.wait_ge(S["xh_done"], i + 1)
                        dve.tensor_tensor(xl[:, blk(i)], bank(B_XT), xh[:, blk(i)].bitcast(F32),
                                          ALU.subtract).then_inc(S["xl_done"], 1)

                def one_block(i, at, odd, live=True):
                    for j in range(nf):
                        if live:
                            apply_gate(i, j, at == 0)
                        for k, first in tail_blocks(i, at, j, AT_ADD):
                            add_residual(k, first)
                        for n in range(LN_STEPS):
                            for k, first in tail_blocks(i, at, j, AT_LN + n // 2):
                                normalise(k, n, first)
                        for k, first in tail_blocks(i, at, j, AT_LOW):
                            next_low(k)

                all_blocks(dve, one_block)

            @block.gpsimd
            def _(pool):
                def low(i, j, first):
                    n = i * nf + j
                    pool.wait_ge(S["hi_done"], n + 1)
                    if not first or j >= SLOTS:
                        pool.wait_ge(S["dn_done"], n - SLOTS + 1)
                    pool.tensor_tensor(hl[:, j % SLOTS, :], hg[:, j % 2, :], hh[:, j % SLOTS, :].bitcast(F32),
                                       ALU.subtract).then_inc(S["lo_done"], 1)

                def one_block(i, at, odd, live=True):
                    for j in range(nf if live else 0):
                        low(i, j, at == 0)

                all_blocks(pool, one_block)

            if final:
                @block.sync
                def _(sp):
                    for i in range(NB):
                        sp.wait_ge(S["added"], i + 1)
                        sp.dma_start(out_v[:, blk(i, BT), :], x[:, blk(i, BT), :]).then_inc(S["stored"], 16)
                    sp.wait_ge(S["stored"], 16 * NB)

    UNROLL = SEQ // BLK

    def square_sums(pe, dst):
        one_per_head = headones[:].rearrange("p (h d) -> p h d", d=HD0)[:, :, 0]
        for t in range(BT):
            last = pe.matmul(dst[:, t * H0:(t + 1) * H0], sq[:, t * P:(t + 1) * P], one_per_head, start=True, stop=True)
        return last

    def expand(act):
        return act.activation(nrm[:].rearrange("p (g d) -> p g d", d=HD0),
                              root[:].unsqueeze(2).to_broadcast([P, BT * H0, HD0]), ACT.Copy)

    def linear_kv():
        names = ("k_done", "v_done", "sq_ready", "vT_ready", "n_done", "root", "eps", "inv", "wide", "w_done",
                 "an_ready", "vt_done", "v_ready", "f_done", "f_ready", "kv_done", "kv_read")
        S = {n: sem(f"a0_{n}") for n in names}
        B_K, B_V, B_N, B_VT, B_F, B_KV, B_W = 0, 1, 2, 3, (4, 5), 6, 7
        kv = bank(B_KV)[:, 0:NCH * (KVW + 1)].rearrange("p (c w) -> p c w", c=NCH)

        def pipeline(e, step):
            for i in range(UNROLL):
                step(i, i - 1)
            with e.Fori(1, BATCH) as b:
                for u in range(UNROLL):
                    step(b * UNROLL + u, u - 1, b)
            step(NB, UNROLL - 1)

        with nc.Block() as block:
            @block.tensor
            def _(pe):
                def keys_values(i, first):
                    if not first:
                        pe.wait_ge(S["sq_ready"], i)
                    product3(pe, bank(B_K), w0[:, 0, 1], w0[:, 1, 1], i).then_inc(S["k_done"], 1)
                    if not first:
                        pe.wait_ge(S["vT_ready"], i)
                    product3(pe, bank(B_V), w0[:, 0, 2], w0[:, 1, 2], i).then_inc(S["v_done"], 1)

                def norms(i, first):
                    pe.wait_ge(S["sq_ready"], i + 1)
                    if not first:
                        pe.wait_ge(S["root"], i)
                    square_sums(pe, bank(B_N)).then_inc(S["n_done"], 1)

                def widen(i, first):
                    pe.wait_ge(S["wide"], i + 1)
                    if not first:
                        pe.wait_ge(S["an_ready"], i)
                    for t in range(BT):
                        last = pe.transpose(tiles(B_W)[:, t, :], nrm[:, t * P:(t + 1) * P], ident[:])
                    last.then_inc(S["w_done"], 1)

                def turn_values(i, first):
                    pe.wait_ge(S["vT_ready"], i + 1)
                    if not first:
                        pe.wait_ge(S["v_ready"], i)
                    for t in range(BT):
                        last = pe.transpose(tiles(B_VT)[:, t, :], vT[:, t * P:(t + 1) * P], ident[:])
                    last.then_inc(S["vt_done"], 1)

                def features(i, ts, first):
                    pe.wait_ge(S["an_ready"], i + 1)
                    for t in ts:
                        if t >= 2 or not first:
                            pe.wait_ge(S["f_ready"], i * BT + t - 1)
                        pe.matmul(bank(B_F[t % 2]), an[:, t * P:(t + 1) * P], pbd[:], start=True,
                                  stop=True).then_inc(S["f_done"], 1)

                def sums(i, u, b):
                    if u == 0 and b is not None:
                        pe.wait_ge(S["kv_read"], b)
                    pe.wait_ge(S["v_ready"], i + 1)
                    for t in range(BT):
                        pe.wait_ge(S["f_ready"], i * BT + t + 1)
                        for c in range(NCH):
                            last = pe.matmul(kv[:, c, :], feat[:, t, c * P:(c + 1) * P], vones[:, t, c, :],
                                             start=(u == 0 and t == 0 and c == 0),
                                             stop=(u == UNROLL - 1 and t == BT - 1), skip_group_check=True)
                    last.then_inc(S["kv_done"], 1)

                def step(i, u_before, b=None):
                    first, live = b is None and i == 0, b is not None or i < NB
                    if live:
                        keys_values(i, first)
                    if not first:
                        features(i - 1, (0, 1), b is None and i == 1)
                    if live:
                        norms(i, first)
                    if not first:
                        features(i - 1, (2, 3), b is None and i == 1)
                    if live:
                        turn_values(i, first)
                        widen(i, first)
                    if not first:
                        sums(i - 1, u_before % UNROLL, b)

                pipeline(pe, step)

            @block.scalar
            def _(act):
                def step(i, u_before, b=None):
                    first, live = b is None and i == 0, b is not None or i < NB
                    if not live:
                        return
                    act.wait_ge(S["k_done"], i + 1)
                    if not first:
                        act.wait_ge(S["an_ready"], i)
                    act.activation(aT[:], bank(B_K), ACT.Identity, bias=bcol[:, 1:2])
                    act.activation(sq[:], bank(B_K), ACT.Square, bias=bcol[:, 1:2]).then_inc(S["sq_ready"], 1)
                    act.wait_ge(S["v_done"], i + 1)
                    if not first:
                        act.wait_ge(S["vt_done"], i)
                    act.activation(vT[:], bank(B_V), ACT.Identity, bias=bcol[:, 2:3]).then_inc(S["vT_ready"], 1)
                    act.wait_ge(S["n_done"], i + 1)
                    act.activation(root[:], bank(B_N)[:, 0:BT * H0], ACT.Sqrt).then_inc(S["root"], 1)
                    act.wait_ge(S["inv"], i + 1)
                    expand(act).then_inc(S["wide"], 1)

                pipeline(act, step)

            @block.vector
            def _(dve):
                def features(i, ts, first):
                    for t in ts:
                        dve.wait_ge(S["f_done"], i * BT + t + 1)
                        if not first:
                            dve.wait_ge(S["kv_done"], i)
                        dve.tensor_scalar(feat[:, t, :], bank(B_F[t % 2]), 0.0, YAT_EPS, ALU.max,
                                          ALU.add).then_inc(S["f_ready"], 1)

                def keep(b):
                    dve.wait_ge(S["kv_done"], UNROLL * b + UNROLL)
                    mine = kvbd[:, bass.ds(b, 1)].rearrange("p a c w -> p (a c) w")
                    dve.tensor_tensor(mine[:, :, 0:KVW], kv[:, :, 0:KVW],
                                      m32[:].unsqueeze(1).to_broadcast([P, NCH, KVW]), ALU.mult)
                    dve.tensor_tensor(mine[:, :, KVW:KVW + HPC], kv[:, :, KVW:KVW + 1].to_broadcast([P, NCH, HPC]),
                                      m4[:].unsqueeze(1).to_broadcast([P, NCH, HPC]), ALU.mult).then_inc(S["kv_read"], 1)

                def step(i, u_before, b=None):
                    first, live = b is None and i == 0, b is not None or i < NB
                    if not first:
                        features(i - 1, (0, 1), b is None and i == 1)
                    if live:
                        dve.wait_ge(S["root"], i + 1)
                        dve.tensor_scalar(root[:], root[:], NORM_EPS, None, ALU.add).then_inc(S["eps"], 1)
                        dve.wait_ge(S["eps"], i + 1)
                        dve.reciprocal(root[:], root[:]).then_inc(S["inv"], 1)
                    if not first:
                        features(i - 1, (2, 3), b is None and i == 1)
                    if live:
                        dve.wait_ge(S["vt_done"], i + 1)
                        if not first:
                            dve.wait_ge(S["kv_done"], i)
                        dve.tensor_copy(vones[:, :, :, 0:KVW],
                                        tiles(B_VT).rearrange("p t (c w) -> p t c w", c=NCH)).then_inc(S["v_ready"], 1)
                        dve.wait_ge(S["w_done"], i + 1)
                        dve.tensor_tensor(an[:], aT[:], bank(B_W), ALU.mult).then_inc(S["an_ready"], 1)
                    if u_before == -1 and b is not None:
                        keep(b - 1)
                    if not live:
                        keep(BATCH - 1)

                pipeline(dve, step)

    def linear_q():
        names = ("q_done", "sq_ready", "n_done", "root", "eps", "inv", "wide", "w_done", "an_ready", "f_done",
                 "f_ready", "qkv_done", "den_max", "den_inv", "o_ready", "oT_done", "oT_ready", "y_done", "added", "step",
                 "xn_ready", "xT_done", "xh_done", "xl_done")
        S = {n: sem(f"a0q_{n}") for n in names}
        B_Q, B_W, B_N, B_OT, B_XT, B_Y, B_F, B_QKV = 0, 0, 1, 1, 2, 3, (4, 5), (6, 7)
        W = KVW + HPC

        def pipeline(e, step):
            for i in range(-1, UNROLL):
                step(i, 0)
            with e.Fori(1, BATCH - 1) as b:
                for u in range(UNROLL):
                    step(b * UNROLL + u, b)
            for i in range(NB - UNROLL, NB + 2):
                step(i, BATCH - 1)

        def there(i):
            return not isinstance(i, int) or 0 <= i < NB

        def first(i):
            return isinstance(i, int) and i == 0

        with nc.Block() as block:
            @block.tensor
            def _(pe):
                def query(i):
                    if not first(i):
                        pe.wait_ge(S["an_ready"], i)
                    product3(pe, bank(B_Q), w0[:, 0, 0], w0[:, 1, 0], i).then_inc(S["q_done"], 1)

                def norms(i):
                    pe.wait_ge(S["sq_ready"], i + 1)
                    square_sums(pe, bank(B_N)).then_inc(S["n_done"], 1)

                def widen(i):
                    pe.wait_ge(S["wide"], i + 1)
                    for t in range(BT):
                        last = pe.transpose(tiles(B_W)[:, t, :], nrm[:, t * P:(t + 1) * P], ident[:])
                    last.then_inc(S["w_done"], 1)

                def features(i, cs):
                    pe.wait_ge(S["an_ready"], i + 1)
                    for c in cs:
                        if c >= 2 or not first(i):
                            pe.wait_ge(S["f_ready"], i * NCH + c - 1)
                        pe.matmul(bank(B_F[c % 2]), pbd[:, c * P:(c + 1) * P], an[:], start=True,
                                  stop=True).then_inc(S["f_done"], 1)

                def attend(i, b):
                    pe.wait_ge(S["f_ready"], i * NCH + NCH)
                    if not first(i):
                        pe.wait_ge(S["o_ready"], i)
                    for t in range(BT):
                        for c in range(NCH):
                            at = (t % 2 * NCH + c) * W
                            last = pe.matmul(bank(B_QKV[t // 2])[:, at:at + W], feat[:, c, t * P:(t + 1) * P],
                                             kvbd[:, bass.ds(b, 1), c, :].rearrange("p a w -> p (a w)"),
                                             start=True, stop=True)
                    last.then_inc(S["qkv_done"], 1)

                def turn(i):
                    pe.wait_ge(S["o_ready"], i + 1)
                    if there(i + 1):
                        pe.wait_ge(S["root"], i + 2)
                    for t in range(BT):
                        last = pe.transpose(tiles(B_OT)[:, t, :], o0[:, t, :], ident[:])
                    last.then_inc(S["oT_done"], 1)

                def project(i):
                    pe.wait_ge(S["oT_ready"], i + 1)
                    if not first(i):
                        pe.wait_ge(S["added"], i)
                    pe.matmul(tiles(B_Y), onerow[:], borow[:].unsqueeze(1).to_broadcast([1, BT, P]), start=True, stop=True)
                    for t in range(BT):
                        last = pe.matmul(tiles(B_Y)[:, t, :], o0T[:, t * P:(t + 1) * P], wo0[:], start=False,
                                         stop=True, skip_group_check=True)
                    last.then_inc(S["y_done"], 1)

                def next_xT(i):
                    pe.wait_ge(S["xn_ready"], i + 1)
                    pe.wait_ge(S["xl_done"], i + 1)
                    for t in range(BT):
                        last = pe.transpose(tiles(B_XT)[:, t, :], xn[:, t, :], ident[:])
                    last.then_inc(S["xT_done"], 1)

                def step(i, b):
                    if there(i + 1):
                        query(i + 1)
                    if there(i - 1):
                        turn(i - 1)
                    if there(i):
                        features(i, (0, 1))
                    if there(i + 1):
                        if there(i - 1):
                            pe.wait_ge(S["oT_ready"], i)
                        norms(i + 1)
                    if there(i):
                        features(i, (2, 3))
                        attend(i, b)
                    if there(i + 1):
                        widen(i + 1)
                    if there(i - 1):
                        project(i - 1)
                    if there(i - 2):
                        next_xT(i - 2)

                pipeline(pe, step)

            @block.scalar
            def _(act):
                def step(i, b):
                    if there(i + 1):
                        act.wait_ge(S["q_done"], i + 2)
                        if there(i):
                            act.wait_ge(S["an_ready"], i + 1)
                        act.activation(aT[:], bank(B_Q), ACT.Identity, bias=bcol[:, 0:1])
                        act.activation(sq[:], bank(B_Q), ACT.Square, bias=bcol[:, 0:1]).then_inc(S["sq_ready"], 1)
                    if there(i - 1):
                        act.wait_ge(S["oT_done"], i)
                        if there(i - 2):
                            act.wait_ge(S["y_done"], i - 1)
                        act.activation(o0T[:], bank(B_OT), ACT.Copy).then_inc(S["oT_ready"], 1)
                    if there(i + 1):
                        act.wait_ge(S["n_done"], i + 2)
                        act.activation(root[:], bank(B_N)[:, 0:BT * H0], ACT.Sqrt).then_inc(S["root"], 1)
                        act.wait_ge(S["inv"], i + 2)
                        expand(act).then_inc(S["wide"], 1)
                    if there(i - 2):
                        act.wait_ge(S["xT_done"], i - 1)
                        act.activation(xh[:, blk(i - 2)], bank(B_XT), ACT.Copy).then_inc(S["xh_done"], 1)

                pipeline(act, step)

            @block.vector
            def _(dve):
                def by_head(ap):
                    return ap.rearrange("p t (c h) -> p (t c) h", c=NCH)

                def output(i):
                    dve.wait_ge(S["qkv_done"], i + 1)
                    acc = [bank(k)[:, 0:2 * NCH * W].rearrange("p (t w) -> p t w", w=W) for k in B_QKV]
                    for g in range(2):
                        last = dve.tensor_scalar(by_head(den[:, 2 * g:2 * g + 2, :]), acc[g][:, :, KVW:W], DEN_MIN, None,
                                                 ALU.max)
                    last.then_inc(S["den_max"], 1)
                    dve.wait_ge(S["den_max"], i + 1)
                    dve.reciprocal(den[:], den[:]).then_inc(S["den_inv"], 1)
                    dve.wait_ge(S["den_inv"], i + 1)
                    if not first(i):
                        dve.wait_ge(S["oT_done"], i)
                    for g in range(2):
                        last = dve.tensor_tensor(
                            o0[:, 2 * g:2 * g + 2, :].rearrange("p t (c h d) -> p (t c) h d", c=NCH, h=HPC),
                            acc[g][:, :, 0:KVW].rearrange("p t (h d) -> p t h d", h=HPC),
                            by_head(den[:, 2 * g:2 * g + 2, :]).unsqueeze(3).to_broadcast([P, 2 * NCH, HPC, HD0]),
                            ALU.mult)
                    last.then_inc(S["o_ready"], 1)

                def normalise(i, steps):
                    if not there(i):
                        return
                    if steps[0] == 0:
                        dve.wait_ge(S["added"], i + 1)
                    for k in steps:
                        ln_step(dve, i, k, S["step"], S["xn_ready"])

                def features(i, c):
                    if not there(i):
                        return
                    dve.wait_ge(S["f_done"], i * NCH + c + 1)
                    if not first(i):
                        dve.wait_ge(S["qkv_done"], i)
                    dve.tensor_scalar(feat[:, c, :], bank(B_F[c % 2]), 0.0, YAT_EPS, ALU.max,
                                      ALU.add).then_inc(S["f_ready"], 1)

                def step(i, b):
                    features(i, 0)
                    normalise(i - 2, (0,))
                    features(i, 1)
                    normalise(i - 2, (1, 2))
                    if there(i + 1):
                        dve.wait_ge(S["root"], i + 2)
                        dve.tensor_scalar(root[:], root[:], NORM_EPS, None, ALU.add).then_inc(S["eps"], 1)
                        normalise(i - 2, (3,))
                        dve.wait_ge(S["eps"], i + 2)
                        dve.reciprocal(root[:], root[:]).then_inc(S["inv"], 1)
                    else:
                        normalise(i - 2, (3,))
                    normalise(i - 2, (4, 5))
                    features(i, 2)
                    normalise(i - 2, (6, 7))
                    features(i, 3)
                    normalise(i - 2, range(8, LN_STEPS - 1))
                    if there(i + 1):
                        dve.wait_ge(S["w_done"], i + 2)
                        dve.tensor_tensor(an[:], aT[:], bank(B_W), ALU.mult).then_inc(S["an_ready"], 1)
                    normalise(i - 2, (LN_STEPS - 1,))
                    if there(i):
                        output(i)
                    if there(i - 1):
                        dve.wait_ge(S["y_done"], i)
                        xb = x[:, blk(i - 1, BT), :]
                        dve.tensor_tensor(xb, xb, tiles(B_Y), ALU.add).then_inc(S["added"], 1)
                    if there(i - 2):
                        dve.wait_ge(S["xh_done"], i - 1)
                        dve.tensor_tensor(xl[:, blk(i - 2)], bank(B_XT), xh[:, blk(i - 2)].bitcast(F32),
                                          ALU.subtract).then_inc(S["xl_done"], 1)

                dve.tensor_copy(spare_v[:], spare_v[:]).then_inc(S["xl_done"], 1)
                pipeline(dve, step)

    def turn_sems(ph):
        return {n: sem(f"{ph}_{n}") for n in ("g_turned", "g_hi", "g_lo")}

    def turn_pe(pe, T, n_exp, banks):
        for i in range(NB):
            if i >= 2:
                pe.wait_ge(T["g_lo"], i - 1)
            for t in range(BT):
                last = pe.transpose(bank(banks[i % 2])[0:n_exp, t * P:(t + 1) * P], gate[:, i * BT + t, 0:n_exp], ident[:])
            last.then_inc(T["g_turned"], 1)

    def turn_act(act, T, n_exp, banks):
        with act.Fori(0, NB // 2) as g:
            for a in range(2):
                act.wait_ge(T["g_turned"], 2 * g + a + 1)
                act.activation(gT[0:n_exp, blk(2 * g + a)], bank(banks[a])[0:n_exp, :], ACT.Copy).then_inc(T["g_hi"], 1)

    def turn_dve(dve, T, n_exp, banks):
        with dve.Fori(0, NB // 2) as g:
            for a in range(2):
                dve.wait_ge(T["g_hi"], 2 * g + a + 1)
                dve.tensor_tensor(gT[LO_ROW:LO_ROW + n_exp, blk(2 * g + a)], bank(banks[a])[0:n_exp, :],
                                  gT[0:n_exp, blk(2 * g + a)].bitcast(F32), ALU.subtract).then_inc(T["g_lo"], 1)

    def route_moe(ph, load_vo):
        names = ("logit_done", "exp_done", "step", "m_ready", "counted")
        S = {n: sem(f"{ph}_{n}") for n in names}
        gate_set, T, TURN = sem(f"{ph}_gate_set"), turn_sems(ph), (0, 1)
        N = NT * E1
        space = [hg[:, a, k * N:(k + 1) * N].rearrange("p (t e) -> p t e", t=NT) for a in range(2) for k in range(2)]
        L, G, A, M1 = space
        B2, M2 = (r[:, 1, k * N:(k + 1) * N].rearrange("p (t e) -> p t e", t=NT) for k in range(2))
        small = st16[:]
        if load_vo:
            v_load, o_load, v_cast, o_turned, o_hi, o_lo = (sem("vo_" + s) for s in (
                "v_load", "o_load", "v_cast", "o_turned", "o_hi", "o_lo"))
            qk_load, qk_turned, qkT_ready, f_done, f_out, f_hi, f_lo = (sem("qk_" + s) for s in (
                "load", "turned", "ready", "f_done", "f_out", "f_hi", "f_lo"))
            PAIRS = H1 // 2
            EARLY = PAIRS // 2
        with nc.Block() as block:
            @block.tensor
            def _(pe):
                token_logits(pe, bank(0), wgw, range(NT)).then_inc(S["logit_done"], 1)
                def forms(pairs):
                    for g in pairs:
                        for a in range(2):
                            for k, w in enumerate((raw_q, raw_k)):
                                last = pe.transpose(bank(6)[0:DK, (2 * a + k) * P:(2 * a + k + 1) * P],
                                                    w[:, (2 * g + a) * DK:(2 * g + a + 1) * DK], ident[:])
                        last.then_inc(qk_turned, 1)
                        pe.wait_ge(qkT_ready, g + 1)
                        for a in range(2):
                            last = pe.matmul(bank(7)[:, a * P:(a + 1) * P], qkT[:, 2 * a, :], qkT[:, 2 * a + 1, :],
                                             start=True, stop=True)
                        last.then_inc(f_done, 1)

                if load_vo:
                    pe.wait_ge(qk_load, 32)
                    forms(range(EARLY))
                pe.wait_ge(S["m_ready"], 1)
                pe.matmul(bank(2), before[:], m16[:].rearrange("p t e -> p (t e)"), start=True,
                          stop=True).then_inc(S["counted"], 1)
                pe.matmul(bank(3), onesb[:], m16[:].rearrange("p t e -> p (t e)"), start=True,
                          stop=True).then_inc(S["counted"], 1)
                if load_vo:
                    forms(range(EARLY, PAIRS))
                    pe.wait_ge(o_load, 16)
                    for k in range(2):
                        for q in range(BT):
                            last = pe.transpose(tiles(4 + k)[:, q, :], raw_o[:, (k * BT + q) * P:(k * BT + q + 1) * P],
                                                ident[:])
                        last.then_inc(o_turned, 1)
                pe.wait_ge(gate_set, 1)
                turn_pe(pe, T, E1, TURN)

            @block.scalar
            def _(act):
                act.wait_ge(S["step"], 3)
                act.activation(G, A, ACT.Exp).then_inc(S["exp_done"], 1)
                if load_vo:
                    def forms(g, slot, first):
                        act.wait_ge(qk_turned, g + 1)
                        act.activation(qkT, bank(6)[0:DK, :].rearrange("p (k d) -> p k d", k=4), ACT.Copy
                                       ).then_inc(qkT_ready, 1)
                        act.wait_ge(f_done, g + 1)
                        if not first:
                            act.wait_ge(f_lo, g - 1)
                        act.activation(form[slot], bank(7)[:, 0:2 * P], ACT.Copy, scale=LOGIT_SCALE).then_inc(f_out, 1)

                    for g in range(2):
                        forms(g, g, True)
                    with act.Fori(1, PAIRS // 2) as g:
                        for a in range(2):
                            forms(2 * g + a, a, False)
                if load_vo:
                    for k in range(2):
                        act.wait_ge(o_turned, k + 1)
                        act.activation(o_h[:, k * BLK:(k + 1) * BLK], bank(4 + k), ACT.Copy).then_inc(o_hi, 1)
                turn_act(act, T, E1, TURN)

            @block.vector
            def _(dve):
                n = 0

                def then(ins):
                    nonlocal n
                    n += 1
                    ins.then_inc(S["step"], 1)
                    dve.wait_ge(S["step"], n)

                def wide(v):
                    return v.unsqueeze(2).to_broadcast([P, NT, E1])

                back8 = iota8[:].unsqueeze(1).to_broadcast([P, NT, E1])
                s1, s2 = small[:, 0, :], small[:, 1, :]

                def first_max(values, mask):
                    then(dve.tensor_reduce(s1, values, AX.X, ALU.max))
                    then(dve.tensor_tensor(A, values, wide(s1), ALU.is_equal))
                    then(dve.tensor_tensor(A, A, back8, ALU.mult))
                    then(dve.tensor_reduce(s2, A, AX.X, ALU.min))
                    then(dve.tensor_tensor(mask, back8, wide(s2), ALU.is_equal))

                dve.wait_ge(S["logit_done"], 1)
                then(dve.tensor_copy(L, bank(0)[:, 0:N].rearrange("p (t e) -> p t e", t=NT)))
                then(dve.tensor_reduce(s1, L, AX.X, ALU.max))
                then(dve.tensor_tensor(A, L, wide(s1), ALU.subtract))
                dve.wait_ge(S["exp_done"], 1)
                then(dve.tensor_reduce(s1, G, AX.X, ALU.add))
                then(dve.reciprocal(s2, s1))
                then(dve.tensor_tensor(G, G, wide(s2), ALU.mult))
                first_max(G, M1)
                then(dve.scalar_tensor_tensor(B2, M1, -3e38, L, ALU.mult, ALU.add))
                first_max(B2, M2)
                then(dve.tensor_copy(m16[:, :, 0:E1], M1))
                n += 1
                dve.tensor_copy(m16[:, :, E1:], M2).then_inc(S["step"], 1)
                dve.wait_ge(S["step"], n)
                dve.tensor_copy(small[:, 2, 0:1], small[:, 2, 0:1]).then_inc(S["m_ready"], 1)
                dve.wait_ge(S["counted"], 2)
                c0 = bank(3).rearrange("p (t e) -> p t e", t=NT)
                then(dve.tensor_copy(p16[:, 0], c0))
                src, reach = 0, 1
                while reach < NT:
                    dve.tensor_copy(p16[:, 1 - src, 0:reach, :], p16[:, src, 0:reach, :])
                    then(dve.tensor_tensor(p16[:, 1 - src, reach:, :], p16[:, src, reach:, :],
                                           p16[:, src, 0:NT - reach, :], ALU.add))
                    src, reach = 1 - src, 2 * reach
                tot, pos = p16[:, src], p16[:, 1 - src]
                then(dve.tensor_tensor(pos, tot, c0, ALU.subtract))
                then(dve.tensor_tensor(pos, pos, bank(2).rearrange("p (t e) -> p t e", t=NT), ALU.add))
                then(dve.tensor_tensor(pos[:, :, E1:], pos[:, :, E1:],
                                       tot[:, NT - 1:NT, 0:E1].to_broadcast([P, NT, E1]), ALU.add))
                then(dve.tensor_scalar(pos, pos, float(CAP), None, ALU.is_lt))
                then(dve.tensor_tensor(A, M1, pos[:, :, 0:E1], ALU.mult))
                then(dve.tensor_tensor(B2, M2, pos[:, :, E1:], ALU.mult))
                then(dve.tensor_tensor(B2, A, B2, ALU.add))
                then(dve.tensor_tensor(A, M1, M2, ALU.add))
                then(dve.tensor_tensor(A, A, G, ALU.mult))
                then(dve.tensor_reduce(s1, A, AX.X, ALU.add))
                then(dve.tensor_scalar(s1, s1, GATE_EPS, None, ALU.add))
                then(dve.reciprocal(s2, s1))
                then(dve.tensor_tensor(G, G, B2, ALU.mult))
                dve.tensor_tensor(gate[:, :, 0:E1], G, wide(s2), ALU.mult).then_inc(gate_set, 1)
                if load_vo:
                    for k in range(2):
                        dve.wait_ge(o_hi, k + 1)
                        dve.tensor_tensor(o_l[:, k * BLK:(k + 1) * BLK], bank(4 + k),
                                          o_h[:, k * BLK:(k + 1) * BLK].bitcast(F32), ALU.subtract).then_inc(o_lo, 1)
                turn_dve(dve, T, E1, TURN)

            if load_vo:
                @block.sync
                def _(sp):
                    for w, n, loaded in ((raw_q, "q", qk_load), (raw_k, "k", qk_load), (raw_v, "v", v_load), (raw_o, "o", o_load)):
                        sp.dma_start(w[:].rearrange("p (h v) -> p h v", h=H1),
                                     I["L1_attn_P_" + n].rearrange("h d v -> d h v")).then_inc(loaded, 16)

                @block.gpsimd
                def _(pool):
                    pool.wait_ge(v_load, 16)
                    pool.tensor_copy(v_h, raw_v[:]).then_inc(v_cast, 1)
                    pool.wait_ge(v_cast, 1)
                    pool.tensor_tensor(v_l, raw_v[:], v_h.bitcast(F32), ALU.subtract)
                    with pool.Fori(0, PAIRS // 2) as g:
                        for a in range(2):
                            two = bass.ds((2 * g + a) * 2 * P, 2 * P)
                            pool.wait_ge(f_out, 2 * g + a + 1)
                            apart(pool, spare_p)
                            pool.tensor_copy(wreg[:, 2, two], form[a]).then_inc(f_hi, 1)
                            pool.wait_ge(f_hi, 2 * g + a + 1)
                            pool.tensor_tensor(wreg[:, 3, two], form[a], wreg[:, 2, two].bitcast(F32), ALU.subtract
                                               ).then_inc(f_lo, 1)

    def softmax_diagonal():
        fold = [gate[:, k * NT // 2:(k + 1) * NT // 2, H1:].rearrange("p (t a) e -> p t a e", a=2) for k in range(2)]
        diag = ed[:].rearrange("p k t d -> p (k t) d")
        names = ("halved", "folded", "w_ready", "y_done", "y_hi", "y_lo", "sc_done", "mx_done", "exp_done", "dg_done", "red_done",
                 "rec_done", "p_set")
        S = {n: sem(f"a1_{n}") for n in names}
        T, TURN = turn_sems("a1"), (0, 1)
        YH, YL = ([w[:].rearrange("p s n -> p (s n)")[:, k * SEQ:(k + 1) * SEQ] for k in range(2)] for w in (hh, hl))
        E = [r[:].rearrange("p s n -> p (s n)"), hg[:].rearrange("p s n -> p (s n)")]
        PER = BATCH
        ORDER = (7, 0, 1, 4, 6, 2, 5, 3)
        Y_AT = {0: 1, 3: 0}
        HIGH_AT = {0: 1, 2: 0}
        LOW_AT = {0: 1, 4: 0}
        BIG = [n for n, q in enumerate(ORDER) if q >= BT]
        PAIR = [k % 3 for k in range(PER * BT - 1)] + [1]

        def scores(b, n):
            q, odd = ORDER[n], b % 2
            if q >= BT:
                k = 2 * PAIR[b * BT + BIG.index(n)]
                return psum[:, k:k + 2, :].rearrange("p k n -> p (k n)")
            k = 7 - odd if q != 3 else 6 + odd
            return bank(k)[:, P:] if q == 1 else bank(k)

        def y_bank(b, half):
            return bank(6 + b % 2)

        def big_before(b, n):
            k = b * BT + BIG.index(n)
            d = next(d for d in range(1, PER * BT + 1) if PAIR[k - d] == PAIR[k])
            back = BIG.index(n) - d
            return QT * (back // BT) + BIG[back % BT]

        with nc.Block() as block:
            @block.gpsimd
            def _(pool):
                def quarter(k):
                    return diag[:, :, 32 * k:32 * (k + 1)].rearrange("p t (a e) -> p t a e", a=2)

                def weights(h):
                    for k, w in enumerate((f_h, f_l)):
                        last = pool.tensor_copy(hw[:, k], w[:, bass.ds(h, 1), :].rearrange("p a d -> p (a d)"))
                    last.then_inc(S["w_ready"], 1)

                def unit(u, b, first, turn):
                    if not (first and b == 0):
                        pool.wait_ge(S["folded"], u)
                    for n, q in enumerate(ORDER):
                        pool.wait_ge(S["exp_done"], u * QT + n + 1)
                        pool.tensor_tensor(diag[:, q, :], E[n % 2][:, q * P:(q + 1) * P], ident[:], ALU.mult
                                           ).then_inc(S["dg_done"], 1)
                        if n == 3 and turn is not None:
                            pool.wait_ge(S["y_done"], 2 * (u + 2))
                            apart(pool, spare_p)
                            weights(turn)
                    pool.wait_ge(S["dg_done"], u * QT + QT)
                    pool.tensor_tensor(diag[:, :, 0:64], diag[:, :, 0:64], diag[:, :, 64:], ALU.add
                                       ).then_inc(S["halved"], 1)
                    pool.wait_ge(S["halved"], u + 1)
                    if not first:
                        pool.wait_ge(S["red_done"], u - 1)
                    pool.tensor_tensor(fold[b % 2], quarter(0), quarter(1), ALU.add).then_inc(S["folded"], 1)

                weights(0)
                for b in range(PER):
                    unit(b, b, b < 2, 1 if b == PER - 2 else None)
                with pool.Fori(1, H1 - 1) as h:
                    for b in range(PER):
                        unit(h * PER + b, b, False, h + 1 if b == PER - 2 else None)
                for b in range(PER):
                    unit((H1 - 1) * PER + b, b, False, None)

            @block.tensor
            def _(pe):
                def product(u, b, half):
                    at = bass.ds(b * SEQ + half * BLK, BLK)
                    dst = y_bank(b + 1, half)
                    pe.matmul(dst, hw[:, 0], xl[:, at], start=True, stop=False)
                    pe.matmul(dst, hw[:, 1], xh[:, at], start=False, stop=False)
                    pe.matmul(dst, hw[:, 0], xh[:, at], start=False, stop=True).then_inc(S["y_done"], 1)

                def logits(u, b, n, first):
                    q, s = ORDER[n], b % 2
                    if q >= BT and not (first and big_before(b, n) < 0):
                        pe.wait_ge(S["exp_done"], u * QT + big_before(b, n) + 1)
                    if n == ORDER.index(0) and not first:
                        pe.wait_ge(S["exp_done"], u * QT)
                    if q == 2:
                        pe.wait_ge(S["exp_done"], u * QT + ORDER.index(1) + 1)
                    if q == 3 and not last_unit:
                        pe.wait_ge(S["y_lo"], 2 * u + 4)
                    dst, width = scores(b, n), (q + 1) * P
                    yh, yl = YH[s][:, q * P:(q + 1) * P], YL[s][:, q * P:(q + 1) * P]
                    for a in range(0, width, BLK):
                        z = min(a + BLK, width)
                        at = bass.ds(b * SEQ + a, z - a)
                        pe.matmul(dst[:, a:z], yh, xl[:, at], start=True, stop=False)
                        pe.matmul(dst[:, a:z], yl, xh[:, at], start=False, stop=False)
                        pe.matmul(dst[:, a:z], yh, xh[:, at], start=False, stop=(z < width))
                    pe.matmul(dst[:, q * P:width], identb[:], cmask[:], start=False, stop=True
                              ).then_inc(S["sc_done"], 1)

                def unit(u, b, first, last, w_count):
                    nonlocal last_unit
                    last_unit = last
                    for n in range(QT):
                        if n == 0:
                            pe.wait_ge(S["y_lo"], 2 * u + 2)
                        logits(u, b, n, first)
                        if n in Y_AT and not last:
                            if Y_AT[n]:
                                if not first:
                                    pe.wait_ge(S["exp_done"], u * QT - QT + ORDER.index(2) + 1)
                                if b == PER - 1:
                                    pe.wait_ge(S["w_ready"], w_count)
                            else:
                                pe.wait_ge(S["y_lo"], 2 * u + 3)
                            product(u + 1, (b + 1) % PER, Y_AT[n])

                last_unit = False
                pe.wait_ge(S["w_ready"], 1)
                product(0, 0, 1)
                pe.wait_ge(S["y_lo"], 1)
                product(0, 0, 0)
                for b in range(PER):
                    unit(b, b, b == 0, False, 2)
                with pe.Fori(1, H1 - 1) as h:
                    for b in range(PER):
                        unit(h * PER + b, b, False, False, h + 2)
                for b in range(PER):
                    unit((H1 - 1) * PER + b, b, False, b == PER - 1, H1)
                pe.wait_ge(S["p_set"], H1 * PER)
                turn_pe(pe, T, H1, TURN)

            @block.scalar
            def _(act):
                def high(u, b, half, first):
                    to = slice(half * BLK, (half + 1) * BLK)
                    act.wait_ge(S["y_done"], 2 * u + (2 - half))
                    if not first:
                        act.wait_ge(S["sc_done"], (u - 1) * QT)
                    act.activation(YH[b % 2][:, to], y_bank(b + 1, half), ACT.Copy).then_inc(S["y_hi"], 1)

                def unit(u, b, first, last):
                    for n, q in enumerate(ORDER):
                        if n in HIGH_AT and not last:
                            high(u + 1, b + 1, HIGH_AT[n], first)
                        act.wait_ge(S["mx_done"], u * QT + n + 1 + (q == 0))
                        if not (first and n < 2):
                            act.wait_ge(S["dg_done"], u * QT + n - 1)
                        if n == 0 and not (isinstance(u, int) and u < 2):
                            act.wait_ge(S["rec_done"], u - 1)
                        act.activation(E[n % 2][:, 0:(q + 1) * P], scores(b, n)[:, 0:(q + 1) * P], ACT.Exp,
                                       bias=nmax[:, b % 2, q:q + 1],
                                       accum_out=esum[:, b % 2, q:q + 1]).then_inc(S["exp_done"], 1)

                high(0, 0, 1, True)
                high(0, 0, 0, True)
                for b in range(PER):
                    unit(b, b, b == 0, False)
                with act.Fori(1, H1 - 1) as h:
                    for b in range(PER):
                        unit(h * PER + b, b, False, False)
                for b in range(PER):
                    unit((H1 - 1) * PER + b, b, False, b == PER - 1)
                turn_act(act, T, H1, TURN)

            @block.vector
            def _(dve):
                def low(u, b, half):
                    to = slice(half * BLK, (half + 1) * BLK)
                    dve.wait_ge(S["y_hi"], 2 * u + (2 - half))
                    dve.tensor_tensor(YL[b % 2][:, to], y_bank(b + 1, half), YH[b % 2][:, to].bitcast(F32), ALU.subtract
                                      ).then_inc(S["y_lo"], 1)

                def weights(u, h, b):
                    dve.wait_ge(S["exp_done"], u * QT + QT)
                    dve.reciprocal(rsum[:], esum[:, b % 2, :]).then_inc(S["rec_done"], 1)
                    dve.wait_ge(S["folded"], u + 1)
                    dve.tensor_reduce(dsum[:], fold[b % 2], AX.XY, ALU.add).then_inc(S["red_done"], 1)
                    dve.wait_ge(S["rec_done"], u + 1)
                    dve.wait_ge(S["red_done"], u + 1)
                    dst = gate[:, b * QT:(b + 1) * QT, bass.ds(h, 1)].rearrange("p t a -> p (t a)")
                    dve.tensor_tensor(dst, dsum[:], rsum[:], ALU.mult).then_inc(S["p_set"], 1)

                def unit(u, h, b, first, last):
                    for n, q in enumerate(ORDER):
                        dve.wait_ge(S["sc_done"], u * QT + n + 1 + (q == 0))
                        if n == 0 and not (isinstance(u, int) and u < 2):
                            dve.wait_ge(S["exp_done"], (u - 1) * QT)
                        dve.tensor_reduce(nmax[:, b % 2, q:q + 1], scores(b, n)[:, 0:(q + 1) * P], AX.X, ALU.max,
                                          negate=True).then_inc(S["mx_done"], 1)
                        if n in LOW_AT and not last:
                            low(u + 1, b + 1, LOW_AT[n])
                        if n == 3 and not first:
                            weights(u - 1, h if b else h - 1, (b - 1) % PER)

                low(0, 0, 1)
                low(0, 0, 0)
                for b in range(PER):
                    unit(b, 0, b, b == 0, False)
                with dve.Fori(1, H1 - 1) as h:
                    for b in range(PER):
                        unit(h * PER + b, h, b, False, False)
                for b in range(PER):
                    unit((H1 - 1) * PER + b, H1 - 1, b, False, b == PER - 1)
                weights(H1 * PER - 1, H1 - 1, PER - 1)
                turn_dve(dve, T, H1, TURN)

    st16 = r[:, 0, NT * E1:NT * E1 + 3 * NT].rearrange("p (k t) -> p k t", k=3)
    m16 = r[:, 0, 0:NT * E1].bitcast(BF16).rearrange("p (t e) -> p t e", t=NT)
    p16 = gate[:].rearrange("p (k t) (a e) -> p k (t a) e", k=2, e=2 * E1)
    iota8 = sb("iota8", [P, E1], F32)
    nmax = sb("nmax", [P, 2, QT], F32)
    esum = sb("esum", [P, 2, QT], F32)
    dsum = sb("dsum", [P, QT], F32)
    rsum = sb("rsum", [P, QT], F32)

    ffn = dict(nf=NF0, up=(f_uph, f_upl), dn=(f_dnh, f_dnl), per_gate=1, func=ACT.Relu, bias=None, b2=None, scale=0.5)
    moe = dict(nf=NF1, up=(m_up[:, 0], m_up[:, 1]), dn=(m_dn[:, 0], m_dn[:, 1]), per_gate=F1 // P, func=ACT.Gelu,
               bias=b1c, b2=b2w, scale=0.5)
    setup()
    end_phase()
    route_ffn("r0", False)
    end_phase()
    gated("f0", final=False, **ffn)
    end_phase()
    linear_kv()
    end_phase()
    linear_q()
    end_phase()
    route_ffn("r1", True)
    end_phase()
    gated("f1", final=False, **ffn)
    end_phase()
    route_moe("r2", True)
    end_phase()
    gated("m0", final=False, **moe)
    end_phase()
    softmax_diagonal()
    end_phase()
    gated("a1o", nf=NF2, up=(v_h, v_l), dn=(o_h, o_l), per_gate=1, func=ACT.Identity, bias=None, b2=None, scale=1.0,
          final=False)
    end_phase()
    route_moe("r4", False)
    end_phase()
    gated("m1", final=True, **moe)
    top.close()


_INS = ['L0_attn_x', 'L0_attn_Wq', 'L0_attn_bq', 'L0_attn_Wk', 'L0_attn_bk', 'L0_attn_Wv', 'L0_attn_bv', 'L0_attn_Wo',
        'L0_attn_bo', 'L0_attn_projection', 'L0_ffn_expert_sel', 'L0_ffn_keys', 'L0_ffn_values', 'L1_attn_P_q',
        'L1_attn_P_k', 'L1_attn_P_v', 'L1_attn_P_o', 'L1_ffn_Wg', 'L1_ffn_W1', 'L1_ffn_b1', 'L1_ffn_W2', 'L1_ffn_b2']
_OUTS = [((BATCH, SEQ, P), 'float32')]


def kernel(**inputs):
    import numpy as _np
    import concourse.bacc as _bacc
    from concourse import mybir as _mybir
    from concourse.bass_utils import run_bass_kernel_spmd as _run

    nc = _bacc.Bacc("TRN2", target_bir_lowering=False, num_devices=1)
    arrays, args = {}, {}
    for name in _INS:
        a = _np.ascontiguousarray(inputs[name])
        arrays[f"in_{name}_dram"] = a
        args[name] = nc.dram_tensor(f"in_{name}_dram", a.shape, _mybir.dt.from_np(a.dtype), kind="ExternalInput").ap()
    (shape, dtype), = _OUTS
    out = nc.dram_tensor("out_0_dram", shape, _mybir.dt.from_np(_np.dtype(dtype)), kind="ExternalOutput").ap()
    build(nc, args, out)
    r = _run(nc, [arrays], core_ids=[0])
    return r.results[0]["out_0_dram"]
```

```python
from contextlib import ExitStack

import concourse.bass as bass
from concourse import mybir

F32 = mybir.dt.float32
F32R = mybir.dt.float32r
BF16 = mybir.dt.bfloat16
I32 = mybir.dt.int32
U32 = mybir.dt.uint32
ALU = mybir.AluOpType
ACT = mybir.ActivationFunctionType
AX = mybir.AxisListType

P = 128
BATCH, SEQ = 4, 1024
T = BATCH * SEQ
NT = T // P
BT = 4
BLK = BT * P
NB = T // BLK
LN_EPS = 1e-5
E0, F0, TOP0 = 32, 64, 4
NF0 = E0 * F0 // P
H0, HD0, FEAT0 = 16, 8, 32
NCH = H0 * FEAT0 // P
HPC = P // FEAT0
KVW = HPC * HD0
YAT_EPS, NORM_EPS, DEN_MIN = 0.1, 1e-8, 1e-6
E1, F1 = 8, 512
NF1 = E1 * F1 // P
CAP = 2 * 2 * T // E1
GATE_EPS = 1e-9
H1, DK = 16, 64
NF2 = H1 * DK // P
QT = SEQ // P
LOGIT_SCALE = 8.0
MASKED = -1e38
LO_ROW = 32
LAG = 4
SLOTS = 4
SPARSE = 2 * T // BLK + E1 - 1
REGION = T + BLK
ROWS = E1 * REGION + BLK
ROW = P + 1
NOWHERE = 1.0
MAGIC = 0x5F3759DF


def build(nc, I, out):
    top = ExitStack()

    def sb(name, shape, dt, stack=top):
        return stack.enter_context(nc.sbuf_tensor(name, shape, dt))

    held = []

    def sem(name):
        held.append(nc.alloc_semaphore(name))
        return held[-1]

    def end_phase():
        nc.clear_and_free_semaphores(list(held))
        nc.all_engine_barrier()
        held.clear()

    x = sb("x", [P, NT, P], F32)
    xh = sb("xh", [P, T], F32R)
    xl = sb("xl", [P, T], F32R)
    wreg = sb("wreg", [P, 4, 2048], F32R)
    r = sb("r", [P, 2, BLK], F32)
    hg = sb("hg", [P, 2, BLK], F32)
    raw_mem = ExitStack()
    raw_all = sb("raw_all", [P, 4, H1 * DK], F32, raw_mem)
    raw_q, raw_k, raw_v, raw_o = (raw_all[:, k, :] for k in range(4))
    raw_mem.close()
    hh = sb("hh", [P, SLOTS, BLK], F32R)
    hl = sb("hl", [P, SLOTS, BLK], F32R)
    gT = sb("gT", [2 * LO_ROW, T], F32R)
    pick = sb("pick", [2 * LO_ROW, 2, P], F32R)
    gate = sb("gate", [P, NT, 32], F32)
    ident = sb("ident", [P, P], F32)
    identb = sb("identb", [P, P], BF16)
    before = sb("before", [P, P], BF16)
    onesb = sb("onesb", [P, P], BF16)
    cmask = sb("cmask", [P, P], BF16)
    iota = sb("iota", [P, 32], F32)
    routers = sb("routers", [P, 2, P], F32R)
    selw, wgw = routers[:, :, 0:E0], routers[:, :, E0:E0 + E1]
    b1c = sb("b1c", [P, NF1], F32)
    b2c = sb("b2c", [P, E1], F32)
    kept_mean, kept_rs = sb("kept_mean", [P, NT], F32), sb("kept_rs", [P, NT], F32)
    weight2 = sb("weight2", [P, 2, NT], F32)
    answer = sb("answer", [P, 2, NT], I32)
    expert_of = sb("expert_of", [P, SPARSE + 2], I32)
    blank = sb("blank", [P, ROW], F32)
    row = sb("row", [P, BT, 2, ROW], F32)
    row_to = sb("row_to", [P, BT, 2], I32)
    b1_now, b2_now = sb("b1_now", [P, 2, F1 // P], F32), sb("b2_now", [P, 2], F32)
    answer_to = sb("answer_to", [P, 2, BT], I32)
    rows = nc.dram_tensor("rows", [ROWS, ROW], F32, kind="Internal").ap()
    answers = nc.dram_tensor("answers", [2 * T, P], F32, kind="Internal").ap()
    st = sb("st", [P, BT, 6], F32)
    mv = sb("mv", [P, BT, 2], F32)
    var, rs, rt = (sb(n, [P, BT], F32) for n in ("var", "rs", "rt"))
    ed = sb("ed", [P, 2, BT, P], F32)
    xn = ed[:, 0]
    oT = ed[:, 1].rearrange("p t d -> p (t d)")
    hw = sb("hw", [P, 2, P], F32R)
    psum = top.enter_context(nc.psum_tensor("psum", [P, 8, BLK], F32))

    def bank(k):
        return psum[:, k, :]

    def tiles(k):
        return psum[:, k, :].rearrange("p (t d) -> p t d", t=BT)

    def blk(i, n=BLK):
        return bass.ds(i * n, n)

    x_in = I["L0_attn_x"].rearrange("b s d -> (b s) d").rearrange("(t p) d -> p t d", p=P)
    out_v = out.rearrange("b s d -> (b s) d").rearrange("(t p) d -> p t d", p=P)

    spare_v, spare_p = sb("spare_v", [P, 1], F32), sb("spare_p", [P, 1], F32)

    def apart(e, spare):
        return e.tensor_tensor(spare[:], spare[:], spare[:], ALU.mult)

    LN_STEPS = 15

    def ln_step(e, i, k, step, xn_ready, nt=BT, keep=False):
        xn = ed[:].rearrange("p k t d -> p (k t) d")
        v, y, z = var[:, 0:nt], rs[:, 0:nt], rt[:, 0:nt]
        if k > 0:
            e.wait_ge(step, (LN_STEPS - 1) * i + k)
        if k == 0:
            apart(e, spare_v)
            for t in range(nt):
                last = e.bn_stats(st[:, t, :], x[:, bass.ds(i * nt + t, 1), :].rearrange("p a d -> p (a d)"))
        elif k == 1:
            apart(e, spare_v)
            for t in range(nt):
                last = e.bn_aggr(mv[:, t, :], st[:, t, :])
        elif k == 2:
            last = e.tensor_scalar(v, mv[:, 0:nt, 1], LN_EPS, None, ALU.add)
        elif k == 3:
            last = e.tensor_scalar(z.bitcast(I32), v.bitcast(I32), 1, None, ALU.logical_shift_right)
        elif k == 4:
            last = e.tensor_scalar(y.bitcast(I32), z.bitcast(I32), -1.0, float(MAGIC), ALU.mult, ALU.add)
        elif k == LN_STEPS - 1:
            for t in range(nt):
                if t == 1 and keep:
                    e.tensor_copy(kept_mean[:, blk(i, nt)], mv[:, 0:nt, 0])
                    e.tensor_copy(kept_rs[:, blk(i, nt)], rs[:, 0:nt])
                last = e.tensor_scalar(xn[:, t, :], x[:, bass.ds(i * nt + t, 1), :].rearrange("p a d -> p (a d)"),
                                       mv[:, t, 0:1], rs[:, t:t + 1], ALU.subtract, ALU.mult)
        elif k % 3 == 2:
            last = e.tensor_tensor(z, y, y, ALU.mult)
        elif k % 3 == 0:
            last = e.scalar_tensor_tensor(z, z, -0.5, v, ALU.mult, ALU.mult)
        else:
            last = e.scalar_tensor_tensor(y, z, 1.5, y, ALU.add, ALU.mult)
        last.then_inc(xn_ready if k == LN_STEPS - 1 else step, 1)

    room = gate[:].rearrange("p t e -> p (t e)")
    stats, aggr = (room[:, a * NT:(a + w) * NT].rearrange("p (t w) -> p t w", w=w) for a, w in ((0, 6), (6, 2)))
    v_all, y_all, z_all = (room[:, (8 + k) * NT:(9 + k) * NT] for k in range(3))

    def measure(dve, i, measured):
        for t in range(i * BT, (i + 1) * BT):
            last = dve.bn_stats(stats[:, t, :], x[:, t, :])
        last.then_inc(measured, 1)

    def gather(dve, i, measured):
        dve.wait_ge(measured, i + 1)
        for t in range(i * BT, (i + 1) * BT):
            last = dve.bn_aggr(aggr[:, t, :], stats[:, t, :])
        return last

    def deviations(dve, then):
        v, y, z = v_all, y_all, z_all
        then(dve.tensor_scalar(v, aggr[:, :, 1], LN_EPS, None, ALU.add))
        then(dve.tensor_scalar(z.bitcast(I32), v.bitcast(I32), 1, None, ALU.logical_shift_right))
        then(dve.tensor_scalar(y.bitcast(I32), z.bitcast(I32), -1.0, float(MAGIC), ALU.mult, ALU.add))
        for _ in range(3):
            then(dve.tensor_tensor(z, y, y, ALU.mult))
            then(dve.scalar_tensor_tensor(z, z, -0.5, v, ALU.mult, ALU.mult))
            then(dve.scalar_tensor_tensor(y, z, 1.5, y, ALU.add, ALU.mult))

    def split_dve(dve, S):
        def low(i):
            dve.wait_ge(S["xh_done"], i + 1)
            dve.tensor_tensor(xl[:, blk(i)], bank(i % 2), xh[:, blk(i)].bitcast(F32), ALU.subtract
                              ).then_inc(S["xl_done"], 1)

        for i in range(NB):
            if i >= 2:
                dve.wait_ge(S["xT_done"], i - 1)
            for t in range(BT):
                at = i * BT + t
                last = dve.tensor_scalar(ed[:, i % 2, t, :], x[:, at, :], aggr[:, at, 0:1], y_all[:, at:at + 1],
                                         ALU.subtract, ALU.mult)
            last.then_inc(S["xn_ready"], 1)
            if i >= 1:
                low(i - 1)
        low(NB - 1)

    def split_pe(pe, S):
        for i in range(NB):
            pe.wait_ge(S["xn_ready"], i + 1)
            if i >= 2:
                pe.wait_ge(S["xl_done"], i - 1)
            for t in range(BT):
                last = pe.transpose(tiles(i % 2)[:, t, :], ed[:, i % 2, t, :], ident[:])
            last.then_inc(S["xT_done"], 1)

    def split_act(act, S, i):
        act.wait_ge(S["xT_done"], i + 1)
        act.activation(xh[:, blk(i)], bank(i % 2), ACT.Copy).then_inc(S["xh_done"], 1)

    scope = ExitStack()
    w0 = sb("w0", [P, 2, 3, P], F32R, scope)
    wo0 = sb("wo0", [P, P], F32, scope)
    bcol = sb("bcol", [P, 3], F32, scope)
    bo_all = sb("bo_all", [P, P], F32, scope)
    headones = sb("headones", [P, P], F32, scope)
    pbd = sb("pbd", [P, NCH * P], F32, scope)
    m32 = sb("m32", [P, KVW], F32, scope)
    m4 = sb("m4", [P, HPC], F32, scope)
    vones = sb("vones", [P, BT, NCH, KVW + 1], F32, scope)
    kvbd = sb("kvbd", [P, BATCH, NCH, KVW + HPC], F32, scope)
    setup_mem = ExitStack()
    rawU = sb("rawU", [P, E0, F0], F32, setup_mem)
    rawD = sb("rawD", [P, NF0, P], F32, setup_mem)
    rawS = sb("rawS", [E0, P], F32, setup_mem)
    rawG = sb("rawG", [P, E1], F32, setup_mem)
    rawB1 = sb("rawB1", [NF1, P], F32, setup_mem)
    rawB2 = sb("rawB2", [E1, P], F32, setup_mem)
    rawA = sb("rawA", [P, 3, P], F32, setup_mem)
    rawP = sb("rawP", [P, NCH, HD0], F32, setup_mem)
    bigP = sb("bigP", [P, NCH, H0, HD0], F32, setup_mem)
    pick32 = sb("pick32", [2 * LO_ROW, 2, P], F32, setup_mem)
    setup_mem.close()
    aT = sb("aT", [P, BLK], F32, scope)
    vT = sb("vT", [P, BLK], F32, scope)
    sq = sb("sq", [P, BLK], F32, scope)
    root = sb("root", [P, BT * H0], F32, scope)
    nrm = sb("nrm", [P, BLK], F32, scope)
    an = sb("an", [P, BLK], F32, scope)
    feat = sb("feat", [P, NCH, BLK], F32, scope)
    feat1 = sb("feat1", [P, NCH, BLK], F32, scope)
    den = sb("den", [P, BT, H0], F32, scope)
    o0 = sb("o0", [P, BT, P], F32, scope)
    o0T = sb("o0T", [P, BLK], F32, scope)
    scope.close()
    m_up = sb("m_up", [P, 2, NF1 * P], F32R)
    m_dn = sb("m_dn", [P, 2, NF1 * P], F32R)

    f_uph, f_upl = wreg[:, 0, :], wreg[:, 1, :]
    f_dnh, f_dnl = wreg[:, 2, :], wreg[:, 3, :]
    NV = H1 * DK
    f_h, f_l = (wreg[:, k, :].rearrange("p (h d) -> p h d", h=H1) for k in (2, 3))
    qkT = ed[0:DK, 0].rearrange("p t d -> p (t d)").rearrange("p (k d) -> p k d", k=4)
    form = [ed[:, 1, 2 * k:2 * k + 2, :].rearrange("p t d -> p (t d)") for k in range(2)]
    v_h, v_l, o_h, o_l = (wreg[:, k // 2, (k % 2) * NV:(k % 2 + 1) * NV] for k in range(4))

    def setup():
        XL = 4
        x_load, w_load, p_load = [sem(f"x_load{k}") for k in range(XL)], sem("w_load"), sem("p_load")
        consts, fixed, cast = sem("consts"), sem("fixed"), sem("cast")
        tr_done, tr_out, a_hi = sem("tr_done"), sem("tr_out"), sem("a_hi")
        S = {n: sem("s_" + n) for n in ("measured", "step", "xn_ready", "xT_done", "xh_done", "xl_done")}
        zeroed = sem("zeroed")
        NLOAD = 13 + P // E0
        def dealt(w):
            return w.rearrange("p (j k e) -> p j k e", j=NF0, e=E0)

        weights = ((dealt(f_uph), dealt(f_upl), rawU[:].rearrange("p e (j k) -> p j k e", j=NF0)),
                   (f_dnh, f_dnl, rawD[:].rearrange("p j d -> p (j d)")),
                   (w0[:, 0], w0[:, 1], rawA[:]))

        def rest_of(e, k):
            hi, lo, w = weights[k]
            e.wait_ge(cast, k + 1)
            e.tensor_tensor(lo, w, hi.bitcast(F32), ALU.subtract)

        with nc.Block() as block:
            @block.sync
            def _(sp):
                for k in range(XL):
                    some = blk(k, NT // XL)
                    sp.dma_start(x[:, some, :], x_in[:, some, :]).then_inc(x_load[k], 16)
                    if k == 0:
                        sp.dma_start(rawP[:], I["L0_attn_projection"].rearrange("(c h) f d -> (h f) c d", c=NCH)
                                     ).then_inc(p_load, 16)
                sp.dma_start(rawS[:], I["L0_ffn_expert_sel"]).then_inc(w_load, 16)
                sp.dma_start(rawU[:], I["L0_ffn_keys"].rearrange("e d f -> d e f")).then_inc(w_load, 16)
                values = I["L0_ffn_values"].rearrange("e (j k) d -> k e j d", j=NF0)
                for k in range(P // E0):
                    sp.dma_start(rawD[k * E0:(k + 1) * E0], values[k]).then_inc(w_load, 16)
                sp.dma_start(rawG[:], I["L1_ffn_Wg"]).then_inc(w_load, 16)
                sp.dma_start(rawB1[:], I["L1_ffn_b1"].rearrange("e (q p) -> (e q) p", p=P)).then_inc(w_load, 16)
                sp.dma_start(rawB2[:], I["L1_ffn_b2"]).then_inc(w_load, 16)
                for k, n in enumerate("qkv"):
                    sp.dma_start(rawA[:, k, :], I["L0_attn_W" + n]).then_inc(w_load, 16)
                    sp.dma_start(bcol[:, k:k + 1], I["L0_attn_b" + n].rearrange("(p a) -> p a", a=1)).then_inc(w_load, 16)
                sp.dma_start(wo0[:], I["L0_attn_Wo"]).then_inc(w_load, 16)
                sp.dma_start(bo_all[:], I["L0_attn_bo"].rearrange("(a p) -> a p", a=1).to_broadcast([P, P])).then_inc(w_load, 16)

            @block.gpsimd
            def _(pool):
                n = 0

                def then(ins):
                    nonlocal n
                    n += 1
                    ins.then_inc(fixed, 1)
                    pool.wait_ge(fixed, n)

                def select(m, pattern, base, cm, op, fill):
                    then(pool.affine_select(out=m, in_=m, compare_op=op, fill=fill, base=base,
                                            pattern=pattern, channel_multiplier=cm))

                then(pool.memset(ident[:], 0.0))
                select(ident[:], [[-1, P]], 0, 1, ALU.not_equal, 1.0)
                pool.tensor_copy(identb[:], ident[:]).then_inc(consts, 1)
                then(pool.memset(before[:], 1.0))
                select(before[:], [[1, P]], 0, -1, ALU.is_gt, 0.0)
                pool.memset(onesb[:], 1.0).then_inc(consts, 1)
                then(pool.memset(cmask[:], 0.0))
                select(cmask[:], [[-1, P]], 0, 1, ALU.is_ge, MASKED)
                pool.iota(iota[:], [[1, 32]], base=0, channel_multiplier=0,
                          allow_small_or_imprecise_dtypes=True).then_inc(consts, 1)
                pool.iota(iota8[:], [[1, E1]], base=-E1, channel_multiplier=0,
                          allow_small_or_imprecise_dtypes=True)
                pool.iota(answer[:], [[T, 2], [P, NT]], base=0, channel_multiplier=1)
                then(pool.memset(blank[:], 0.0))
                pool.memset(blank[:, P:], NOWHERE)
                pool.memset(spare_p[:], 0.0).then_inc(consts, 1)
                then(pool.memset(headones[:], 1.0))
                v = headones[:].rearrange("p (g d) -> p g d", d=HD0)
                select(v, [[-HD0, H0], [0, HD0]], 0, 1, ALU.is_ge, 0.0)
                select(v, [[HD0, H0], [0, HD0]], HD0 - 1, -1, ALU.is_ge, 0.0)
                then(pool.memset(m32[:], 1.0))
                v = m32[:].rearrange("p (g d) -> p g d", d=HD0)
                select(v, [[-FEAT0, HPC], [0, HD0]], 0, 1, ALU.is_ge, 0.0)
                select(v, [[FEAT0, HPC], [0, HD0]], FEAT0 - 1, -1, ALU.is_ge, 0.0)
                then(pool.memset(m4[:], 1.0))
                select(m4[:], [[-FEAT0, HPC]], 0, 1, ALU.is_ge, 0.0)
                select(m4[:], [[FEAT0, HPC]], FEAT0 - 1, -1, ALU.is_ge, 0.0)
                then(pool.memset(pick32[:], 0.0))
                for base in (0, -LO_ROW):
                    select(pick32[:, 0, :], [[0, P // E0], [-1, E0]], base, 1, ALU.not_equal, 1.0)
                    select(pick32[:, 1, :], [[-1, H1], [0, P // H1]], base, 1, ALU.not_equal, 1.0)
                pool.tensor_copy(iota[0:1, 0:1], iota[0:1, 0:1]).then_inc(consts, 1)
                pool.memset(gT[:].bitcast(F32), 0.0)
                pool.memset(vones[:], 1.0).then_inc(consts, 1)
                pool.wait_ge(p_load, 16)
                for c in range(NCH):
                    then(pool.tensor_copy(bigP[:, c], rawP[:, c:c + 1, :].to_broadcast([P, H0, HD0])))
                    select(bigP[:, c], [[-FEAT0, H0], [0, HD0]], FEAT0 * HPC * c, 1, ALU.is_ge, 0.0)
                    select(bigP[:, c], [[FEAT0, H0], [0, HD0]], FEAT0 - 1 - FEAT0 * HPC * c, -1, ALU.is_ge, 0.0)
                pool.tensor_copy(iota[0:1, 0:1], iota[0:1, 0:1]).then_inc(consts, 1)
                for k in (0, 2):
                    rest_of(pool, k)

            @block.tensor
            def _(pe):
                pe.wait_ge(consts, 1)
                split_pe(pe, S)
                pe.wait_ge(w_load, 16 * NLOAD)
                pe.wait_ge(consts, 7)
                pe.transpose(bank(2)[:, 0:E0], rawS[:], ident[0:E0, 0:E0]).then_inc(tr_done, 1)
                pe.transpose(bank(3)[:, 0:NF1], rawB1[:], ident[0:NF1, 0:NF1]).then_inc(tr_done, 1)
                pe.transpose(bank(3)[:, NF1:NF1 + E1], rawB2[:], ident[0:E1, 0:E1]).then_inc(tr_done, 1)
                for c in range(NCH):
                    last = pe.transpose(tiles(4)[:, c, :], bigP[:, c].rearrange("p h d -> p (h d)"), ident[:])
                last.then_inc(tr_done, 1)

            @block.scalar
            def _(act):
                act.wait_ge(consts, 5)
                act.activation(pick[:], pick32[:], ACT.Copy)
                for i in range(NB):
                    split_act(act, S, i)
                    if 1 <= i <= len(weights):
                        act.wait_ge(w_load, 16 * NLOAD)
                        hi, lo, w = weights[i - 1]
                        act.activation(hi, w, ACT.Copy).then_inc(cast, 1)
                act.wait_ge(tr_done, 4)
                act.wait_ge(S["xl_done"], 1)
                act.activation(selw[:, 0], bank(2)[:, 0:E0], ACT.Copy).then_inc(a_hi, 1)
                act.activation(wgw[:, 0], rawG[:], ACT.Copy).then_inc(a_hi, 1)
                act.activation(b1c[:], bank(3)[:, 0:NF1], ACT.Copy).then_inc(tr_out, 1)
                act.activation(b2c[:], bank(3)[:, NF1:NF1 + E1], ACT.Copy).then_inc(tr_out, 1)
                act.activation(pbd[:], bank(4), ACT.Copy).then_inc(tr_out, 1)

            @block.vector
            def _(dve):
                n = 0

                def then(ins):
                    nonlocal n
                    n += 1
                    ins.then_inc(S["step"], 1)
                    dve.wait_ge(S["step"], n)

                dve.memset(routers[:].bitcast(F32), 0.0)
                dve.memset(spare_v[:], 0.0)
                dve.memset(kvbd[:], 0.0).then_inc(zeroed, 1)
                dve.wait_ge(zeroed, 1)
                for i in range(NB):
                    dve.wait_ge(x_load[i * XL // NB], 16)
                    measure(dve, i, S["measured"])
                    if i >= 1:
                        gather(dve, i - 1, S["measured"])
                then(gather(dve, NB - 1, S["measured"]))
                deviations(dve, then)
                split_dve(dve, S)
                rest_of(dve, 1)
                dve.wait_ge(a_hi, 2)
                dve.tensor_tensor(selw[:, 1], bank(2)[:, 0:E0], selw[:, 0].bitcast(F32), ALU.subtract)
                dve.tensor_tensor(wgw[:, 1], rawG[:], wgw[:, 0].bitcast(F32), ALU.subtract)

    top8 = sb("top8", [P, BT, 8], F32)
    GW = E0 + 8 - TOP0
    FILL = -1.0

    def product3(pe, dst, wh, wl, i, start=True, stop=True):
        pe.matmul(dst, wh, xl[:, blk(i)], start=start, stop=False)
        pe.matmul(dst, wl, xh[:, blk(i)], start=False, stop=False)
        return pe.matmul(dst, wh, xh[:, blk(i)], start=False, stop=stop)

    def wait_past(e, semaphore, count):
        if not isinstance(count, int) or count > 0:
            e.wait_ge(semaphore, count)

    def route_ffn(ph, load_moe):
        names = ("filled", "logit_done", "gate_in", "e_turned", "tok_in", "max_done", "top_set", "rest_set", "gate_set",
                 "gT_ps", "gT_hi", "gT_lo")
        S = {n: sem(f"{ph}_{n}") for n in names}
        gE = [ed[:, a].rearrange("p t d -> p (t d)") for a in range(2)]
        gtok, gsel = ([r[:, a, k:k + BT * w].rearrange("p (t e) -> p t e", t=BT) for a in range(2)]
                      for k, w in ((0, GW), (BLK // 2, E0)))
        rest = [hg[:, a, 0:BT * GW].rearrange("p (t e) -> p t e", t=BT) for a in range(2)]
        B_L, B_T, B_G = (0, 1), (2, 3), (4, 5)
        RAW = 4
        if load_moe:
            m_load, m_cast, m_split = [sem(f"m_load{k}") for k in range(E1)], sem("m_cast"), sem("m_split")

        def raw_pair(slot):
            both = raw_all[:, bass.ds(slot, 1), :].rearrange("p a n -> p (a n)")
            return both[:, 0:BLK], both[:, BLK:]

        def pipeline(step):
            for i in range(NB + 2):
                step(i, i % 2)

        def there(i):
            return 0 <= i < NB

        with nc.Block() as block:
            @block.tensor
            def _(pe):
                def step(i, a):
                    if there(i):
                        wait_past(pe, S["gate_in"], i - 1)
                        product3(pe, bank(B_L[a]), routers[:, 0], routers[:, 1], i).then_inc(S["logit_done"], 1)
                    if there(i - 1):
                        pe.wait_ge(S["gate_in"], i)
                        wait_past(pe, S["tok_in"], i - 2)
                        for t in range(BT):
                            last = pe.transpose(tiles(B_T[1 - a])[:, t, :], gE[1 - a][:, t * P:(t + 1) * P], ident[:])
                        last.then_inc(S["e_turned"], 1)
                    if there(i - 2):
                        pe.wait_ge(S["gate_set"], i - 1)
                        wait_past(pe, S["gT_lo"], i - 3)
                        for t in range(BT):
                            last = pe.transpose(bank(B_G[a])[0:E0, t * P:(t + 1) * P], gsel[a][:, t, :], ident[:])
                        last.then_inc(S["gT_ps"], 1)

                pipeline(step)

            @block.scalar
            def _(act):
                def step(i, a):
                    if there(i):
                        act.wait_ge(S["logit_done"], i + 1)
                        wait_past(act, S["e_turned"], i - 1)
                        act.activation(gE[a], bank(B_L[a]), ACT.Sigmoid).then_inc(S["gate_in"], 1)
                        if load_moe:
                            act.wait_ge(m_load[i], 32)
                            for w, raw_one in zip((m_up, m_dn), raw_pair(i % RAW)):
                                last = act.activation(w[:, 0, blk(i)], raw_one, ACT.Copy)
                            last.then_inc(m_cast, 1)
                    if there(i - 2):
                        act.wait_ge(S["gT_ps"], i - 1)
                        act.activation(gT[0:E0, blk(i - 2)], bank(B_G[a])[0:E0, :], ACT.Copy).then_inc(S["gT_hi"], 1)

                pipeline(step)

            @block.vector
            def _(dve):
                def choose(k, a):
                    dve.wait_ge(S["e_turned"], k + 1)
                    dve.tensor_copy(gtok[a][:, :, 0:E0], tiles(B_T[a])[:, :, 0:E0]).then_inc(S["tok_in"], 1)
                    dve.wait_ge(S["tok_in"], k + 1)
                    apart(dve, spare_v)
                    for t in range(BT):
                        last = dve.max(top8[:, t, :], gtok[a][:, t, 0:E0])
                    last.then_inc(S["max_done"], 1)
                    dve.wait_ge(S["max_done"], k + 1)
                    dve.memset(top8[:, :, TOP0:], FILL).then_inc(S["top_set"], 1)
                    dve.wait_ge(S["top_set"], k + 1)
                    apart(dve, spare_v)
                    for t in range(BT):
                        last = dve.match_replace(rest[a][:, t, :], top8[:, t, :], gtok[a][:, t, :], 0.0)
                    last.then_inc(S["rest_set"], 1)
                    dve.wait_ge(S["rest_set"], k + 1)
                    wait_past(dve, S["gT_ps"], k - 1)
                    dve.tensor_tensor(gsel[a], gtok[a][:, :, 0:E0], rest[a][:, :, 0:E0], ALU.subtract
                                      ).then_inc(S["gate_set"], 1)
                    dve.wait_ge(S["gate_set"], k + 1)
                    if there(k - 1):
                        low(k - 1, 1 - a)

                def low(k, a):
                    dve.wait_ge(S["gT_hi"], k + 1)
                    dve.tensor_tensor(gT[LO_ROW:LO_ROW + E0, blk(k)], bank(B_G[a])[0:E0, :],
                                      gT[0:E0, blk(k)].bitcast(F32), ALU.subtract).then_inc(S["gT_lo"], 1)

                def step(i, a):
                    if there(i - 1):
                        choose(i - 1, 1 - a)
                    elif there(i - 2):
                        low(i - 2, a)

                for a in range(2):
                    last = dve.memset(gtok[a][:, :, E0:], FILL)
                last.then_inc(S["filled"], 1)
                dve.wait_ge(S["filled"], 1)
                pipeline(step)

            if load_moe:
                W1 = I["L1_ffn_W1"].rearrange("e d f -> d e f")
                W2 = I["L1_ffn_W2"].rearrange("e (q p) d -> p (e q) d", p=P)

                @block.sync
                def _(sp):
                    def load(e, slot, loaded):
                        w1, w2 = raw_pair(slot)
                        sp.dma_start(w1, W1[:, bass.ds(e, 1), :].rearrange("d a f -> d (a f)")).then_inc(loaded, 16)
                        sp.dma_start(w2.rearrange("p (q d) -> p q d", q=BT), W2[:, blk(e, BT), :]).then_inc(loaded, 16)

                    for e in range(E1):
                        wait_past(sp, m_split, e - RAW + 1)
                        load(e, e % RAW, m_load[e])

                @block.gpsimd
                def _(pool):
                    def rest_of(e, slot):
                        pool.wait_ge(m_cast, e + 1)
                        for w, raw_one in zip((m_up, m_dn), raw_pair(slot)):
                            last = pool.tensor_tensor(w[:, 1, blk(e)], raw_one, w[:, 0, blk(e)].bitcast(F32), ALU.subtract)
                        last.then_inc(m_split, 1)

                    with pool.Fori(0, RAW) as k:
                        rest_of(k, k)
                    with pool.Fori(0, E1 - RAW) as k:
                        rest_of(RAW + k, k)

    m16 = sb("m16", [P, 2 * E1, NT], BF16)
    lg, eq, rest = (sb(n, [P, BT, E1], F32) for n in ("lg", "eq", "rest"))
    most, top_at = sb("most", [P, BT], F32), sb("top_at", [P, BT], F32)
    run, place = sb("run", [P, (E1 + 1) * 2 * BT], F32), sb("place", [P, E1, 2 * BT], F32)
    taken, shift = sb("taken", [P, E1], F32), sb("shift", [P, E1], F32)
    row_sum, row_no = sb("row_sum", [P, 2, BT], F32), sb("row_no", [P, 2, BT], I32)
    tokens_of = sb("tokens_of", [P, E1], I32)
    row_at = sb("row_at", [P, SPARSE + 2], I32)
    CHOOSE, COUNT_AT = 21, 13
    N = NT * E1
    G, A = (hg[:, 0, k * N:(k + 1) * N].rearrange("p (t e) -> p t e", t=NT) for k in range(2))
    flat = gate[:].rearrange("p t e -> p (t e)")
    turned = flat[:, 0:BLK]
    L = flat[:, 3 * N:4 * N].rearrange("p (t e) -> p t e", t=NT)
    before_all, upto, pos = flat[:, 0:1], flat[:, 1:1 + 2 * N], flat[:, 0:2 * N]
    pos2 = pos.rearrange("p (e t) -> p e t", t=NT)
    base = pos2[:, :, 0]
    ends = flat[:, 0:(2 * E1 + 1) * NT].rearrange("p (e t) -> p e t", t=NT)[:, :, 0]
    adj, both, last_of, shifted, found, first_of, sums, s1, s2 = (
        r[:, 1, a:a + w] for a, w in ((0, 2 * E1), (16, 2 * E1), (32, E1), (64, 32), (96, 32), (128, 32), (160, 2 * NT),
                                      (224, NT), (256, NT)))
    sums = sums.rearrange("p (c t) -> p c t", c=2)
    tmp = hg[:, 1, :].rearrange("p (c e t) -> p c e t", c=2, e=E1)
    pos4 = pos2.rearrange("p (c e) t -> p c e t", c=2)

    def choose_step(dve, i, k, S, counts, first):
        step, four = S["rstep"], blk(i, BT)
        if k > 0 or not first:
            dve.wait_ge(step, CHOOSE * i + k)
        if k == 0:
            dve.wait_ge(S["lg_turned"], i + 1)
        if k == COUNT_AT:
            dve.wait_ge(S["counted"], i + 1)

        def wide(v):
            return v[:].unsqueeze(2).to_broadcast([P, BT, E1])

        back8 = iota8[:].unsqueeze(1).to_broadcast([P, BT, E1])
        m1, m2 = (m16[:, c * E1:(c + 1) * E1, four].rearrange("p e t -> p t e") for c in range(2))
        before_e, behind_e = (run[:].rearrange("p (e k) -> p e k", e=E1 + 1)[:, a:a + E1, 0] for a in range(2))
        if k == 0:
            last = dve.tensor_copy(lg[:], counts.rearrange("p (t d) -> p t d", t=BT)[:, :, E0:E0 + E1])
        elif k == 1:
            last = dve.tensor_scalar(L[:, four, :], lg[:], 0.0, None, ALU.add)
        elif k in (2, 8):
            last = dve.tensor_reduce(most[:], (lg if k == 2 else rest)[:], AX.X, ALU.max)
        elif k in (3, 9):
            last = dve.tensor_tensor(eq[:], (lg if k == 3 else rest)[:], wide(most), ALU.is_equal)
        elif k in (4, 10):
            last = dve.tensor_tensor(eq[:], eq[:], back8, ALU.mult)
        elif k in (5, 11):
            last = dve.tensor_reduce(top_at[:], eq[:], AX.X, ALU.min)
        elif k in (6, 12):
            last = dve.tensor_tensor(m1 if k == 6 else m2, back8, wide(top_at), ALU.is_equal)
        elif k == 7:
            last = dve.scalar_tensor_tensor(rest[:], m1, -3e38, lg[:], ALU.mult, ALU.add)
        elif k == 13:
            last = dve.tensor_tensor_scan(run[:, 1:1 + 2 * E1 * BT], onesb[:, 0:1].to_broadcast([P, 2 * E1 * BT]),
                                          counts[:, 2 * E1 * BT:4 * E1 * BT], 0.0, ALU.mult, ALU.add)
        elif k == 14:
            last = dve.tensor_tensor(shift[:], taken[:], before_e, ALU.subtract)
        elif k == 15:
            last = dve.tensor_tensor(place[:].rearrange("p e k -> p (e k)"), run[:, 0:2 * E1 * BT], counts[:, 0:2 * E1 * BT],
                                     ALU.add)
        elif k == 16:
            last = dve.tensor_tensor(place[:], place[:], shift[:].unsqueeze(2).to_broadcast([P, E1, 2 * BT]), ALU.add)
        elif k == 17:
            v = place[:].rearrange("p e (c t) -> p e c t", c=2)
            last = dve.tensor_tensor(v, v, m16[:, :, four].rearrange("p (c e) t -> p e c t", c=2), ALU.mult)
        elif k == 18:
            last = dve.tensor_reduce(row_sum[:], place[:].rearrange("p e (c t) -> p c t e", c=2), AX.X, ALU.add)
        elif k == 19:
            last = dve.tensor_copy(row_no[:], row_sum[:])
        else:
            last = dve.tensor_tensor(taken[:], shift[:], behind_e, ALU.add)
        last.then_inc(step, 1)

    def fill_row(dve, i, t, S, sent, first):
        if t == 0:
            dve.wait_ge(S["xn_ready"], i + 1)
            dve.wait_ge(S["rstep"], CHOOSE * i + CHOOSE)
        if not first:
            dve.wait_ge(sent[t], 32 * i)
        one = bass.ds(i * BT + t, 1)
        xn2 = x[:, one, :].to_broadcast([P, 2, P])
        dve.tensor_scalar(row[:, t, :, 0:P], xn2, kept_mean[:, one], kept_rs[:, one], ALU.subtract, ALU.mult)
        dve.tensor_copy(row[:, t, :, P:].bitcast(I32), answer[:, :, one])
        dve.tensor_copy(row_to[:, t, :], row_no[:, :, t]).then_inc(S["row_ready"], 1)

    def send_row(pool, i, t, S, sent, first):
        if not (first and t == 0):
            pool.wait_ge(S["spaced"], i * BT + t)
        pool.wait_ge(S["row_ready"], i * BT + t + 1)
        apart(pool, spare_p).then_inc(S["spaced"], 1)
        for c in range(2):
            pool.indirect_dma_start(rows, bass.IndirectOffsetOnAxis(ap=row_to[:, t, c:c + 1], axis=0), row[:, t, c, :],
                                    None).then_inc(sent[t], 16)

    def count_all(pe, S):
        pe.wait_ge(S["rstep"], CHOOSE * NB)
        for k, m in ((2, before), (3, onesb)):
            pe.matmul(bank(k), m[:], m16[:].rearrange("p e t -> p (e t)"), start=True, stop=True).then_inc(S["all_counted"], 1)

    def weights_and_experts(dve, S):
        n = 0

        def then(ins):
            nonlocal n
            n += 1
            ins.then_inc(S["end_step"], 1)
            dve.wait_ge(S["end_step"], n)

        def wide(v):
            return v.unsqueeze(2).to_broadcast([P, NT, E1])

        M1, M2 = (m16[:, k * E1:(k + 1) * E1, :].rearrange("p e t -> p t e") for k in range(2))
        dve.wait_ge(S["rstep"], CHOOSE * NB)
        then(dve.tensor_reduce(s1, L, AX.X, ALU.max))
        then(dve.tensor_tensor(A, L, wide(s1), ALU.subtract))
        dve.memset(before_all, 0.0)
        dve.wait_ge(S["all_counted"], 2)
        then(dve.tensor_tensor_scan(upto, onesb[:, 0:1].to_broadcast([P, NT * 2 * E1]), bank(3), 0.0, ALU.mult, ALU.add))
        then(dve.tensor_tensor(both, ends[:, 1:], ends[:, 0:2 * E1], ALU.subtract))
        then(dve.tensor_scalar(adj[:, 0:E1], base[:, 0:E1], -1.0, None, ALU.mult))
        then(dve.tensor_tensor(adj[:, E1:], both[:, 0:E1], base[:, E1:], ALU.subtract))
        then(dve.tensor_tensor(both[:, 0:E1], both[:, 0:E1], both[:, E1:], ALU.add))
        dve.tensor_copy(tokens_of[:], both[:, 0:E1]).then_inc(S["n_set"], 1)
        then(dve.tensor_tensor(pos, pos, bank(2), ALU.add))
        then(dve.tensor_tensor(pos2, pos2, adj[:].unsqueeze(2).to_broadcast([P, 2 * E1, NT]), ALU.add))
        dve.wait_ge(S["exp_done"], 1)
        then(dve.tensor_reduce(s1, G, AX.X, ALU.add))
        then(dve.reciprocal(s2, s1))
        then(dve.tensor_tensor(G, G, wide(s2), ALU.mult))
        then(dve.tensor_tensor(A, M1, M2, ALU.add))
        then(dve.tensor_tensor(A, A, G, ALU.mult))
        then(dve.tensor_reduce(s1, A, AX.X, ALU.add))
        then(dve.tensor_scalar(s1, s1, GATE_EPS, None, ALU.add))
        then(dve.reciprocal(s2, s1))
        then(dve.tensor_tensor(G, G, wide(s2), ALU.mult))
        then(dve.scalar_tensor_tensor(pos, pos, float(CAP), m16[:].rearrange("p e t -> p (e t)"), ALU.is_lt, ALU.mult))
        for c in range(2):
            then(dve.tensor_tensor(tmp[:, c], pos4[:, c], G.rearrange("p t e -> p e t"), ALU.mult))
        then(dve.tensor_reduce(sums, tmp.rearrange("p c e t -> p c t e"), AX.X, ALU.add))
        then(dve.tensor_scalar(weight2[:], sums, 0.5, None, ALU.mult))
        then(dve.tensor_scalar(whole[:], both[:, 0:E1], float(BLK - 1), None, ALU.add))
        then(dve.tensor_scalar(whole[:], whole[:], BLK.bit_length() - 1, None, ALU.logical_shift_right))
        then(dve.tensor_copy(both[:, E1:], whole[:]))
        then(dve.tensor_tensor_scan(last_of, onesb[:, 0:1].to_broadcast([P, E1]), both[:, E1:], 0.0, ALU.mult, ALU.add))
        near = hg[:, 1, 0:32 * E1].rearrange("p (b e) -> p b e", e=E1)
        then(dve.tensor_scalar(shifted, iota[:], -1.0, None, ALU.add))
        then(dve.tensor_tensor(near, shifted.unsqueeze(2).to_broadcast([P, 32, E1]),
                               last_of.unsqueeze(1).to_broadcast([P, 32, E1]), ALU.is_ge))
        then(dve.tensor_reduce(found, near, AX.X, ALU.add))
        then(dve.tensor_tensor(near, near, both[:, E1:].unsqueeze(1).to_broadcast([P, 32, E1]), ALU.mult))
        then(dve.tensor_reduce(first_of, near, AX.X, ALU.add))
        then(dve.tensor_tensor(first_of, shifted, first_of, ALU.subtract))
        then(dve.tensor_scalar(first_of, first_of, float(BLK), None, ALU.mult))
        then(dve.scalar_tensor_tensor(first_of, found, float(E1), first_of, ALU.is_lt, ALU.mult))
        then(dve.scalar_tensor_tensor(first_of, found, float(REGION), first_of, ALU.mult, ALU.add))
        then(dve.tensor_scalar(found, found, float(E1 - 1), None, ALU.min))
        dve.tensor_copy(row_at[:], first_of[:, 0:SPARSE + 2])
        dve.tensor_copy(expert_of[:], found[:, 0:SPARSE + 2])

    def blank_rows(sp, S):
        sp.wait_ge(S["n_set"], 1)
        for e in range(E1 + 1):
            n = sp.value_load(tokens_of[0:1, e:e + 1], min_val=0, max_val=T) if e < E1 else 0
            sp.dma_start(rows[bass.ds(n + e * REGION, BLK), :].rearrange("(t p) w -> p t w", p=P),
                         blank[:].unsqueeze(1).to_broadcast([P, BT, ROW])).then_inc(S["blanked"], 16)
        sp.wait_ge(S["blanked"], 16 * (E1 + 1))

    PAIRS = H1 // 2
    B_TURN, B_FORM, B_O = 0, 1, (4, 7)

    def heads_sems():
        return {n: sem("heads_" + n) for n in ("q_load", "k_load", "v_load", "o_load", "qk_turned", "qkT_ready", "f_done", "f_out",
                                               "f_hi", "f_lo", "v_cast", "v_split", "o_dealt", "o_turned", "o_hi", "o_lo")}

    def heads_load(sp, H):
        for w, n in ((raw_q, "q"), (raw_k, "k"), (raw_v, "v"), (raw_o, "o")):
            sp.dma_start(w.rearrange("p (h v) -> p h v", h=H1),
                         I["L1_attn_P_" + n].rearrange("h d v -> d h v")).then_inc(H[n + "_load"], 16)

    def heads_pe(pe, H):
        pe.wait_ge(H["q_load"], 16)
        pe.wait_ge(H["k_load"], 16)
        for g in range(PAIRS):
            for a in range(2):
                for k, w in enumerate((raw_q, raw_k)):
                    last = pe.transpose(bank(B_TURN)[0:DK, (2 * a + k) * P:(2 * a + k + 1) * P],
                                        w[:, (2 * g + a) * DK:(2 * g + a + 1) * DK], ident[:])
            last.then_inc(H["qk_turned"], 1)
            pe.wait_ge(H["qkT_ready"], g + 1)
            for a in range(2):
                last = pe.matmul(bank(B_FORM)[:, a * P:(a + 1) * P], qkT[:, 2 * a, :], qkT[:, 2 * a + 1, :],
                                 start=True, stop=True)
            last.then_inc(H["f_done"], 1)
        pe.wait_ge(H["o_dealt"], 1)
        for k in range(2):
            for q in range(BT):
                last = pe.transpose(tiles(B_O[k])[:, q, :], raw_v[:, (k * BT + q) * P:(k * BT + q + 1) * P], ident[:])
            last.then_inc(H["o_turned"], 1)

    def heads_act(act, H):
        for g in range(PAIRS):
            act.wait_ge(H["qk_turned"], g + 1)
            act.activation(qkT, bank(B_TURN)[0:DK, :].rearrange("p (k d) -> p k d", k=4), ACT.Copy).then_inc(H["qkT_ready"], 1)
            act.wait_ge(H["f_done"], g + 1)
            if g >= 2:
                act.wait_ge(H["f_lo"], g - 1)
            act.activation(form[g % 2], bank(B_FORM)[:, 0:2 * P], ACT.Copy, scale=LOGIT_SCALE).then_inc(H["f_out"], 1)
        act.wait_ge(H["o_load"], 16)
        act.wait_ge(H["v_split"], 1)
        act.activation(raw_v.rearrange("p (j h k) -> p j h k", j=NF2, h=H1),
                       raw_o.rearrange("p (h j k) -> p j h k", h=H1, j=NF2), ACT.Copy).then_inc(H["o_dealt"], 1)
        for k in range(2):
            act.wait_ge(H["o_turned"], k + 1)
            act.activation(o_h[:, k * BLK:(k + 1) * BLK], bank(B_O[k]), ACT.Copy).then_inc(H["o_hi"], 1)

    def heads_dve(dve, H):
        dve.wait_ge(H["v_load"], 16)
        v_in = raw_v.rearrange("p (h j k) -> p j h k", h=H1, j=NF2)
        v_hi, v_lo = (w.rearrange("p (j h k) -> p j h k", j=NF2, h=H1) for w in (v_h, v_l))
        dve.tensor_copy(v_hi, v_in).then_inc(H["v_cast"], 1)
        dve.wait_ge(H["v_cast"], 1)
        dve.tensor_tensor(v_lo, v_in, v_hi.bitcast(F32), ALU.subtract).then_inc(H["v_split"], 1)
        for g in range(PAIRS):
            two = slice(g * 2 * P, (g + 1) * 2 * P)
            dve.wait_ge(H["f_out"], g + 1)
            dve.tensor_copy(wreg[:, 2, two], form[g % 2]).then_inc(H["f_hi"], 1)
            dve.wait_ge(H["f_hi"], g + 1)
            dve.tensor_tensor(wreg[:, 3, two], form[g % 2], wreg[:, 2, two].bitcast(F32), ALU.subtract).then_inc(H["f_lo"], 1)
        for k in range(2):
            dve.wait_ge(H["o_hi"], k + 1)
            dve.tensor_tensor(o_l[:, k * BLK:(k + 1) * BLK], bank(B_O[k]), o_h[:, k * BLK:(k + 1) * BLK].bitcast(F32),
                              ALU.subtract).then_inc(H["o_lo"], 1)

    def gated(ph, nf, up, dn, picked, func, scale, route=False, load_heads=False):
        names = ["up_done", "g_done", "act_done", "hg_done", "hi_done", "lo_dve", "lo_pool", "dn_done", "oT_ready",
                 "back_done", "added", "xn_ready", "xT_done", "xh_done", "xl_done", "step"]
        if route:
            names += ["r_init", "logit_done", "lg_ready", "lg_turned", "rstep", "counted", "row_ready", "spaced",
                      "all_counted", "end_step", "exp_done", "n_set", "blanked"]
        S = {n: sem(f"{ph}_{n}") for n in names}
        sent = [sem(f"{ph}_sent{t}") for t in range(BT)] if route else []
        H = heads_sems() if load_heads else None
        B_UP, B_G, B_OUT, B_BACK, B_XT, B_R = (0, 1), (2, 3), (4, 7), 5, 5 if route else 6, 6
        RATE = 2 if nf == NF0 else 5
        FREE = nf // BT - 2
        APART = nf // BT
        AT_EVAC, AT_BACK, AT_ADD = nf + LAG, nf + LAG + 3, nf + LAG + 4
        AT_LN = AT_ADD + 1
        AT_XT = AT_LN + (LN_STEPS + RATE - 1) // RATE + (nf == NF0)
        AT_HIGH, AT_LOW = AT_XT + 1, AT_XT + 2
        AT_LOGIT, AT_LCOPY, AT_LTURN = AT_LOW + 1, AT_LOW + 1, AT_LOW + 2
        AT_CHOOSE = AT_LN + nf
        AT_COUNT = AT_CHOOSE + (COUNT_AT + RATE - 1) // RATE
        AT_PLACE = AT_COUNT + 1
        AT_FILL = AT_PLACE + (CHOOSE - COUNT_AT + RATE - 1) // RATE
        AT_FILL += (FREE - 1 - AT_FILL) % APART
        AT_SEND = AT_FILL + 1
        PEEL = 1 + (AT_SEND + (BT - 1) * APART if route else AT_LOW) // nf

        def tail_blocks(i, at, j, place):
            back_by = place // nf
            past = isinstance(i, int) and i - back_by >= NB
            return [(i - back_by, at == back_by)] if j == place % nf and at >= back_by and not past else []

        def all_blocks(e, one_block):
            for i in range(PEEL):
                one_block(i, i, i % 2)
            with e.Fori(0, (NB - PEEL) // 2) as g:
                for a in range(2):
                    one_block(2 * g + PEEL + a, PEEL, (PEEL + a) % 2)
            for i in range(NB - (NB - PEEL) % 2, NB + PEEL):
                one_block(i, PEEL, i % 2, i < NB)

        def col(w, j):
            return w[:, j * P:(j + 1) * P]

        def by_dve(j):
            return j % APART == FREE if route else j % 4 == 2

        N_DVE = sum(by_dve(j) for j in range(nf))

        def lows(i, j):
            d = sum(by_dve(k) for k in range(j))
            return i * N_DVE + d, i * (nf - N_DVE) + j - d

        def wait_low(e, i, j):
            if by_dve(j):
                e.wait_ge(S["lo_dve"], lows(i, j)[0] + 1)
            else:
                e.wait_ge(S["lo_pool"], lows(i, j)[1] + 1)

        with nc.Block() as block:
            @block.tensor
            def _(pe):
                def up_product(i, j, at, odd):
                    n = i * nf + j
                    if at >= 1 or j >= 2:
                        pe.wait_ge(S["act_done"], n - 1)
                    product3(pe, bank(B_UP[j % 2]), col(up[0], j), col(up[1], j), i).then_inc(S["up_done"], 1)
                    if j == 0:
                        if at >= 2:
                            pe.wait_ge(S["hg_done"], n - nf)
                        pe.matmul(bank(B_G[odd]), pick[:, picked, :], gT[:, blk(i)], start=True,
                                  stop=True).then_inc(S["g_done"], 1)

                def down_product(i, j, at, odd):
                    n = i * nf + j
                    s = j % SLOTS
                    dst = bank(B_OUT[odd])
                    if j == 0 and at >= 2:
                        pe.wait_ge(S["oT_ready"], i - 1)
                    wait_low(pe, i, j)
                    pe.matmul(dst, col(dn[1], j), hh[:, s, :], start=(j == 0), stop=False)
                    pe.matmul(dst, col(dn[0], j), hl[:, s, :], start=False, stop=False)
                    last = pe.matmul(dst, col(dn[0], j), hh[:, s, :], start=False,
                                     stop=(j == nf - 1))
                    last.then_inc(S["dn_done"], 1)

                def back(i, first):
                    pe.wait_ge(S["oT_ready"], i + 1)
                    if not first:
                        pe.wait_ge(S["xl_done" if route else "added"], i)
                    for t in range(BT):
                        last = pe.transpose(tiles(B_BACK)[:, t, :], oT[:, t * P:(t + 1) * P], ident[:])
                    last.then_inc(S["back_done"], 1)

                def next_xT(i, first):
                    pe.wait_ge(S["xn_ready"], i + 1)
                    if not first:
                        pe.wait_ge(S["xl_done"], i)
                    for t in range(BT):
                        last = pe.transpose(tiles(B_XT)[:, t, :], xn[:, t, :], ident[:])
                    last.then_inc(S["xT_done"], 1)

                def logits_of(i, first):
                    pe.wait_ge(S["xl_done"], i + 1)
                    if not first:
                        pe.wait_ge(S["rstep"], CHOOSE * (i - 1) + CHOOSE - 5)
                    product3(pe, bank(B_R), routers[:, 0], routers[:, 1], i).then_inc(S["logit_done"], 1)

                def turn_logits(i):
                    pe.wait_ge(S["lg_ready"], i + 1)
                    for t in range(BT):
                        last = pe.transpose(tiles(B_R)[:, t, :], turned[:, t * P:(t + 1) * P], ident[:])
                    last.then_inc(S["lg_turned"], 1)

                def count(i):
                    pe.wait_ge(S["rstep"], CHOOSE * i + COUNT_AT)
                    chosen = m16[:, :, blk(i, BT)].rearrange("p (c e) t -> p e c t", c=2)
                    w = 2 * E1 * BT
                    for k, m in enumerate((before, onesb)):
                        last = pe.matmul(bank(B_R)[:, k * w:(k + 1) * w], m[:], chosen, start=True, stop=True)
                    last.then_inc(S["counted"], 1)

                def one_block(i, at, odd, live=True):
                    for j in range(nf):
                        if live:
                            up_product(i, j, at, odd)
                        if j < LAG and at >= 1 and (live or i == NB):
                            down_product(i - 1, j - LAG + nf, at - 1, 1 - odd)
                        if j >= LAG and live:
                            down_product(i, j - LAG, at, odd)
                        for k, first in tail_blocks(i, at, j, AT_BACK):
                            back(k, first)
                        for k, first in tail_blocks(i, at, j, AT_XT):
                            next_xT(k, first)
                        if route:
                            for k, first in tail_blocks(i, at, j, AT_LOGIT):
                                logits_of(k, first)
                            for k, first in tail_blocks(i, at, j, AT_LTURN):
                                turn_logits(k)
                            for k, first in tail_blocks(i, at, j, AT_COUNT):
                                count(k)

                all_blocks(pe, one_block)
                if route:
                    pe.wait_ge(S["hg_done"], NB * nf)
                    count_all(pe, S)
                if load_heads:
                    pe.wait_ge(S["act_done"], NB * nf)
                    heads_pe(pe, H)

            @block.scalar
            def _(act):
                def activate(i, j, first):
                    n = i * nf + j
                    act.wait_ge(S["up_done"], n + 1)
                    if not first or j >= 2:
                        act.wait_ge(S["hg_done"], n - 1)
                    act.activation(r[:, j % 2, :], bank(B_UP[j % 2]), func).then_inc(S["act_done"], 1)

                def high(i, j, first):
                    n = i * nf + j
                    act.wait_ge(S["hg_done"], n + 1)
                    if not first or j >= SLOTS:
                        act.wait_ge(S["dn_done"], n - SLOTS + 1)
                    act.activation(hh[:, j % SLOTS, :], hg[:, j % 2, :], ACT.Copy).then_inc(S["hi_done"], 1)

                def evacuate(i, odd, first):
                    act.wait_ge(S["dn_done"], nf * i + nf)
                    if not first:
                        act.wait_ge(S["back_done"], i)
                    act.activation(oT, bank(B_OUT[odd]), ACT.Copy, scale=scale).then_inc(S["oT_ready"], 1)

                def next_high(i):
                    act.wait_ge(S["xT_done"], i + 1)
                    act.activation(xh[:, blk(i)], bank(B_XT), ACT.Copy).then_inc(S["xh_done"], 1)

                def logits_out(i, first):
                    act.wait_ge(S["logit_done"], i + 1)
                    if not first:
                        act.wait_ge(S["lg_turned"], i)
                    act.activation(turned, bank(B_R), ACT.Copy).then_inc(S["lg_ready"], 1)

                def one_block(i, at, odd, live=True):
                    for j in range(nf):
                        if live:
                            activate(i, j, at == 0)
                        if j == 0 and at >= 1 and (live or i == NB):
                            high(i - 1, nf - 1, at == 1)
                        if j >= 1 and live:
                            high(i, j - 1, at == 0)
                        for k, first in tail_blocks(i, at, j, AT_EVAC):
                            evacuate(k, 1 - odd, first)
                        for k, first in tail_blocks(i, at, j, AT_HIGH):
                            next_high(k)
                        if route:
                            for k, first in tail_blocks(i, at, j, AT_LCOPY):
                                logits_out(k, first)

                all_blocks(act, one_block)
                if route:
                    act.wait_ge(S["end_step"], 2)
                    act.activation(G, A, ACT.Exp).then_inc(S["exp_done"], 1)
                if load_heads:
                    heads_act(act, H)

            @block.vector
            def _(dve):
                def apply_gate(i, j, at, odd):
                    n = i * nf + j
                    dve.wait_ge(S["act_done"], n + 1)
                    if j == 0:
                        dve.wait_ge(S["g_done"], i + 1)
                    if at >= 1 or j >= 2:
                        wait_low(dve, i - (j < 2), (j - 2) % nf)
                    dve.tensor_tensor(hg[:, j % 2, :], r[:, j % 2, :], bank(B_G[odd]), ALU.mult).then_inc(S["hg_done"], 1)

                def low(i, j, at):
                    n = i * nf + j
                    dve.wait_ge(S["hi_done"], n + 1)
                    if at >= 1 or j >= SLOTS:
                        dve.wait_ge(S["dn_done"], n - SLOTS + 1)
                    dve.tensor_tensor(hl[:, j % SLOTS, :], hg[:, j % 2, :], hh[:, j % SLOTS, :].bitcast(F32),
                                      ALU.subtract).then_inc(S["lo_dve"], 1)

                def add_residual(i, first):
                    dve.wait_ge(S["back_done"], i + 1)
                    xb = x[:, blk(i, BT), :]
                    dve.tensor_tensor(xb, xb, tiles(B_BACK), ALU.add).then_inc(S["added"], 1)

                def normalise(i, k, first):
                    if k == 0:
                        dve.wait_ge(S["added"], i + 1)
                    if k == LN_STEPS - 1 and not first:
                        dve.wait_ge(S["xT_done"], i)
                    ln_step(dve, i, k, S["step"], S["xn_ready"], keep=route)

                def next_low(i):
                    dve.wait_ge(S["xh_done"], i + 1)
                    dve.tensor_tensor(xl[:, blk(i)], bank(B_XT), xh[:, blk(i)].bitcast(F32),
                                      ALU.subtract).then_inc(S["xl_done"], 1)

                def one_block(i, at, odd, live=True):
                    for j in range(nf):
                        if live:
                            apply_gate(i, j, at, odd)
                            if j >= 1 and by_dve(j - 1):
                                low(i, j - 1, at)
                        for k, first in tail_blocks(i, at, j, AT_ADD):
                            add_residual(k, first)
                        for n in range(LN_STEPS):
                            for k, first in tail_blocks(i, at, j, AT_LN + n // RATE):
                                normalise(k, n, first)
                            if route and n < COUNT_AT:
                                for k, first in tail_blocks(i, at, j, AT_CHOOSE + n // RATE):
                                    choose_step(dve, k, n, S, bank(B_R), first)
                        for k, first in tail_blocks(i, at, j, AT_LOW):
                            next_low(k)
                        if route:
                            for t in range(BT):
                                for k, first in tail_blocks(i, at, j, AT_FILL + t * APART):
                                    fill_row(dve, k, t, S, sent, first)
                            for n in range(COUNT_AT, CHOOSE):
                                for k, first in tail_blocks(i, at, j, AT_PLACE + (n - COUNT_AT) // RATE):
                                    choose_step(dve, k, n, S, bank(B_R), first)

                if route:
                    dve.tensor_scalar(taken[:], iota[:, 0:E1], float(REGION), None, ALU.mult).then_inc(S["r_init"], 1)
                    dve.memset(run[:, 0:1], 0.0).then_inc(S["r_init"], 1)
                    dve.wait_ge(S["r_init"], 2)
                all_blocks(dve, one_block)
                if route:
                    weights_and_experts(dve, S)
                if load_heads:
                    heads_dve(dve, H)

            @block.gpsimd
            def _(pool):
                def low(i, j, first):
                    n = i * nf + j
                    pool.wait_ge(S["hi_done"], n + 1)
                    if not first or j >= SLOTS:
                        pool.wait_ge(S["dn_done"], n - SLOTS + 1)
                    pool.tensor_tensor(hl[:, j % SLOTS, :], hg[:, j % 2, :], hh[:, j % SLOTS, :].bitcast(F32),
                                       ALU.subtract).then_inc(S["lo_pool"], 1)

                def one_block(i, at, odd, live=True):
                    for j in range(nf):
                        if live and not by_dve(j):
                            low(i, j, at == 0)
                        if route:
                            for t in range(BT):
                                for k, first in tail_blocks(i, at, j, AT_SEND + t * APART):
                                    send_row(pool, k, t, S, sent, first)

                all_blocks(pool, one_block)
                for t in range(BT if route else 0):
                    pool.wait_ge(sent[t], 32 * NB)

            if route:
                @block.sync
                def _(sp):
                    if load_heads:
                        sp.wait_ge(S["dn_done"], NB * nf)
                        heads_load(sp, H)
                    blank_rows(sp, S)

    UNROLL = SEQ // BLK

    def square_sums(pe, dst):
        one_per_head = headones[:].rearrange("p (h d) -> p h d", d=HD0)[:, :, 0]
        for t in range(BT):
            last = pe.matmul(dst[:, t * H0:(t + 1) * H0], sq[:, t * P:(t + 1) * P], one_per_head, start=True, stop=True)
        return last

    def expand(act):
        return act.activation(nrm[:].rearrange("p (g d) -> p g d", d=HD0),
                              root[:].unsqueeze(2).to_broadcast([P, BT * H0, HD0]), ACT.Copy)

    def linear_kv():
        names = ("k_done", "v_done", "sq_ready", "vT_ready", "n_done", "root", "eps", "inv", "wide", "w_done",
                 "an_ready", "vt_done", "v_ready", "f_done", "f_ready", "kv_done", "kv_read")
        S = {n: sem(f"a0_{n}") for n in names}
        B_K, B_V, B_N, B_VT, B_F, B_KV, B_W = 0, 1, 2, 3, (4, 5), 6, 7
        kv = bank(B_KV)[:, 0:NCH * (KVW + 1)].rearrange("p (c w) -> p c w", c=NCH)

        def pipeline(e, step):
            for i in range(UNROLL):
                step(i, i - 1)
            with e.Fori(1, BATCH) as b:
                for u in range(UNROLL):
                    step(b * UNROLL + u, u - 1, b)
            step(NB, UNROLL - 1)

        with nc.Block() as block:
            @block.tensor
            def _(pe):
                def keys_values(i, first):
                    if not first:
                        pe.wait_ge(S["sq_ready"], i)
                    product3(pe, bank(B_K), w0[:, 0, 1], w0[:, 1, 1], i).then_inc(S["k_done"], 1)
                    if not first:
                        pe.wait_ge(S["vT_ready"], i)
                    product3(pe, bank(B_V), w0[:, 0, 2], w0[:, 1, 2], i).then_inc(S["v_done"], 1)

                def norms(i, first):
                    pe.wait_ge(S["sq_ready"], i + 1)
                    if not first:
                        pe.wait_ge(S["root"], i)
                    square_sums(pe, bank(B_N)).then_inc(S["n_done"], 1)

                def widen(i, first):
                    pe.wait_ge(S["wide"], i + 1)
                    if not first:
                        pe.wait_ge(S["an_ready"], i)
                    for t in range(BT):
                        last = pe.transpose(tiles(B_W)[:, t, :], nrm[:, t * P:(t + 1) * P], ident[:])
                    last.then_inc(S["w_done"], 1)

                def turn_values(i, first):
                    pe.wait_ge(S["vT_ready"], i + 1)
                    if not first:
                        pe.wait_ge(S["v_ready"], i)
                    for t in range(BT):
                        last = pe.transpose(tiles(B_VT)[:, t, :], vT[:, t * P:(t + 1) * P], ident[:])
                    last.then_inc(S["vt_done"], 1)

                def features(i, ts, first):
                    pe.wait_ge(S["an_ready"], i + 1)
                    for t in ts:
                        if t >= 2 or not first:
                            pe.wait_ge(S["f_ready"], i * BT + t - 1)
                        pe.matmul(bank(B_F[t % 2]), an[:, t * P:(t + 1) * P], pbd[:], start=True,
                                  stop=True).then_inc(S["f_done"], 1)

                def sums(i, u, b):
                    if u == 0 and b is not None:
                        pe.wait_ge(S["kv_read"], b)
                    pe.wait_ge(S["v_ready"], i + 1)
                    for t in range(BT):
                        pe.wait_ge(S["f_ready"], i * BT + t + 1)
                        for c in range(NCH):
                            last = pe.matmul(kv[:, c, :], feat[:, t, c * P:(c + 1) * P], vones[:, t, c, :],
                                             start=(u == 0 and t == 0 and c == 0),
                                             stop=(u == UNROLL - 1 and t == BT - 1), skip_group_check=True)
                    last.then_inc(S["kv_done"], 1)

                def step(i, u_before, b=None):
                    first, live = b is None and i == 0, b is not None or i < NB
                    if live:
                        keys_values(i, first)
                    if not first:
                        features(i - 1, (0, 1), b is None and i == 1)
                    if live:
                        norms(i, first)
                    if live:
                        turn_values(i, first)
                    if not first:
                        features(i - 1, (2, 3), b is None and i == 1)
                    if not first:
                        sums(i - 1, u_before % UNROLL, b)
                    if live:
                        widen(i, first)

                pipeline(pe, step)

            @block.gpsimd
            def _(pool):
                with pool.Fori(0, NB) as i:
                    xb = x[:, blk(i, BT), :]
                    pool.tensor_tensor(xb, xb, bo_all[:].unsqueeze(1).to_broadcast([P, BT, P]), ALU.add)

            @block.scalar
            def _(act):
                def step(i, u_before, b=None):
                    first, live = b is None and i == 0, b is not None or i < NB
                    if not live:
                        return
                    act.wait_ge(S["k_done"], i + 1)
                    if not first:
                        act.wait_ge(S["an_ready"], i)
                    act.activation(aT[:], bank(B_K), ACT.Identity, bias=bcol[:, 1:2])
                    act.activation(sq[:], bank(B_K), ACT.Square, bias=bcol[:, 1:2]).then_inc(S["sq_ready"], 1)
                    act.wait_ge(S["v_done"], i + 1)
                    if not first:
                        act.wait_ge(S["vt_done"], i)
                    act.activation(vT[:], bank(B_V), ACT.Identity, bias=bcol[:, 2:3]).then_inc(S["vT_ready"], 1)
                    act.wait_ge(S["n_done"], i + 1)
                    act.activation(root[:], bank(B_N)[:, 0:BT * H0], ACT.Sqrt).then_inc(S["root"], 1)
                    act.wait_ge(S["inv"], i + 1)
                    expand(act).then_inc(S["wide"], 1)

                pipeline(act, step)

            @block.vector
            def _(dve):
                def features(i, ts, first):
                    for t in ts:
                        dve.wait_ge(S["f_done"], i * BT + t + 1)
                        if not first:
                            dve.wait_ge(S["kv_done"], i)
                        dve.tensor_scalar(feat[:, t, :], bank(B_F[t % 2]), 0.0, YAT_EPS, ALU.max,
                                          ALU.add).then_inc(S["f_ready"], 1)

                def keep(b):
                    dve.wait_ge(S["kv_done"], UNROLL * b + UNROLL)
                    mine = kvbd[:, bass.ds(b, 1)].rearrange("p a c w -> p (a c) w")
                    dve.tensor_tensor(mine[:, :, 0:KVW], kv[:, :, 0:KVW],
                                      m32[:].unsqueeze(1).to_broadcast([P, NCH, KVW]), ALU.mult)
                    dve.tensor_tensor(mine[:, :, KVW:KVW + HPC], kv[:, :, KVW:KVW + 1].to_broadcast([P, NCH, HPC]),
                                      m4[:].unsqueeze(1).to_broadcast([P, NCH, HPC]), ALU.mult).then_inc(S["kv_read"], 1)

                def step(i, u_before, b=None):
                    first, live = b is None and i == 0, b is not None or i < NB
                    if not first:
                        features(i - 1, (0, 1), b is None and i == 1)
                    if live:
                        dve.wait_ge(S["root"], i + 1)
                        dve.tensor_scalar(root[:], root[:], NORM_EPS, None, ALU.add).then_inc(S["eps"], 1)
                        dve.wait_ge(S["eps"], i + 1)
                        dve.reciprocal(root[:], root[:]).then_inc(S["inv"], 1)
                    if not first:
                        features(i - 1, (2, 3), b is None and i == 1)
                    if live:
                        dve.wait_ge(S["vt_done"], i + 1)
                        if not first:
                            dve.wait_ge(S["kv_done"], i)
                        dve.tensor_copy(vones[:, :, :, 0:KVW],
                                        tiles(B_VT).rearrange("p t (c w) -> p t c w", c=NCH)).then_inc(S["v_ready"], 1)
                        dve.wait_ge(S["w_done"], i + 1)
                        dve.tensor_tensor(an[:], aT[:], bank(B_W), ALU.mult).then_inc(S["an_ready"], 1)
                    if u_before == -1 and b is not None:
                        keep(b - 1)
                    if not live:
                        keep(BATCH - 1)

                pipeline(dve, step)

    def linear_q():
        names = ("q_done", "sq_ready", "n_done", "root", "eps", "inv", "wide", "w_done", "an_ready", "f_done",
                 "f_ready", "qkv_done", "den_max", "den_inv", "o_ready", "oT_done", "oT_ready", "y_done", "added", "step",
                 "xn_ready", "xT_done", "xh_done", "xl_done")
        S = {n: sem(f"a0q_{n}") for n in names}
        B_Q, B_W, B_N, B_OT, B_XT, B_Y, B_F, B_QKV = 0, 0, 1, 1, 2, 3, (4, 5), (6, 7)
        W = KVW + HPC
        feats = (feat, feat1)

        def pipeline(e, step):
            for i in range(-1, 3):
                step(i, i % 2, (i - 1) // UNROLL)
            with e.Fori(1, BATCH - 1) as b:
                for u in range(UNROLL):
                    step(b * UNROLL + 1 + u, (1 + u) % 2, b)
            for i in range(NB - 1, NB + 3):
                step(i, i % 2, (i - 1) // UNROLL)

        def there(i):
            return not isinstance(i, int) or 0 <= i < NB

        def first(i):
            return isinstance(i, int) and i == 0

        with nc.Block() as block:
            @block.tensor
            def _(pe):
                def query(i):
                    if not first(i):
                        pe.wait_ge(S["an_ready"], i)
                    product3(pe, bank(B_Q), w0[:, 0, 0], w0[:, 1, 0], i).then_inc(S["q_done"], 1)

                def norms(i):
                    pe.wait_ge(S["sq_ready"], i + 1)
                    square_sums(pe, bank(B_N)).then_inc(S["n_done"], 1)

                def widen(i):
                    pe.wait_ge(S["wide"], i + 1)
                    for t in range(BT):
                        last = pe.transpose(tiles(B_W)[:, t, :], nrm[:, t * P:(t + 1) * P], ident[:])
                    last.then_inc(S["w_done"], 1)

                def features(i, cs):
                    pe.wait_ge(S["an_ready"], i + 1)
                    for c in cs:
                        if c >= 2 or not first(i):
                            pe.wait_ge(S["f_ready"], i * NCH + c - 1)
                        pe.matmul(bank(B_F[c % 2]), pbd[:, c * P:(c + 1) * P], an[:], start=True,
                                  stop=True).then_inc(S["f_done"], 1)

                def attend(i, odd, b):
                    pe.wait_ge(S["f_ready"], i * NCH + NCH)
                    if not first(i):
                        pe.wait_ge(S["o_ready"], i)
                    for t in range(BT):
                        for c in range(NCH):
                            at = (t % 2 * NCH + c) * W
                            last = pe.matmul(bank(B_QKV[t // 2])[:, at:at + W], feats[odd][:, c, t * P:(t + 1) * P],
                                             kvbd[:, bass.ds(b, 1), c, :].rearrange("p a w -> p (a w)"),
                                             start=True, stop=True)
                    last.then_inc(S["qkv_done"], 1)

                def turn(i):
                    pe.wait_ge(S["o_ready"], i + 1)
                    if there(i + 2):
                        pe.wait_ge(S["root"], i + 3)
                    for t in range(BT):
                        last = pe.transpose(tiles(B_OT)[:, t, :], o0[:, t, :], ident[:])
                    last.then_inc(S["oT_done"], 1)

                def project(i):
                    pe.wait_ge(S["oT_ready"], i + 1)
                    if not first(i):
                        pe.wait_ge(S["added"], i)
                    for t in range(BT):
                        last = pe.matmul(tiles(B_Y)[:, t, :], o0T[:, t * P:(t + 1) * P], wo0[:], start=True, stop=True)
                    last.then_inc(S["y_done"], 1)

                def next_xT(i):
                    pe.wait_ge(S["xn_ready"], i + 1)
                    pe.wait_ge(S["xl_done"], i + 1)
                    for t in range(BT):
                        last = pe.transpose(tiles(B_XT)[:, t, :], xn[:, t, :], ident[:])
                    last.then_inc(S["xT_done"], 1)

                def step(i, odd, b):
                    if there(i + 1):
                        query(i + 1)
                    if there(i - 2):
                        turn(i - 2)
                    if there(i):
                        features(i, (0, 1))
                    if there(i + 1):
                        if there(i - 2):
                            pe.wait_ge(S["oT_ready"], i - 1)
                        norms(i + 1)
                    if there(i):
                        features(i, (2, 3))
                    if there(i - 1):
                        attend(i - 1, 1 - odd, b)
                    if there(i + 1):
                        widen(i + 1)
                    if there(i - 2):
                        project(i - 2)
                    if there(i - 3):
                        next_xT(i - 3)

                pipeline(pe, step)

            @block.scalar
            def _(act):
                def step(i, odd, b):
                    if there(i + 1):
                        act.wait_ge(S["q_done"], i + 2)
                        if there(i):
                            act.wait_ge(S["an_ready"], i + 1)
                        act.activation(aT[:], bank(B_Q), ACT.Identity, bias=bcol[:, 0:1])
                        act.activation(sq[:], bank(B_Q), ACT.Square, bias=bcol[:, 0:1]).then_inc(S["sq_ready"], 1)
                    if there(i - 2):
                        act.wait_ge(S["oT_done"], i - 1)
                        if there(i - 3):
                            act.wait_ge(S["y_done"], i - 2)
                        act.activation(o0T[:], bank(B_OT), ACT.Copy).then_inc(S["oT_ready"], 1)
                    if there(i + 1):
                        act.wait_ge(S["n_done"], i + 2)
                        act.activation(root[:], bank(B_N)[:, 0:BT * H0], ACT.Sqrt).then_inc(S["root"], 1)
                        act.wait_ge(S["inv"], i + 2)
                        expand(act).then_inc(S["wide"], 1)
                    if there(i - 3):
                        act.wait_ge(S["xT_done"], i - 2)
                        act.activation(xh[:, blk(i - 3)], bank(B_XT), ACT.Copy).then_inc(S["xh_done"], 1)

                pipeline(act, step)

            @block.vector
            def _(dve):
                def by_head(ap):
                    return ap.rearrange("p t (c h) -> p (t c) h", c=NCH)

                def output(i):
                    dve.wait_ge(S["qkv_done"], i + 1)
                    acc = [bank(k)[:, 0:2 * NCH * W].rearrange("p (t w) -> p t w", w=W) for k in B_QKV]
                    for g in range(2):
                        last = dve.tensor_scalar(by_head(den[:, 2 * g:2 * g + 2, :]), acc[g][:, :, KVW:W], DEN_MIN, None,
                                                 ALU.max)
                    last.then_inc(S["den_max"], 1)
                    dve.wait_ge(S["den_max"], i + 1)
                    dve.reciprocal(den[:], den[:]).then_inc(S["den_inv"], 1)
                    dve.wait_ge(S["den_inv"], i + 1)
                    if not first(i):
                        dve.wait_ge(S["oT_done"], i)
                    for g in range(2):
                        last = dve.tensor_tensor(
                            o0[:, 2 * g:2 * g + 2, :].rearrange("p t (c h d) -> p (t c) h d", c=NCH, h=HPC),
                            acc[g][:, :, 0:KVW].rearrange("p t (h d) -> p t h d", h=HPC),
                            by_head(den[:, 2 * g:2 * g + 2, :]).unsqueeze(3).to_broadcast([P, 2 * NCH, HPC, HD0]),
                            ALU.mult)
                    last.then_inc(S["o_ready"], 1)

                def normalise(i, steps):
                    if not there(i):
                        return
                    if steps[0] == 0:
                        dve.wait_ge(S["added"], i + 1)
                    for k in steps:
                        ln_step(dve, i, k, S["step"], S["xn_ready"])

                def features(i, odd, c):
                    if not there(i):
                        return
                    dve.wait_ge(S["f_done"], i * NCH + c + 1)
                    if not isinstance(i, int) or i >= 2:
                        dve.wait_ge(S["qkv_done"], i - 1)
                    dve.tensor_scalar(feats[odd][:, c, :], bank(B_F[c % 2]), 0.0, YAT_EPS, ALU.max,
                                      ALU.add).then_inc(S["f_ready"], 1)

                def step(i, odd, b):
                    features(i, odd, 0)
                    normalise(i - 3, (0,))
                    features(i, odd, 1)
                    normalise(i - 3, (1, 2))
                    if there(i + 1):
                        dve.wait_ge(S["root"], i + 2)
                        dve.tensor_scalar(root[:], root[:], NORM_EPS, None, ALU.add).then_inc(S["eps"], 1)
                        normalise(i - 3, (3,))
                        dve.wait_ge(S["eps"], i + 2)
                        dve.reciprocal(root[:], root[:]).then_inc(S["inv"], 1)
                    else:
                        normalise(i - 3, (3,))
                    normalise(i - 3, (4, 5))
                    features(i, odd, 2)
                    normalise(i - 3, (6, 7))
                    features(i, odd, 3)
                    normalise(i - 3, range(8, LN_STEPS - 1))
                    if there(i + 1):
                        dve.wait_ge(S["w_done"], i + 2)
                        dve.tensor_tensor(an[:], aT[:], bank(B_W), ALU.mult).then_inc(S["an_ready"], 1)
                    normalise(i - 3, (LN_STEPS - 1,))
                    if there(i - 1):
                        output(i - 1)
                    if there(i - 2):
                        dve.wait_ge(S["y_done"], i - 1)
                        xb = x[:, blk(i - 2, BT), :]
                        dve.tensor_tensor(xb, xb, tiles(B_Y), ALU.add).then_inc(S["added"], 1)
                    if there(i - 3):
                        dve.wait_ge(S["xh_done"], i - 2)
                        dve.tensor_tensor(xl[:, blk(i - 3)], bank(B_XT), xh[:, blk(i - 3)].bitcast(F32),
                                          ALU.subtract).then_inc(S["xl_done"], 1)

                dve.tensor_copy(spare_v[:], spare_v[:]).then_inc(S["xl_done"], 1)
                pipeline(dve, step)

    def turn_sems(ph):
        return {n: sem(f"{ph}_{n}") for n in ("g_turned", "g_hi", "g_lo")}

    def turn_pe(pe, T, n_exp, banks):
        ring = len(banks)
        for i in range(NB):
            if i >= ring:
                pe.wait_ge(T["g_lo"], i - ring + 1)
            for t in range(BT):
                last = pe.transpose(bank(banks[i % ring])[0:n_exp, t * P:(t + 1) * P], gate[:, i * BT + t, 0:n_exp], ident[:])
            last.then_inc(T["g_turned"], 1)

    def turn_act(act, T, n_exp, banks):
        ring = len(banks)
        with act.Fori(0, NB // ring) as g:
            for a in range(ring):
                i = ring * g + a
                act.wait_ge(T["g_turned"], i + 1)
                act.activation(gT[0:n_exp, blk(i)], bank(banks[a])[0:n_exp, :], ACT.Copy).then_inc(T["g_hi"], 1)

    def turn_dve(dve, T, n_exp, banks):
        ring = len(banks)
        with dve.Fori(0, NB // ring) as g:
            for a in range(ring):
                i = ring * g + a
                dve.wait_ge(T["g_hi"], i + 1)
                dve.tensor_tensor(gT[LO_ROW:LO_ROW + n_exp, blk(i)], bank(banks[a])[0:n_exp, :],
                                  gT[0:n_exp, blk(i)].bitcast(F32), ALU.subtract).then_inc(T["g_lo"], 1)

    def moe_experts(ph):
        Q = F1 // P
        names = ("up_done", "act_done", "hi_done", "lo_done", "dn_done", "xt_done", "xh_done", "xl_done", "w_up", "w_dn",
                 "b1_set", "b2_set", "oT_ready", "back_done", "y_out", "spaced")
        S = {n: sem(f"{ph}_{n}") for n in names}
        x_load, to_load, y_sent = ([sem(f"{ph}_{n}{a}") for a in range(2)] for n in ("x_load", "to_load", "y_sent"))
        w_now = xh[:].rearrange("p (a k n) -> p a k n", a=2, k=4)
        xb = xl[:, 0:4 * BLK].rearrange("p (a k n) -> p a k n", a=2, k=2)
        x_in = row[:].rearrange("p s c w -> p (s c w)")[:, 0:2 * BLK].rearrange("p (a t d) -> p a t d", a=2, t=BT)
        y_row = ed
        gates = gate[:].rearrange("p t e -> p (t e)")
        hid = [r[:, 0, :], r[:, 1, :], gates[:, 0:BLK], gates[:, BLK:]]
        yT = hg[:, 0, :]
        B_UP, B_OUT, B_BACK, B_XT = (0, 1, 2, 3), (4, 7), 5, 6

        UP_AT, DOWN_AT, LEAVE_AT = (0, 0), (1, 1), 2

        class Block:
            def __init__(self, g, c, loop):
                self.g, self.c, self.loop = g, c, loop
                self.n, self.odd, self.half = 2 * g + c, c % 2, g + c // 2

            def there(self):
                return self.loop or 0 <= self.c < SPARSE

            def past(self, k):
                return self.loop or self.c >= k

            def __add__(self, k):
                return Block(self.g, self.c + k, self.loop)

        def iterations(e, one):
            for c in (-1, 0, 1):
                one(Block(0, c, False))
            with e.Fori(1, (SPARSE - 1) // 2) as g:
                for a in range(2):
                    one(Block(g, a, True))
            for c in range(SPARSE - 1, SPARSE + 2):
                one(Block(0, c, False))

        with nc.Block() as block:
            @block.sync
            def _(sp):
                def rows_from(sp, b):
                    first = sp.value_load(row_at[0:1, bass.ds(b.n + 1, 1)], min_val=0, max_val=ROWS - BLK)
                    return rows[bass.ds(first, BLK), :].rearrange("(t p) w -> p t w", p=P)

                def one(b):
                    nxt, back = b + 1, b + -2
                    if nxt.there():
                        if nxt.past(2):
                            sp.wait_ge(S["xt_done"], nxt.n - 1)
                        sp.dma_start(x_in[:, nxt.odd], rows_from(sp, nxt)[:, :, 0:P]).then_inc(x_load[nxt.odd], 16)
                    if back.there():
                        if back.past(2):
                            sp.wait_ge(y_sent[back.odd], 16 * BT * back.half)
                        sp.dma_start(answer_to[:, back.odd, :].unsqueeze(2), rows_from(sp, back)[:, :, P:].bitcast(I32),
                                     allow_slow_non_contiguous=True).then_inc(to_load[back.odd], 16)

                iterations(sp, one)

            @block.tensor
            def _(pe):
                def turn(b):
                    pe.wait_ge(x_load[b.odd], 16 * (b.half + 1))
                    if b.past(1):
                        pe.wait_ge(S["xl_done"], b.n)
                    for t in range(BT):
                        last = pe.transpose(tiles(B_XT)[:, t, :], x_in[:, b.odd, t, :], ident[:])
                    last.then_inc(S["xt_done"], 1)

                def up(b, j):
                    n = b.n * Q + j
                    if b.past(1):
                        pe.wait_ge(S["act_done"], n - Q + 1)
                    if j == 0:
                        pe.wait_ge(S["xl_done"], b.n + 1)
                        pe.wait_ge(S["w_up"], b.n + 1)
                    dst, cols = bank(B_UP[j]), slice(j * P, (j + 1) * P)
                    high, low = (w_now[:, b.odd, k, cols] for k in (0, 1))
                    pe.matmul(dst, high, xb[:, b.odd, 1], start=True, stop=False)
                    pe.matmul(dst, low, xb[:, b.odd, 0], start=False, stop=False)
                    pe.matmul(dst, high, xb[:, b.odd, 0], start=False, stop=True).then_inc(S["up_done"], 1)

                def down(b, j):
                    if j == 0:
                        pe.wait_ge(S["w_dn"], b.n + 1)
                        if b.past(2):
                            pe.wait_ge(S["oT_ready"], b.n - 1)
                    pe.wait_ge(S["lo_done"], b.n * Q + j + 1)
                    dst, cols = bank(B_OUT[b.odd]), slice(j * P, (j + 1) * P)
                    high, low = (w_now[:, b.odd, k, cols] for k in (2, 3))
                    pe.matmul(dst, low, hh[:, j, :], start=(j == 0), stop=False)
                    pe.matmul(dst, high, hl[:, j, :], start=False, stop=False)
                    pe.matmul(dst, high, hh[:, j, :], start=False, stop=(j == Q - 1)).then_inc(S["dn_done"], 1)

                def back(b):
                    pe.wait_ge(S["oT_ready"], b.n + 1)
                    if b.past(1):
                        pe.wait_ge(S["y_out"], b.n)
                    for t in range(BT):
                        last = pe.transpose(tiles(B_BACK)[:, t, :], yT[:, t * P:(t + 1) * P], ident[:])
                    last.then_inc(S["back_done"], 1)

                def one(b):
                    for j in range(Q):
                        if j == 0 and (b + 1).there():
                            turn(b + 1)
                        if b.there():
                            up(b, j)
                        if (b + -1).there():
                            down(b + -1, j)
                        if j == 1 and (b + -2).there():
                            back(b + -2)

                iterations(pe, one)

            @block.scalar
            def _(act):
                def activate(b, j):
                    n = b.n * Q + j
                    act.wait_ge(S["up_done"], n + 1)
                    if j == 0:
                        act.wait_ge(S["b1_set"], b.n + 1)
                    if b.past(1):
                        act.wait_ge(S["lo_done"], n - Q + 1)
                    act.activation(hid[j], bank(B_UP[j]), ACT.Gelu, bias=b1_now[:, b.odd, j:j + 1]
                                   ).then_inc(S["act_done"], 1)

                def high(b, j):
                    n = b.n * Q + j
                    act.wait_ge(S["act_done"], n + 1)
                    if b.past(1):
                        act.wait_ge(S["dn_done"], n - Q + 1)
                    act.activation(hh[:, j, :], hid[j], ACT.Copy).then_inc(S["hi_done"], 1)

                def evacuate(b):
                    act.wait_ge(S["dn_done"], b.n * Q + Q)
                    act.wait_ge(S["b2_set"], b.n + 1)
                    if b.past(1):
                        act.wait_ge(S["back_done"], b.n)
                    act.activation(yT, bank(B_OUT[b.odd]), ACT.Identity, bias=b2_now[:, b.odd:b.odd + 1]
                                   ).then_inc(S["oT_ready"], 1)

                def next_high(b):
                    act.wait_ge(S["xt_done"], b.n + 1)
                    if b.past(2):
                        act.wait_ge(S["up_done"], (b.n - 1) * Q)
                    act.activation(xb[:, b.odd, 0], bank(B_XT), ACT.Copy).then_inc(S["xh_done"], 1)

                def one(b):
                    for j in range(Q):
                        if j == 0 and (b + 1).there():
                            next_high(b + 1)
                        if b.there():
                            activate(b, j)
                        if j == 0 and (b + -1).there():
                            high(b + -1, Q - 1)
                        if j >= 1 and b.there():
                            high(b, j - 1)
                        if j == 0 and (b + -2).there():
                            evacuate(b + -2)

                iterations(act, one)

            @block.vector
            def _(dve):
                def low(b, j):
                    n = b.n * Q + j
                    dve.wait_ge(S["hi_done"], n + 1)
                    if b.past(1):
                        dve.wait_ge(S["dn_done"], n - Q + 1)
                    dve.tensor_tensor(hl[:, j, :], hid[j], hh[:, j, :].bitcast(F32), ALU.subtract
                                      ).then_inc(S["lo_done"], 1)

                def up_weights(b, e, k):
                    if k == 0 and b.past(2):
                        dve.wait_ge(S["up_done"], (b.n - 1) * Q)
                        dve.wait_ge(S["up_done"], 1)
                    last = dve.tensor_copy(w_now[:, b.odd, k], m_up[:, k, bass.ds(e * F1, F1)])
                    if k == 1:
                        last.then_inc(S["w_up"], 1)
                        dve.tensor_copy(b1_now[:, b.odd, :], b1c[:, bass.ds(e * Q, Q)]).then_inc(S["b1_set"], 1)

                def down_weights(b, e, k):
                    if k == 0 and b.past(2):
                        dve.wait_ge(S["dn_done"], (b.n - 1) * Q)
                        dve.wait_ge(S["dn_done"], 1)
                    last = dve.tensor_copy(w_now[:, b.odd, 2 + k], m_dn[:, k, bass.ds(e * F1, F1)])
                    if k == 1:
                        last.then_inc(S["w_dn"], 1)

                def answer_bias(b, e):
                    if b.past(2):
                        dve.wait_ge(S["oT_ready"], b.n - 1)
                        dve.wait_ge(S["oT_ready"], 1)
                    dve.tensor_copy(b2_now[:, b.odd:b.odd + 1], b2c[:, bass.ds(e, 1)]).then_inc(S["b2_set"], 1)

                def next_low(b):
                    dve.wait_ge(S["xh_done"], b.n + 1)
                    dve.tensor_tensor(xb[:, b.odd, 1], bank(B_XT), xb[:, b.odd, 0].bitcast(F32), ALU.subtract
                                      ).then_inc(S["xl_done"], 1)

                def leave(b):
                    dve.wait_ge(S["back_done"], b.n + 1)
                    if b.past(2):
                        dve.wait_ge(y_sent[b.odd], 16 * BT * b.half)
                    dve.tensor_copy(y_row[:, b.odd], tiles(B_BACK)).then_inc(S["y_out"], 1)

                def one(b):
                    last, nxt, out = b + -1, b + 1, b + -2
                    e_last, e_now, e_next = (
                        dve.value_load(expert_of[0:1, bass.ds(k.n + 1, 1)], min_val=0, max_val=E1 - 1) if k.there() else None
                        for k in (last, b, nxt))
                    for j in range(Q):
                        if j == 0 and last.there():
                            low(last, Q - 1)
                        if j >= 1 and b.there():
                            low(b, j - 1)
                        if j == 0 and nxt.there():
                            next_low(nxt)
                        for k in range(2):
                            if j == UP_AT[k] and nxt.there():
                                up_weights(nxt, e_next, k)
                            if j == DOWN_AT[k] and b.there():
                                down_weights(b, e_now, k)
                        if j == LEAVE_AT and out.there():
                            leave(out)
                        if j == 3 and last.there():
                            answer_bias(last, e_last)

                iterations(dve, one)

            @block.gpsimd
            def _(pool):
                def one(b):
                    out = b + -2
                    if out.there():
                        pool.wait_ge(S["y_out"], out.n + 1)
                        pool.wait_ge(to_load[out.odd], 16 * (out.half + 1))
                        if out.past(1):
                            pool.wait_ge(S["spaced"], out.n)
                        apart(pool, spare_p).then_inc(S["spaced"], 1)
                        for t in range(BT):
                            pool.indirect_dma_start(answers, bass.IndirectOffsetOnAxis(ap=answer_to[:, out.odd, t:t + 1], axis=0),
                                                    y_row[:, out.odd, t, :], None, bounds_check=2 * T - 1, oob_is_err=False
                                                    ).then_inc(y_sent[out.odd], 16)

                iterations(pool, one)
                for a in range(2):
                    pool.wait_ge(y_sent[a], 16 * BT * ((SPARSE + 1 - a) // 2))

    def moe_combine(ph, final):
        names = ("scaled", "summed", "added", "step", "measured", "xn_ready", "xT_done", "xh_done", "xl_done", "stored")
        S = {n: sem(f"{ph}_{n}") for n in names}
        AHEAD = 4
        y_in = [sem(f"{ph}_y_in{a}") for a in range(AHEAD)]
        answers_v = answers.rearrange("(c t p) d -> p c t d", c=2, p=P)
        slots = raw_all[:].rearrange("p a (c t d) -> p c a t d", c=2, t=BT)

        def store(e, i):
            e.wait_ge(S["added"], i + 1)
            e.dma_start(out_v[:, blk(i, BT), :], x[:, blk(i, BT), :]).then_inc(S["stored"], 16)

        with nc.Block() as block:
            @block.sync
            def _(sp):
                for i in range(NB):
                    wait_past(sp, S["added"], i - AHEAD + 1)
                    sp.dma_start(slots[:, 0, i % AHEAD], answers_v[:, 0, blk(i, BT), :]).then_inc(y_in[i % AHEAD], 16)
                    sp.dma_start(slots[:, 1, i % AHEAD], answers_v[:, 1, blk(i, BT), :]).then_inc(y_in[i % AHEAD], 16)

            @block.scalar
            def _(act):
                for i in range(NB):
                    act.wait_ge(y_in[i % AHEAD], 32 * (i // AHEAD + 1))
                    for t in range(BT):
                        y1 = slots[:, 0, i % AHEAD, t, :]
                        last = act.activation(y1, y1, ACT.Identity, scale=weight2[:, 0, i * BT + t:i * BT + t + 1])
                    last.then_inc(S["scaled"], 1)
                    if final and i >= 2:
                        store(act, i - 2)
                if final:
                    for i in range(NB - 2, NB):
                        store(act, i)
                    act.wait_ge(S["stored"], 16 * NB)
                else:
                    for i in range(NB):
                        split_act(act, S, i)

            @block.vector
            def _(dve):
                n = 0

                def then(ins):
                    nonlocal n
                    n += 1
                    ins.then_inc(S["step"], 1)
                    dve.wait_ge(S["step"], n)

                for i in range(NB):
                    dve.wait_ge(y_in[i % AHEAD], 32 * (i // AHEAD + 1))
                    dve.wait_ge(S["scaled"], i + 1)
                    for t in range(BT):
                        y1, y2 = (slots[:, c, i % AHEAD, t, :] for c in range(2))
                        last = dve.scalar_tensor_tensor(y1, y2, weight2[:, 1, i * BT + t:i * BT + t + 1], y1, ALU.mult, ALU.add)
                    last.then_inc(S["summed"], 1)
                    if i >= 1 and not final:
                        dve.wait_ge(S["added"], i)
                        measure(dve, i - 1, S["measured"])
                    if i >= 2 and not final:
                        gather(dve, i - 2, S["measured"])
                if final:
                    return
                dve.wait_ge(S["added"], NB)
                measure(dve, NB - 1, S["measured"])
                gather(dve, NB - 2, S["measured"])
                then(gather(dve, NB - 1, S["measured"]))
                deviations(dve, then)
                split_dve(dve, S)

            @block.gpsimd
            def _(pool):
                for i in range(NB):
                    pool.wait_ge(S["summed"], i + 1)
                    xb = x[:, blk(i, BT), :]
                    pool.tensor_tensor(xb, xb, slots[:, 0, i % AHEAD], ALU.add).then_inc(S["added"], 1)

            if not final:
                @block.tensor
                def _(pe):
                    split_pe(pe, S)

    def softmax_diagonal():
        fold = [gate[:, k * NT // 2:(k + 1) * NT // 2, H1:].rearrange("p (t a) e -> p t a e", a=2) for k in range(2)]
        diag = ed[:].rearrange("p k t d -> p (k t) d")
        names = ("halved", "folded", "w_ready", "y_done", "y_hi", "y_lo", "sc_done", "mx_done", "exp_done", "dg_done", "red_done",
                 "rec_done", "p_set")
        S = {n: sem(f"a1_{n}") for n in names}
        T, TURN = turn_sems("a1"), (0, 1, 2, 3)
        YH, YL = ([w[:].rearrange("p s n -> p (s n)")[:, k * SEQ:(k + 1) * SEQ] for k in range(2)] for w in (hh, hl))
        E = [r[:].rearrange("p s n -> p (s n)"), hg[:].rearrange("p s n -> p (s n)")]
        PER = BATCH
        ORDER = (7, 0, 1, 4, 6, 2, 5, 3)
        Y_AT = {0: 1, 3: 0}
        HIGH_AT = {0: 1, 2: 0}
        LOW_AT = {0: 1, 4: 0}
        BIG = [n for n, q in enumerate(ORDER) if q >= BT]
        PAIR = [k % 3 for k in range(PER * BT - 1)] + [1]

        def scores(b, n):
            q, odd = ORDER[n], b % 2
            if q >= BT:
                k = 2 * PAIR[b * BT + BIG.index(n)]
                return psum[:, k:k + 2, 0:(q + 1) * P // 2]
            k = 7 - odd if q != 3 else 6 + odd
            a = P if q == 1 else 0
            return psum[:, k:k + 1, a:a + (q + 1) * P]

        def y_bank(b, half):
            return bank(6 + b % 2)

        def big_before(b, n):
            k = b * BT + BIG.index(n)
            d = next(d for d in range(1, PER * BT + 1) if PAIR[k - d] == PAIR[k])
            back = BIG.index(n) - d
            return QT * (back // BT) + BIG[back % BT]

        with nc.Block() as block:
            @block.gpsimd
            def _(pool):
                def quarter(k):
                    return diag[:, :, 32 * k:32 * (k + 1)].rearrange("p t (a e) -> p t a e", a=2)

                def weights(h):
                    for k, w in enumerate((f_h, f_l)):
                        last = pool.tensor_copy(hw[:, k], w[:, bass.ds(h, 1), :].rearrange("p a d -> p (a d)"))
                    last.then_inc(S["w_ready"], 1)

                def unit(u, b, first, turn):
                    if not (first and b == 0):
                        pool.wait_ge(S["folded"], u)
                    for n, q in enumerate(ORDER):
                        pool.wait_ge(S["exp_done"], u * QT + n + 1)
                        pool.tensor_tensor(diag[:, q, :], E[n % 2][:, q * P:(q + 1) * P], ident[:], ALU.mult
                                           ).then_inc(S["dg_done"], 1)
                        if n == 3 and turn is not None:
                            pool.wait_ge(S["y_done"], 2 * (u + 2))
                            apart(pool, spare_p)
                            weights(turn)
                    pool.wait_ge(S["dg_done"], u * QT + QT)
                    pool.tensor_tensor(diag[:, :, 0:64], diag[:, :, 0:64], diag[:, :, 64:], ALU.add
                                       ).then_inc(S["halved"], 1)
                    pool.wait_ge(S["halved"], u + 1)
                    if not first:
                        pool.wait_ge(S["red_done"], u - 1)
                    pool.tensor_tensor(fold[b % 2], quarter(0), quarter(1), ALU.add).then_inc(S["folded"], 1)

                weights(0)
                for b in range(PER):
                    unit(b, b, b < 2, 1 if b == PER - 2 else None)
                with pool.Fori(1, H1 - 1) as h:
                    for b in range(PER):
                        unit(h * PER + b, b, False, h + 1 if b == PER - 2 else None)
                for b in range(PER):
                    unit((H1 - 1) * PER + b, b, False, None)

            @block.tensor
            def _(pe):
                def product(u, b, half):
                    at = bass.ds(b * SEQ + half * BLK, BLK)
                    dst = y_bank(b + 1, half)
                    pe.matmul(dst, hw[:, 0], xl[:, at], start=True, stop=False)
                    pe.matmul(dst, hw[:, 1], xh[:, at], start=False, stop=False)
                    pe.matmul(dst, hw[:, 0], xh[:, at], start=False, stop=True).then_inc(S["y_done"], 1)

                def logits(u, b, n, first):
                    q, s = ORDER[n], b % 2
                    if q >= BT and not (first and big_before(b, n) < 0):
                        pe.wait_ge(S["exp_done"], u * QT + big_before(b, n) + 1)
                    if n == ORDER.index(0) and not first:
                        pe.wait_ge(S["exp_done"], u * QT)
                    if q == 2:
                        pe.wait_ge(S["exp_done"], u * QT + ORDER.index(1) + 1)
                    if q == 3 and not last_unit:
                        pe.wait_ge(S["y_lo"], 2 * u + 4)
                    dst = scores(b, n)
                    halves, width = dst.shape[1], dst.shape[2]
                    yh, yl = YH[s][:, q * P:(q + 1) * P], YL[s][:, q * P:(q + 1) * P]
                    if q == 0:
                        two = bank(7 - b % 2).rearrange("p (a d) -> p a d", a=2)[:, :, 0:P]
                        pe.matmul(two, identb[:], cmask[:].unsqueeze(1).to_broadcast([P, 2, P]), start=True, stop=False,
                                  skip_group_check=True)
                    for k in range(halves):
                        at = bass.ds(b * SEQ + k * width, width)
                        pe.matmul(dst[:, k, :], yh, xl[:, at], start=(q > 1), stop=False, skip_group_check=(q < 2))
                        pe.matmul(dst[:, k, :], yl, xh[:, at], start=False, stop=False, skip_group_check=(q < 2))
                        last = pe.matmul(dst[:, k, :], yh, xh[:, at], start=False, stop=(q < 2 or k < halves - 1),
                                         skip_group_check=(q < 2))
                    if q > 1:
                        last = pe.matmul(dst[:, halves - 1, width - P:], identb[:], cmask[:], start=False, stop=True)
                    last.then_inc(S["sc_done"], 1)

                def unit(u, b, first, last, w_count):
                    nonlocal last_unit
                    last_unit = last
                    for n in range(QT):
                        if n == 0:
                            pe.wait_ge(S["y_lo"], 2 * u + 2)
                        logits(u, b, n, first)
                        if n in Y_AT and not last:
                            if Y_AT[n]:
                                if not first:
                                    pe.wait_ge(S["exp_done"], u * QT - QT + ORDER.index(2) + 1)
                                if b == PER - 1:
                                    pe.wait_ge(S["w_ready"], w_count)
                            else:
                                pe.wait_ge(S["y_lo"], 2 * u + 3)
                            product(u + 1, (b + 1) % PER, Y_AT[n])

                last_unit = False
                pe.wait_ge(S["w_ready"], 1)
                product(0, 0, 1)
                pe.wait_ge(S["y_lo"], 1)
                product(0, 0, 0)
                for b in range(PER):
                    unit(b, b, b == 0, False, 2)
                with pe.Fori(1, H1 - 1) as h:
                    for b in range(PER):
                        unit(h * PER + b, b, False, False, h + 2)
                for b in range(PER):
                    unit((H1 - 1) * PER + b, b, False, b == PER - 1, H1)
                pe.wait_ge(S["p_set"], H1 * PER)
                turn_pe(pe, T, H1, TURN)

            @block.scalar
            def _(act):
                def high(u, b, half, first):
                    to = slice(half * BLK, (half + 1) * BLK)
                    act.wait_ge(S["y_done"], 2 * u + (2 - half))
                    if not first:
                        act.wait_ge(S["sc_done"], (u - 1) * QT)
                    act.activation(YH[b % 2][:, to], y_bank(b + 1, half), ACT.Copy).then_inc(S["y_hi"], 1)

                def unit(u, b, first, last):
                    for n, q in enumerate(ORDER):
                        if n in HIGH_AT and not last:
                            high(u + 1, b + 1, HIGH_AT[n], first)
                        act.wait_ge(S["mx_done"], u * QT + n + 1 + (q == 0))
                        if not (first and n < 2):
                            act.wait_ge(S["dg_done"], u * QT + n - 1)
                        if n == 0 and not (isinstance(u, int) and u < 2):
                            act.wait_ge(S["rec_done"], u - 1)
                        src = scores(b, n)
                        act.activation(E[n % 2][:, 0:(q + 1) * P].rearrange("p (k n) -> p k n", k=src.shape[1]), src, ACT.Exp,
                                       bias=nmax[:, b % 2, q:q + 1],
                                       accum_out=esum[:, b % 2, q:q + 1]).then_inc(S["exp_done"], 1)

                high(0, 0, 1, True)
                high(0, 0, 0, True)
                for b in range(PER):
                    unit(b, b, b == 0, False)
                with act.Fori(1, H1 - 1) as h:
                    for b in range(PER):
                        unit(h * PER + b, b, False, False)
                for b in range(PER):
                    unit((H1 - 1) * PER + b, b, False, b == PER - 1)
                turn_act(act, T, H1, TURN)

            @block.vector
            def _(dve):
                def low(u, b, half):
                    to = slice(half * BLK, (half + 1) * BLK)
                    dve.wait_ge(S["y_hi"], 2 * u + (2 - half))
                    dve.tensor_tensor(YL[b % 2][:, to], y_bank(b + 1, half), YH[b % 2][:, to].bitcast(F32), ALU.subtract
                                      ).then_inc(S["y_lo"], 1)

                def weights(u, h, b):
                    dve.wait_ge(S["exp_done"], u * QT + QT)
                    dve.reciprocal(rsum[:], esum[:, b % 2, :]).then_inc(S["rec_done"], 1)
                    dve.wait_ge(S["folded"], u + 1)
                    dve.tensor_reduce(dsum[:], fold[b % 2], AX.XY, ALU.add).then_inc(S["red_done"], 1)
                    dve.wait_ge(S["rec_done"], u + 1)
                    dve.wait_ge(S["red_done"], u + 1)
                    dst = gate[:, b * QT:(b + 1) * QT, bass.ds(h, 1)].rearrange("p t a -> p (t a)")
                    dve.tensor_tensor(dst, dsum[:], rsum[:], ALU.mult).then_inc(S["p_set"], 1)

                def unit(u, h, b, first, last):
                    for n, q in enumerate(ORDER):
                        dve.wait_ge(S["sc_done"], u * QT + n + 1 + (q == 0))
                        if n == 0 and not (isinstance(u, int) and u < 2):
                            dve.wait_ge(S["exp_done"], (u - 1) * QT)
                        dve.tensor_reduce(nmax[:, b % 2, q:q + 1], scores(b, n), AX.XY, ALU.max,
                                          negate=True).then_inc(S["mx_done"], 1)
                        if n in LOW_AT and not last:
                            low(u + 1, b + 1, LOW_AT[n])
                        if n == 3 and not first:
                            weights(u - 1, h if b else h - 1, (b - 1) % PER)

                low(0, 0, 1)
                low(0, 0, 0)
                for b in range(PER):
                    unit(b, 0, b, b == 0, False)
                with dve.Fori(1, H1 - 1) as h:
                    for b in range(PER):
                        unit(h * PER + b, h, b, False, False)
                for b in range(PER):
                    unit((H1 - 1) * PER + b, H1 - 1, b, False, b == PER - 1)
                weights(H1 * PER - 1, H1 - 1, PER - 1)
                turn_dve(dve, T, H1, TURN)

    whole = sb("whole", [P, E1], I32)
    iota8 = sb("iota8", [P, E1], F32)
    nmax = sb("nmax", [P, 2, QT], F32)
    esum = sb("esum", [P, 2, QT], F32)
    dsum = sb("dsum", [P, QT], F32)
    rsum = sb("rsum", [P, QT], F32)

    ffn = dict(nf=NF0, up=(f_uph, f_upl), dn=(f_dnh, f_dnl), picked=0, func=ACT.Relu, scale=0.5)
    heads = dict(nf=NF2, up=(v_h, v_l), dn=(o_h, o_l), picked=1, func=ACT.Identity, scale=1.0)

    def moe(ph, final):
        moe_experts(ph + "e")
        end_phase()
        moe_combine(ph + "c", final)

    setup()
    end_phase()
    route_ffn("r0", False)
    end_phase()
    gated("f0", **ffn)
    end_phase()
    linear_kv()
    end_phase()
    linear_q()
    end_phase()
    route_ffn("r1", True)
    end_phase()
    gated("f1", route=True, load_heads=True, **ffn)
    end_phase()
    moe("m0", False)
    end_phase()
    softmax_diagonal()
    end_phase()
    gated("a1o", route=True, **heads)
    end_phase()
    moe("m1", True)
    top.close()


_INS = ['L0_attn_x', 'L0_attn_Wq', 'L0_attn_bq', 'L0_attn_Wk', 'L0_attn_bk', 'L0_attn_Wv', 'L0_attn_bv', 'L0_attn_Wo',
        'L0_attn_bo', 'L0_attn_projection', 'L0_ffn_expert_sel', 'L0_ffn_keys', 'L0_ffn_values', 'L1_attn_P_q',
        'L1_attn_P_k', 'L1_attn_P_v', 'L1_attn_P_o', 'L1_ffn_Wg', 'L1_ffn_W1', 'L1_ffn_b1', 'L1_ffn_W2', 'L1_ffn_b2']
_OUTS = [((BATCH, SEQ, P), 'float32')]


def kernel(**inputs):
    import numpy as _np
    import concourse.bacc as _bacc
    from concourse import mybir as _mybir
    from concourse.bass_utils import run_bass_kernel_spmd as _run

    nc = _bacc.Bacc("TRN2", target_bir_lowering=False, num_devices=1)
    arrays, args = {}, {}
    for name in _INS:
        a = _np.ascontiguousarray(inputs[name])
        arrays[f"in_{name}_dram"] = a
        args[name] = nc.dram_tensor(f"in_{name}_dram", a.shape, _mybir.dt.from_np(a.dtype), kind="ExternalInput").ap()
    (shape, dtype), = _OUTS
    out = nc.dram_tensor("out_0_dram", shape, _mybir.dt.from_np(_np.dtype(dtype)), kind="ExternalOutput").ap()
    build(nc, args, out)
    r = _run(nc, [arrays], core_ids=[0])
    return r.results[0]["out_0_dram"]
```
